# Optimizing a Trainium2 kernel written in Bass

```python
import numpy as np
import jax
import jax.numpy as jnp

def _softmax(x, axis=-1):
    return jax.nn.softmax(x, axis=axis)

def _gelu(x):
    return jax.nn.gelu(x, approximate=True)

def _silu(x):
    return jax.nn.silu(x)

def _sigmoid(x):
    return jax.nn.sigmoid(x)

def _layernorm(x, axis=-1, eps=1e-05):
    m = jnp.mean(x, axis=axis, keepdims=True)
    v = jnp.var(x, axis=axis, keepdims=True)
    return (x - m) / jnp.sqrt(v + eps)

def _scatter_add(tgt, idx, src, axis=0):
    return tgt.at[idx].add(src)

def _segment_sum(src, seg, n):
    return jax.ops.segment_sum(src, seg, n)
kernel_name = 'mk_adaln_ffn_d2_seqx_r4_d31ccf'

def setup_inputs(seed: int=0):
    np.random.seed(seed)
    _w = jnp.asarray

    def _rec_inputs():
        import jax
        import jax.numpy as jnp
        _rk = jax.random.key(seed)
        x = -7.109e-05 + 0.9999 * jax.random.normal(jax.random.fold_in(_rk, 1), (32, 64, 1024), jnp.float32)
        _lenS = 64 - jax.random.randint(jax.random.fold_in(_rk, 7), (32,), 0, max(1, 64 // 4) + 1, jnp.int32)
        _lenS2 = 64 - jax.random.randint(jax.random.fold_in(_rk, 8), (32,), 0, max(1, 64 // 4) + 1, jnp.int32)
        itok_B_0_15 = jax.random.randint(jax.random.fold_in(_rk, 11), (32,), 0, 16, jnp.int32)
        itok_B_3_7 = jax.random.randint(jax.random.fold_in(_rk, 12), (32,), 3, 8, jnp.int32)
        return (x, itok_B_0_15, itok_B_3_7)
    x, itok_B_0_15, itok_B_3_7 = _rec_inputs()

    def _L0_cond_setup():
        import jax, jax.numpy as jnp
        import numpy as np
        NUM_CONDITIONS = 16
        IN_CH = 64
        OUT_CH = 64
        B = 64
        T = 1024
        key = jax.random.key(seed)
        k_x, k_w, k_c = jax.random.split(key, 3)
        x = jax.random.normal(k_x, (B, IN_CH, T), dtype=jnp.float32)
        bound = float(np.sqrt(6.0 / IN_CH))
        weights = jax.random.uniform(k_w, (NUM_CONDITIONS, IN_CH, OUT_CH), dtype=jnp.float32, minval=-bound, maxval=bound)
        condition = jax.random.randint(k_c, (B,), 0, NUM_CONDITIONS, dtype=jnp.int64)
        return {'x': x, 'weights': weights, 'condition': condition}
    _L0_cond_all = _L0_cond_setup()
    _L0_cond_in = {k: v for k, v in _L0_cond_all.items() if k in ('weights',)}
    del _L0_cond_all

    def _L0_ffn_setup():
        import jax, jax.numpy as jnp
        import numpy as np
        B, S, IN, OUT = (4, 512, 1024, 1024)
        E, K, R = (8, 2, 16)
        CAP_FACTOR = 3.0
        ALPHA = 1.0 / R
        LN_EPS = 1e-05
        key = jax.random.key(seed)
        ks = jax.random.split(key, 6)
        return {'x': jax.random.normal(ks[0], (B, S, IN), dtype=jnp.float32), 'weight': jax.random.normal(ks[1], (OUT, IN), dtype=jnp.float32) * 0.02, 'lora_A': jax.random.normal(ks[2], (E, IN, R), dtype=jnp.float32) / np.sqrt(R), 'lora_B': jax.random.normal(ks[3], (E, R, OUT), dtype=jnp.float32) * 0.02, 'gw1': jax.random.normal(ks[4], (4 * E, IN), dtype=jnp.float32) * 0.02, 'gb1': jnp.zeros((4 * E,), dtype=jnp.float32), 'ln_gamma': jnp.ones((4 * E,), dtype=jnp.float32), 'ln_beta': jnp.zeros((4 * E,), dtype=jnp.float32), 'gw2': jax.random.normal(ks[5], (E, 4 * E), dtype=jnp.float32) * 0.02, 'gb2': jnp.zeros((E,), dtype=jnp.float32)}
    _L0_ffn_all = _L0_ffn_setup()
    _L0_ffn_in = {k: v for k, v in _L0_ffn_all.items() if k in ('weight', 'lora_A', 'lora_B', 'gw1', 'gb1', 'ln_gamma', 'ln_beta', 'gw2', 'gb2')}
    del _L0_ffn_all

    def _L1_cond_setup():
        import jax, jax.numpy as jnp
        import numpy as np
        MAX_LORAS, OUT, IN = (8, 1024, 1024)
        B, S = (4, 512)
        key = jax.random.key(seed)
        k1, k2, k3 = jax.random.split(key, 3)
        x = jax.random.normal(k1, (B, S, IN), dtype=jnp.float32)
        weight = jax.random.normal(k2, (MAX_LORAS, OUT, IN), dtype=jnp.float32) * 0.02
        adapter_ids = jax.random.randint(k3, (B,), 0, MAX_LORAS, dtype=jnp.int32)
        return {'x': x, 'weight': weight, 'adapter_ids': adapter_ids}
    _L1_cond_all = _L1_cond_setup()
    _L1_cond_in = {k: v for k, v in _L1_cond_all.items() if k in ('weight',)}
    del _L1_cond_all

    def _L1_ffn_setup():
        import jax, jax.numpy as jnp
        import numpy as np
        EPS = 1e-05

        def _bitlinear(x, w):
            scale = jnp.mean(jnp.abs(w))
            q = jnp.round(jnp.clip(w / (scale + EPS), -1.0, 1.0))
            deq = q * scale
            return x @ deq.T
        key = jax.random.key(seed)
        k1, k2, k3, k4 = jax.random.split(key, 4)
        B, S, H, I = (4, 512, 1024, 2752)
        return {'hidden_states': jax.random.normal(k1, (B, S, H), dtype=jnp.float32), 'w_gate': jax.random.normal(k2, (I, H), dtype=jnp.float32) * 0.02, 'w_up': jax.random.normal(k3, (I, H), dtype=jnp.float32) * 0.02, 'w_down': jax.random.normal(k4, (H, I), dtype=jnp.float32) * 0.02}
    _L1_ffn_all = _L1_ffn_setup()
    _L1_ffn_in = {k: v for k, v in _L1_ffn_all.items() if k in ('w_gate', 'w_up', 'w_down')}
    del _L1_ffn_all
    return {'x': x, 'itok_B_0_15': itok_B_0_15, 'itok_B_3_7': itok_B_3_7, 'L0_cond_weights': _L0_cond_in['weights'], 'L0_ffn_weight': _L0_ffn_in['weight'], 'L0_ffn_lora_A': _L0_ffn_in['lora_A'], 'L0_ffn_lora_B': _L0_ffn_in['lora_B'], 'L0_ffn_gw1': _L0_ffn_in['gw1'], 'L0_ffn_gb1': _L0_ffn_in['gb1'], 'L0_ffn_ln_gamma': _L0_ffn_in['ln_gamma'], 'L0_ffn_ln_beta': _L0_ffn_in['ln_beta'], 'L0_ffn_gw2': _L0_ffn_in['gw2'], 'L0_ffn_gb2': _L0_ffn_in['gb2'], 'L1_cond_weight': _L1_cond_in['weight'], 'L1_ffn_w_gate': _L1_ffn_in['w_gate'], 'L1_ffn_w_up': _L1_ffn_in['w_up'], 'L1_ffn_w_down': _L1_ffn_in['w_down']}

def reference(x, itok_B_0_15, itok_B_3_7, L0_cond_weights, L0_ffn_weight, L0_ffn_lora_A, L0_ffn_lora_B, L0_ffn_gw1, L0_ffn_gb1, L0_ffn_ln_gamma, L0_ffn_ln_beta, L0_ffn_gw2, L0_ffn_gb2, L1_cond_weight, L1_ffn_w_gate, L1_ffn_w_up, L1_ffn_w_down):
    import jax
    import jax.numpy as jnp

    def _L0_cond_ref(x, weights, condition):
        import jax, jax.numpy as jnp
        import numpy as np
        NUM_CONDITIONS = 16
        IN_CH = 64
        OUT_CH = 64
        B = 64
        T = 1024
        W = weights[condition]
        return jnp.einsum('bct,bcd->bdt', x, W)

    def _L0_ffn_ref(x, weight, lora_A, lora_B, gw1, gb1, ln_gamma, ln_beta, gw2, gb2):
        import jax, jax.numpy as jnp
        import numpy as np
        B, S, IN, OUT = (4, 512, 1024, 1024)
        E, K, R = (8, 2, 16)
        CAP_FACTOR = 3.0
        ALPHA = 1.0 / R
        LN_EPS = 1e-05
        orig_shape = x.shape
        xf = x.reshape(-1, orig_shape[-1])
        N = xf.shape[0]
        capacity = int(CAP_FACTOR * N / E)
        h = xf @ gw1.T + gb1
        mu = jnp.mean(h, axis=-1, keepdims=True)
        var = jnp.mean((h - mu) ** 2, axis=-1, keepdims=True)
        h = (h - mu) * jax.lax.rsqrt(var + LN_EPS) * ln_gamma + ln_beta
        h = jax.nn.relu(h)
        gates = h @ gw2.T + gb2
        top_v, top_i = jax.lax.top_k(gates, K)
        top_g = jax.nn.softmax(top_v, axis=-1)
        onehot = (top_i[..., None] == jnp.arange(E)).astype(xf.dtype)
        counts = onehot.sum(axis=0)
        allowed = (counts <= capacity).astype(xf.dtype)
        w = jnp.einsum('nke,nk,ke->ne', onehot, top_g, allowed)
        main = xf @ weight.T
        tmp = jnp.einsum('ni,eir->enr', xf, lora_A)
        tmp = tmp * w.T[:, :, None]
        lora = jnp.einsum('enr,ero->no', tmp, lora_B) * ALPHA
        out = main + lora
        return out.reshape(*orig_shape[:-1], weight.shape[0])

    def _L1_cond_ref(x, weight, adapter_ids):
        import jax, jax.numpy as jnp
        import numpy as np
        MAX_LORAS, OUT, IN = (8, 1024, 1024)
        B, S = (4, 512)
        w = weight[adapter_ids]
        return jnp.einsum('bsi,boi->bso', x, w)

    def _L1_ffn_ref(hidden_states, w_gate, w_up, w_down):
        import jax, jax.numpy as jnp
        import numpy as np
        EPS = 1e-05

        def _bitlinear(x, w):
            scale = jnp.mean(jnp.abs(w))
            q = jnp.round(jnp.clip(w / (scale + EPS), -1.0, 1.0))
            deq = q * scale
            return x @ deq.T
        gate = _bitlinear(hidden_states, w_gate)
        up = _bitlinear(hidden_states, w_up)
        inter = gate * up
        out = _bitlinear(inter, w_down)
        return out
    x = x + _L0_ffn_ref(_L0_cond_ref(x, L0_cond_weights, itok_B_0_15), L0_ffn_weight, L0_ffn_lora_A, L0_ffn_lora_B, L0_ffn_gw1, L0_ffn_gb1, L0_ffn_ln_gamma, L0_ffn_ln_beta, L0_ffn_gw2, L0_ffn_gb2)
    x = x + _L1_ffn_ref(_L1_cond_ref(x, L1_cond_weight, itok_B_3_7), L1_ffn_w_gate, L1_ffn_w_up, L1_ffn_w_down)
    return x

_drawn_inputs = setup_inputs


def setup_inputs(seed=0):
    import zlib

    import numpy as np

    out = dict(_drawn_inputs(seed))
    spreads = {'L0_ffn_gb1': (0.0, 0.8),
     'L0_ffn_ln_gamma': (1.0, 0.6),
     'L0_ffn_ln_beta': (0.0, 0.8),
     'L0_ffn_gb2': (0.0, 0.318)}
    factors = {'L0_ffn_lora_A': 3.082, 'L0_ffn_lora_B': 3.096, 'L0_ffn_gw1': 3.433, 'L0_ffn_gw2': 3.559}
    for name, (base, spread) in spreads.items():
        noise = np.random.default_rng([zlib.crc32(name.encode()), seed]).standard_normal(out[name].shape)
        drawn = base * np.exp(spread * noise) if base else spread * noise
        out[name] = jnp.asarray(drawn.astype(out[name].dtype))
    for name, factor in factors.items():
        out[name] = (out[name] * factor).astype(out[name].dtype)
    return out
```

```python
from contextlib import ExitStack

import concourse.bass as bass
from concourse import mybir

F32 = mybir.dt.float32
F16 = mybir.dt.float16
I8 = mybir.dt.int8
I32 = mybir.dt.int32
U8 = mybir.dt.uint8
ALU = mybir.AluOpType
ACT = mybir.ActivationFunctionType
X = mybir.AxisListType.X
ds = bass.ds

P = 128
NB, SEQ, D = 32, 64, 1024
NTOK = NB * SEQ
NT = NTOK // P
KC = D // P
H = D // 2
E, R, GH = 8, 16, 32
ER = E * R
CAPACITY = 3 * NTOK // E
NADP = 8
NSLOT = (NB + NADP) // 2
INNER = 2752
IC = (INNER + P - 1) // P
LAST = INNER - (IC - 1) * P
GRP = 512
NG = NTOK // GRP
TPG = GRP // P
READ_DUMMY, WRITE_DUMMY, SECOND_DUMMY = NB, NB + 2, NB + 3
ACT_COLS = (NB + 4) * SEQ

ACT_SCALE = 2.0 ** 4
WGT_SCALE = 2.0 ** 10
PROD = ACT_SCALE * WGT_SCALE
INTER_SCALE = 2.0 ** 6
LN_EPS = 1e-5
Q_EPS = 1e-5

NPIECE = 16
PIECE = INNER * D // P // NPIECE

F_PERM, F_COND, F_READ, F_WRITE, F_SECOND, F_RANK, F_ADP, F_CUM, F_USED = 0, 32, 64, 84, 104, 124, 144, 152, 160
NFIELD = 161


def build_program(nc, x, adapter_id, cond_id, cond_w, w0, lora_a, lora_b, gw1, gb1, ln_g, ln_b, gw2, gb2,
                  w1, w_gate, w_up, w_down, out):
    ctx = ExitStack()
    with ctx:
        def sb(name, shape, dt):
            return ctx.enter_context(nc.sbuf_tensor(name, shape, dt))

        def sem(name):
            return ctx.enter_context(nc.semaphore(name))

        w1t_dram = nc.dram_tensor("w1t_scratch", [NADP, KC, P, 2 * KC * P], F16, kind="Internal").ap()
        x1_dram = nc.dram_tensor("x1_scratch", [NTOK, D], F32, kind="Internal").ap()

        act_t = sb("act_t", [P, 2, KC, ACT_COLS], F16)
        region_q = sb("region_q", [P, 66 * 1024], U8)
        region_w = sb("region_w", [P, 64 * 1024], U8)
        region_s = sb("region_s", [P, 8 * 1024], U8)
        region_g = sb("region_g", [P, 8 * 1024], U8)

        def view(region, kb, dims, dt):
            n = 1
            for d in dims:
                n *= d
            at = int(kb * 1024)
            size = {F32: 4, I32: 4, F16: 2, I8: 1}[dt]
            v = region[:, at:at + n * size].bitcast(dt)
            names = "abcd"[:len(dims)]
            if len(dims) == 1:
                return v
            return v.rearrange(f"p ({' '.join(names)}) -> p {' '.join(names)}", **dict(zip(names, dims)))

        w_nat = [view(region_q, 4 * i, [D], F32) for i in range(4)]
        w_split = [view(region_q, 16 + 4 * i, [2, KC, P], F16) for i in range(4)]
        x_nat = [view(region_q, 32 + 4 * i, [D], F32) for i in range(2)]
        x1_nat = [view(region_q, 40 + 4 * i, [D], F32) for i in range(2)]
        gw1_nat = x1_nat[0]
        tmpw_t = view(region_q, 48, [2, NTOK], F16)
        lora_a_nat = view(region_q, 56, [KC, E, R], F32)
        lora_b_nat = view(region_q, 60, [D], F32)
        gate_prod = view(region_q, 56, [NT // 2, E, GH], F32)
        w0_t = view(region_w, 0, [KC, 2, KC, P], F16)
        cond_bd = view(region_w, 32, [NT, P], F32)
        tmp = view(region_w, 40, [NT, ER + GH], F32)
        ag = view(region_w, 50, [2, KC, ER + GH], F16)
        lb = view(region_w, 55, [2, D], F16)
        tmpw = view(region_s, 0, [NT, E, R], F32)
        w1_t = region_w[:, :].bitcast(F16).rearrange("p (b o s k c) -> p b o s k c", b=2, o=KC, s=2, k=KC)
        z_nat = [view(region_q, 36 + 4 * i, [D], F32) for i in range(2)]
        stat_in = [view(region_q, 18 * i, [3, PIECE], F32) for i in range(2)]
        q_gate = view(region_q, 0, [KC, IC * P], I8)
        q_up = view(region_q, 22, [KC, IC * P], I8)
        q_down = view(region_q, 44, [IC, D], I8)
        inter = view(region_w, 0, [2, IC, GRP], F16)
        gate_s = [view(region_w, 44 + 2 * i, [GRP], F32) for i in range(2)]
        res = [view(region_w, 48 + 4 * i, [D], F32) for i in range(TPG)]
        wq_nat = [view(region_w, 48 + 4 * i, [D], F32) for i in range(3)]
        wide = [view(region_g, 2 * i, [D], F16) for i in range(4)]
        q16 = [view(region_s, 2 * i, [D], F16) for i in range(3)]
        le_mask = view(region_s, 6, [D], F16)

        ident = sb("ident", [P, P], F32)
        ident16 = sb("ident16", [P, P], F16)
        ones = sb("ones", [P, P], F32)
        g1b = sb("g1b", [P, GH], F32)
        lng = sb("lng", [P, GH], F32)
        lnb = sb("lnb", [P, GH], F32)
        g2w = view(region_q, 64, [E * GH], F32)
        g2b = sb("g2b", [P, E], F32)
        ids_i = sb("ids_i", [1, 2 * NB], I32)
        iota_i = sb("iota_i", [P, NB], I32)
        iota = sb("iota", [P, NB], F32)
        stat = sb("stat", [P, 3, NPIECE], F32)
        ssum = sb("ssum", [P, 4], F32)
        mean = sb("mean", [P, 4], F32)
        thr = sb("thr", [P, 4], F32)
        nthr = sb("nthr", [P, 4], F32)
        inter_c = sb("inter_c", [P, 1], F32)
        out_c = sb("out_c", [P, 1], F32)
        ixf = view(region_q, 65, [NFIELD], F32)[0:1]
        ixi = sb("ixi", [1, NFIELD], I32)
        ix_a = view(region_g, 0, [16, NB], F32)[0:1]
        ix_i = view(region_q, 65.75, [NB], I32)[0:1]
        ix_m = view(region_s, 0, [NB * NB], F32)[0:1, :].rearrange("p (a b) -> p a b", a=NB)
        ix_o = view(region_s, 4, [NB * NB], F32)[0:1, :].rearrange("p (a b) -> p a b", a=NB)
        hid = view(region_g, 2, [NT, GH], F32)
        hid2 = gate_prod[:, 0:2, :, :].rearrange("p a b c -> p (a b c)").rearrange("p (a b) -> p a b", a=NT)
        row = view(region_g, 4, [8, NT], F32)
        gts = view(region_g, 5, [6, NT, E], F32)
        cnt = sb("cnt", [P, 2, E], F32)
        okay = sb("okay", [P, 2, E], F32)

        pair = [ctx.enter_context(nc.psum_tensor(f"pair{i}", [P, D], F32)) for i in range(4)]

        def bank16(i):
            return pair[i // 2][:, (i % 2) * H:(i % 2 + 1) * H].bitcast(F16)

        ids_loaded = sem("ids_loaded")
        small_loaded = sem("small_loaded")
        gw1_loaded = sem("gw1_loaded")
        lora_loaded = sem("lora_loaded")
        w_loaded = [sem(f"w_loaded{i}") for i in range(4)]
        x_loaded = [sem(f"x_loaded{i}") for i in range(2)]
        consts_ready = sem("consts_ready")
        index_step = sem("index_step")
        index_ready = sem("index_ready")
        gw1_transposed = sem("gw1_transposed")
        ag_high = sem("ag_high")
        ag_low = sem("ag_low")
        w_transposed = sem("w_transposed")
        w_high = sem("w_high")
        w_low = sem("w_low")
        w_stored = [sem(f"w_stored{i}") for i in range(4)]
        y_done = sem("y_done")
        y_high = sem("y_high")
        y_low = sem("y_low")
        tmp_done = sem("tmp_done")
        tmp_copied = sem("tmp_copied")
        gate_step = sem("gate_step")
        gate_half = sem("gate_half")
        var_ready = sem("var_ready")
        gap_ready = sem("gap_ready")
        count_ready = sem("count_ready")
        tmpw_ready = sem("tmpw_ready")
        gate_std = sem("gate_std")
        gate_exp = sem("gate_exp")
        counted = sem("counted")
        tmpw_transposed = sem("tmpw_transposed")
        tmpw_high = sem("tmpw_high")
        acc_released = sem("acc_released")
        main_done = sem("main_done")
        x1_transposed = sem("x1_transposed")
        x1_high = sem("x1_high")
        x1_low = sem("x1_low")
        x1_stored = [sem(f"x1_stored{i}") for i in range(2)]
        w1_loaded = sem("w1_loaded")
        stat_loaded = [sem(f"stat_loaded{i}") for i in range(2)]
        stat_done = sem("stat_done")
        stat_summed = sem("stat_summed")
        stat_step = sem("stat_step")
        mean_done = sem("mean_done")
        scales_ready = sem("scales_ready")
        z_done = sem("z_done")
        z_copied_a = sem("z_copied_a")
        z_copied_v = sem("z_copied_v")
        z_transposed = sem("z_transposed")
        z_high = sem("z_high")
        z_low = sem("z_low")
        wq_loaded = [sem(f"wq_loaded{i}") for i in range(3)]
        mask_ready = sem("mask_ready")
        zeroed = sem("zeroed")
        q_ready = sem("q_ready")
        q_transposed = sem("q_transposed")
        q_stored = sem("q_stored")
        gate_wide = sem("gate_wide")
        up_wide = sem("up_wide")
        down_wide = [sem(f"down_wide{i}") for i in range(2)]
        down_step = sem("down_step")
        gu_done = sem("gu_done")
        gate_scaled = sem("gate_scaled")
        prod_done = sem("prod_done")
        inter_high = sem("inter_high")
        inter_low = sem("inter_low")
        down_done = sem("down_done")
        res_loaded = [sem(f"res_loaded{i}") for i in range(TPG)]
        res_done = sem("res_done")
        out_stored = [sem(f"out_stored{i}") for i in range(TPG)]

        x_rows = x.rearrange("b c t -> (b c) t")
        out_rows = out.rearrange("b c t -> (b c) t")
        cond_rows = cond_w.rearrange("b c t -> (b c) t")
        w1_rows = w1.rearrange("a o i -> (a o) i")
        w1t_rows = w1t_dram.rearrange("a o p n -> (a o) p n")
        w1t_flat = w1t_dram.rearrange("a o p n -> a p o n")

        def wait_if(eng, sem, n):
            if not isinstance(n, int) or n > 0:
                eng.wait_ge(sem, n)

        def at(a, i):
            if isinstance(i, int):
                return a[:, i]
            names = "bcd"[:len(a.shape) - 2]
            return a[:, ds(i, 1)].rearrange(f"p x {' '.join(names)} -> p (x {names[0]}) {' '.join(names[1:])}")

        def widen_half(g, ic):
            return (ic + g) % 2

        def down_slot(g, c):
            return 2 * ((c % 4 // 2 + g) % 2) + c % 2

        def chunked(a):
            return a.rearrange("p (k c) -> p k c", k=KC)

        def field(eng, at, i, hi):
            return eng.value_load(ixi[0:1, ds(at + i, 1)], min_val=0, max_val=hi)

        NPREP0 = KC
        NPREP = KC + NADP * KC
        NSRC = NB * SEQ

        block = ctx.enter_context(nc.Block())

        @block.sync
        def _(sp):
            def load_w(rows, r, slot, first):
                if not first:
                    sp.wait_ge(w_transposed, r - 3)
                sp.dma_start(w_nat[slot], rows).then_inc(w_loaded[slot], 16)

            def load_x(t, slot, released, with_cond):
                b0 = field(sp, F_PERM, 2 * t, NB - 1)
                b1 = field(sp, F_PERM, 2 * t + 1, NB - 1)
                if released is not None:
                    sp.wait_ge(*released)
                if with_cond:
                    c0 = field(sp, F_COND, 2 * t, 15)
                    c1 = field(sp, F_COND, 2 * t + 1, 15)
                    sp.dma_start(at(cond_bd[0:SEQ], t)[:, 0:SEQ],
                                 cond_rows[ds(c0 * SEQ, SEQ), :]).then_inc(x_loaded[slot], 16)
                    sp.dma_start(at(cond_bd[SEQ:P], t)[:, SEQ:P],
                                 cond_rows[ds(c1 * SEQ, SEQ), :]).then_inc(x_loaded[slot], 16)
                sp.dma_start(x_nat[slot][0:SEQ, :], x_rows[ds(b0 * SEQ, SEQ), :]).then_inc(x_loaded[slot], 16)
                sp.dma_start(x_nat[slot][SEQ:P, :], x_rows[ds(b1 * SEQ, SEQ), :]).then_inc(x_loaded[slot], 16)

            sp.dma_start(ids_i[0:1, 0:NB], adapter_id.unsqueeze(0)).then_inc(ids_loaded, 16)
            sp.dma_start(ids_i[0:1, NB:2 * NB], cond_id.unsqueeze(0)).then_inc(ids_loaded, 16)
            sp.dma_start(gw1_nat[0:GH, :], gw1).then_inc(gw1_loaded, 16)
            for r in range(4):
                load_w(w0[r * P:(r + 1) * P, :], r, r, True)
            for k in range(KC):
                sp.dma_start(lora_a_nat[:, k], lora_a[:, k * P:(k + 1) * P, :].rearrange("e i r -> i e r"))\
                  .then_inc(lora_loaded, 16)
            sp.dma_start(lora_b_nat, lora_b.rearrange("e r o -> (e r) o")).then_inc(lora_loaded, 16)
            for dst, src in ((g1b[:, :], gb1), (lng[:, :], ln_g), (lnb[:, :], ln_b),
                             (g2w[:, :], gw2.rearrange("e h -> (e h)")), (g2b[:, :], gb2)):
                sp.dma_start(dst, src.partition_broadcast(P)).then_inc(small_loaded, 16)
            sp.wait_ge(index_ready, 1)
            sp.wait_ge(consts_ready, 5)
            load_x(0, 0, None, True)
            load_x(1, 1, None, True)
            for r in range(4, NPREP0):
                load_w(w0[r * P:(r + 1) * P, :], r, r % 4, False)
            with sp.Fori(1, NT // 2) as i:
                for s in range(2):
                    load_x(2 * i + s, s, (y_done, 2 * i + s - 1), True)
            with sp.Fori(0, NT // 2) as i:
                for s in range(2):
                    for q in range(4):
                        r1 = 8 * i + 4 * s + q
                        load_w(w1_rows[ds(r1 * P, P), :], NPREP0 + r1, q, False)
                    load_x(2 * i + s, s, (acc_released, 2 * i + s + 1), False)

            sp.wait_ge(index_ready, 2)
            for s in range(4):
                sp.wait_ge(w_stored[s], 16 * (NPREP - NPREP0) // 4)
            sp.wait_ge(main_done, NT)
            used = field(sp, F_USED, 0, NADP)
            for r in range(NADP):
                a = field(sp, F_ADP, r, NADP - 1)
                before = field(sp, F_CUM, r - 2, NSLOT) if r >= 2 else None
                with sp.If(used > r):
                    if r >= 1:
                        sp.wait_ge(w1_loaded, 16 * r)
                    if r >= 2:
                        sp.wait_ge(z_done, before)
                    sp.dma_start(region_w[:, ((r + 1) % 2) * 32768:((r + 1) % 2 + 1) * 32768].bitcast(F16)
                                 .rearrange("p (o n) -> p o n", o=KC),
                                 w1t_flat[ds(a, 1)].rearrange("a p o n -> (a p) o n"))\
                      .then_inc(w1_loaded, 16)

            wd_view = w_down.rearrange("(t p) i -> p t i", p=P)

            def load_q(ic, last=False):
                n = LAST if last else P
                for kind, src in enumerate((w_gate, w_up)):
                    if not isinstance(ic, int) or ic > 0:
                        sp.wait_ge(q_ready, 3 * ic - 2 + kind)
                    sp.dma_start(wq_nat[kind][0:n, :], src[(IC - 1) * P:INNER, :] if last else src[ds(ic * P, P), :])\
                      .then_inc(wq_loaded[kind], 16)
                if not isinstance(ic, int) or ic > 0:
                    sp.wait_ge(q_ready, 3 * ic)
                dst = wq_nat[2].rearrange("p (t i) -> p t i", t=KC)
                sp.dma_start(dst[:, :, 0:n], wd_view[:, :, (IC - 1) * P:INNER] if last else wd_view[:, :, ds((ic - 1) * P + P, P)])\
                  .then_inc(wq_loaded[2], 16)

            sp.wait_ge(z_done, NSLOT)
            load_q(0)
            with sp.Fori(1, IC - 1) as ic:
                load_q(ic)
            load_q(IC - 1, last=True)

            def load_res(m, slot):
                sp.dma_start(res[slot], x1_dram[ds(m * P, P), :]).then_inc(res_loaded[slot], 16)

            def store_out(m, slot):
                b0 = field(sp, F_PERM, 2 * m, NB - 1)
                b1 = field(sp, F_PERM, 2 * m + 1, NB - 1)
                sp.wait_ge(res_done, m + 1)
                sp.dma_start(out_rows[ds(b0 * SEQ, SEQ), :], res[slot][0:SEQ, :]).then_inc(out_stored[slot], 16)
                sp.dma_start(out_rows[ds(b1 * SEQ, SEQ), :], res[slot][SEQ:P, :]).then_inc(out_stored[slot], 16)

            sp.wait_ge(q_ready, 3 * IC)
            for s in range(2):
                sp.wait_ge(x1_stored[s], 16 * NT // 2)
            for s in range(TPG):
                load_res(s, s)
            for s in range(TPG):
                store_out(s, s)
            with sp.Fori(1, NG) as g:
                for s in range(TPG):
                    sp.wait_ge(out_stored[s], 32 * g)
                    load_res(TPG * g + s, s)
                for s in range(TPG):
                    store_out(TPG * g + s, s)
            for s in range(TPG):
                sp.wait_ge(out_stored[s], 32 * NG)

        @block.gpsimd
        def _(pool):
            pool.iota(iota_i[:, :], pattern=[[1, NB]], base=0, channel_multiplier=0).then_inc(consts_ready, 1)
            pool.memset(ones[:, :], 1.0).then_inc(consts_ready, 1)
            pool.memset(ident[:, :], 0.0).then_inc(consts_ready, 1)
            pool.memset(ident16[:, :], 0.0).then_inc(consts_ready, 1)
            pool.memset(cond_bd, 0.0).then_inc(consts_ready, 1)
            pool.wait_ge(consts_ready, 5)
            for m in (ident, ident16):
                pool.affine_select(out=m[:, :], in_=m[:, :], compare_op=ALU.not_equal, fill=1.0, base=0,
                                   pattern=[[-1, P]], channel_multiplier=1).then_inc(consts_ready, 1)
            pool.memset(act_t[:, :, :, NTOK:ACT_COLS], 0.0).then_inc(consts_ready, 1)

            def widen_up(g, ic, s):
                if g == 0:
                    pool.wait_ge(q_stored, 3 * ic + 2)
                pool.tensor_copy(chunked(wide[2 * widen_half(g, s) + 1]), q_up[:, :, ds(ic * P, P)])\
                    .then_inc(up_wide, 1)

            def low_inter(g, ic, s):
                pool.wait_ge(inter_high, g * IC + ic + 1)
                pool.tensor_tensor(at(inter[:, 1], ic), gate_s[s], at(inter[:, 0], ic), ALU.subtract)\
                    .then_inc(inter_low, 1)

            for g in range(NG):
                wait_if(pool, down_step, g * (IC - 2))
                widen_up(g, 0, 0)
                wait_if(pool, down_done, TPG * g)
                widen_up(g, 1, 1)
                low_inter(g, 0, 0)
                with pool.Fori(0, IC // 2 - 1) as i:
                    for s in range(2):
                        ic = 2 * i + 1 + s
                        pool.wait_ge(gu_done, g * IC + ic)
                        widen_up(g, ic + 1, s)
                        low_inter(g, ic, 1 - s)
                low_inter(g, IC - 1, 1)

        @block.tensor
        def _(pe):
            def transpose8(dst, src, idn):
                for k in range(KC):
                    mm = pe.transpose(dst[:, k * P:(k + 1) * P], src[:, k * P:(k + 1) * P], idn[:, :])
                return mm

            def prep(r, slot, loads, first=False):
                pe.wait_ge(w_loaded[slot], loads)
                if not first:
                    pe.wait_ge(w_low, r)
                transpose8(pair[3], w_nat[slot], ident).then_inc(w_transposed, 1)

            pe.wait_ge(consts_ready, 8)
            pe.wait_ge(gw1_loaded, 16)
            for k in range(KC):
                mm = pe.transpose(pair[3][:, k * GH:(k + 1) * GH], gw1_nat[0:GH, k * P:(k + 1) * P],
                                  ident[0:GH, 0:GH])
            mm.then_inc(gw1_transposed, 1)
            pe.wait_ge(ag_low, 1)
            for r in range(NPREP0):
                prep(r, r % 4, 16 * (r // 4 + 1), first=(r == 0))

            def mix(t, s, loads, released):
                pe.wait_ge(x_loaded[s], loads)
                if released is not None:
                    pe.wait_ge(y_low, released)
                bd = at(cond_bd, t)
                for k in range(KC):
                    mm = pe.matmul(pair[s][:, k * P:(k + 1) * P], x_nat[s][:, k * P:(k + 1) * P], bd,
                                   start=True, stop=True)
                mm.then_inc(y_done, 1)

            def gate(t, s, released):
                pe.wait_ge(y_low, t + 1)
                if released is not None:
                    pe.wait_ge(tmp_copied, released)
                dst = pair[2][:, s * H:s * H + ER + GH]
                n = 0
                for k in range(KC):
                    for a, b in ((0, 0), (0, 1), (1, 0)):
                        mm = pe.matmul(dst, act_t[:, a, k, ds(t * P, P)], ag[:, b, k, :],
                                       start=(n == 0), stop=(n == 3 * KC - 1))
                        n += 1
                mm.then_inc(tmp_done, 1)

            mix(0, 0, 64, None)
            mix(1, 1, 64, None)
            pe.wait_ge(ag_low, 3)
            gate(0, 0, None)
            mix(2, 0, 128, 1)
            gate(1, 1, None)
            mix(3, 1, 128, 2)
            gate(2, 0, 1)
            with pe.Fori(2, NT // 2) as i:
                mix(2 * i, 0, 64 * i + 64, 2 * i - 1)
                gate(2 * i - 1, 1, 2 * i - 2)
                mix(2 * i + 1, 1, 64 * i + 64, 2 * i)
                gate(2 * i, 0, 2 * i - 1)
            gate(NT - 1, 1, NT - 2)

            pe.wait_ge(count_ready, 1)
            pe.wait_ge(tmp_copied, NT)
            pe.matmul(pair[2][:, 0:2 * E], ones[:, :], cnt[:, :, :].rearrange("p a b -> p (a b)"),
                      start=True, stop=True).then_inc(counted, 1)
            pe.wait_ge(tmpw_ready, 1)
            pe.wait_ge(y_low, NT)
            for t in range(NT):
                mm = pe.transpose(pair[t // 8][:, (t % 8) * P:(t % 8 + 1) * P],
                                  tmpw[:, t, :, :].rearrange("p a b -> p (a b)"), ident[:, :])
                if t % 8 == 7:
                    mm.then_inc(tmpw_transposed, 1)

            def main(t, s, q):
                if q == 0:
                    pe.wait_ge(acc_released, t + 1)
                for k in (2 * q, 2 * q + 1):
                    for a, b in ((0, 0), (0, 1), (1, 0)):
                        for h in range(2):
                            pe.matmul(pair[s][:, h * H:(h + 1) * H], act_t[:, a, k, ds(t * P, P)],
                                      w0_t[:, 4 * h:4 * h + 4, b, k, :],
                                      start=(k == 0 and a + b == 0), stop=False)
                if q == 3:
                    for a, b in ((0, 0), (0, 1), (1, 0)):
                        for h in range(2):
                            mm = pe.matmul(pair[s][:, h * H:(h + 1) * H], tmpw_t[:, a, ds(t * P, P)],
                                           lb[:, b, h * H:(h + 1) * H], start=False, stop=(a == 1))
                    mm.then_inc(main_done, 1)

            def layer0(i):
                for s in range(2):
                    t = 2 * i + s
                    for q in range(4):
                        main(t, s, q)
                        prep(NPREP0 + 4 * t + q, q, 16 * (3 + t))
                    pe.wait_ge(acc_released, t + 3)
                    wait_if(pe, x1_low, t)
                    transpose8(pair[2], x1_nat[s], ident).then_inc(x1_transposed, 1)

            layer0(0)
            with pe.Fori(1, NT // 2) as i:
                layer0(i)

            def linear(k, s):
                rank = field(pe, F_RANK, k, NADP - 1)
                at = field(pe, F_READ, k, NB * SEQ)
                pe.wait_ge(w1_loaded, rank * 16 + 16)
                wait_if(pe, z_copied_a, k - 1)
                wait_if(pe, z_copied_v, k - 1)
                buf = (rank + 1) % 2
                n = 0
                for c in range(KC):
                    for a, b in ((0, 0), (0, 1), (1, 0)):
                        for h in range(2):
                            mm = pe.matmul(pair[s][:, h * H:(h + 1) * H], act_t[:, a, c, ds(at, P)],
                                           w1_t[:, ds(buf, 1), 4 * h:4 * h + 4, b, c, :].rearrange("p x o c -> p (x o) c"),
                                           start=(n == 0), stop=(n == 3 * KC - 1))
                        n += 1
                mm.then_inc(z_done, 1)

            def linear_t(k, s):
                pe.wait_ge(z_copied_a, k + 1)
                pe.wait_ge(z_copied_v, k + 1)
                wait_if(pe, z_low, k)
                transpose8(pair[2], z_nat[s], ident).then_inc(z_transposed, 1)

            pe.wait_ge(x1_low, NT)
            def layer1(i):
                linear(2 * i + 1, 1)
                linear_t(2 * i, 0)
                linear(2 * i + 2, 0)
                linear_t(2 * i + 1, 1)

            linear(0, 0)
            layer1(0)
            with pe.Fori(1, NSLOT // 2 - 1) as i:
                layer1(i)
            linear(NSLOT - 1, 1)
            linear_t(NSLOT - 2, 0)
            linear_t(NSLOT - 1, 1)
            pe.wait_ge(stat_summed, 1)
            pe.matmul(pair[3][:, 0:3], ones[:, :], ssum[:, 0:3], start=True, stop=True).then_inc(mean_done, 1)

            def turn_q(ic, first=False):
                for kind in range(3):
                    pe.wait_ge(q_ready, 3 * ic + kind + 1)
                    if not first:
                        pe.wait_ge(q_stored, 3 * ic - 2 + kind)
                    transpose8(bank16(4 + kind), q16[kind], ident16).then_inc(q_transposed, 1)

            def gate_up(g, ic, s):
                n = g * IC + ic
                pe.wait_ge(gate_wide, n + 1)
                pe.wait_ge(up_wide, n + 1)
                wait_if(pe, prod_done, n - 1)
                half = widen_half(g, s)
                for w, dst in ((wide[2 * half], pair[0]), (wide[2 * half + 1], pair[1])):
                    for k in range(KC):
                        for a in range(2):
                            mm = pe.matmul(dst[:, s * H:(s + 1) * H], w[:, k * P:(k + 1) * P],
                                           act_t[:, a, k, g * GRP:(g + 1) * GRP],
                                           start=(k == 0 and a == 0), stop=(k == KC - 1 and a == 1))
                mm.then_inc(gu_done, 1)

            def down(ic, tt, slot):
                for a in range(2):
                    for h in range(2):
                        mm = pe.matmul(pair[tt][:, h * H:(h + 1) * H], at(inter[:, a], ic)[:, tt * P:(tt + 1) * P],
                                       wide[slot][:, h * H:(h + 1) * H],
                                       start=(isinstance(ic, int) and ic == 0 and a == 0),
                                       stop=(isinstance(ic, int) and ic == IC - 1 and a == 1))
                return mm

            def down_chunk(g, ic, c):
                pe.wait_ge(down_wide[c % 2], IC // 2 * g + (ic - c % 2) // 2 + 1)
                for tt in (2, 3, 0, 1):
                    if g > 0 and isinstance(ic, int) and ic == 0 and tt == 2:
                        pe.wait_ge(res_done, TPG * g)
                    if isinstance(ic, int) and ic == 0 and tt == 0:
                        pe.wait_ge(prod_done, IC * (g + 1))
                    mm = down(ic, tt, down_slot(g, c))
                mm.then_inc(down_step, 1)

            pe.wait_ge(scales_ready, 1)
            turn_q(0, first=True)
            pe.wait_ge(z_low, NSLOT)
            for g in range(NG):
                if g == 0:
                    for s in range(2):
                        turn_q(s + 1)
                        gate_up(0, s, s)
                    with pe.Fori(1, IC // 2 - 1) as i:
                        for s in range(2):
                            turn_q(2 * i + s + 1)
                            gate_up(0, 2 * i + s, s)
                    turn_q(IC - 1)
                    gate_up(0, IC - 2, 0)
                    gate_up(0, IC - 1, 1)
                    pe.wait_ge(q_stored, 3 * IC)
                else:
                    pe.wait_ge(res_done, TPG * (g - 1) + 2)
                    with pe.Fori(0, IC // 2) as i:
                        for s in range(2):
                            gate_up(g, 2 * i + s, s)
                pe.wait_ge(inter_low, IC * (g + 1) - 2)
                for c in range(4):
                    down_chunk(g, c, c)
                with pe.Fori(1, (IC - 2) // 4) as i:
                    for c in range(4):
                        down_chunk(g, 4 * i + c, c)
                for c in range(2):
                    pe.wait_ge(down_wide[c], IC // 2 * (g + 1))
                pe.wait_ge(inter_low, IC * (g + 1))
                for tt in range(TPG):
                    for c in range(2):
                        mm = down(IC - 2 + c, tt, down_slot(g, c))
                    mm.then_inc(down_done, 1)

        @block.scalar
        def _(act):
            def high(dst, src, scale):
                return act.activation(dst, src, ACT.Copy, scale=scale)

            ps8 = [p[:, :].rearrange("p (k c) -> p k c", k=KC) for p in pair]

            act.wait_ge(gw1_transposed, 1)
            high(ag[:, 0, :, ER:ER + GH], pair[3][:, 0:KC * GH].rearrange("p (k c) -> p k c", k=KC),
                 WGT_SCALE).then_inc(ag_high, 1)
            for r in range(NPREP0):
                act.wait_ge(w_transposed, r + 1)
                high(w0_t[:, r, 0], ps8[3], WGT_SCALE).then_inc(w_high, 1)
            act.wait_ge(lora_loaded, 16 * (KC + 1))
            high(ag[:, 0, :, 0:ER], lora_a_nat.rearrange("p k e r -> p k (e r)"), WGT_SCALE).then_inc(ag_high, 1)
            high(lb[:, 0, :], lora_b_nat, WGT_SCALE).then_inc(ag_high, 1)

            def y_part(t, s):
                act.wait_ge(y_done, t + 1)
                high(act_t[:, 0, :, ds(t * P, P)], ps8[s], ACT_SCALE).then_inc(y_high, 1)

            def tmp_part(t, s):
                act.wait_ge(tmp_done, t + 1)
                high(at(tmp, t),
                     pair[2][:, s * H:s * H + ER + GH], 1.0 / PROD).then_inc(tmp_copied, 1)

            y_part(0, 0)
            y_part(1, 1)
            tmp_part(0, 0)
            with act.Fori(1, NT // 2) as i:
                y_part(2 * i, 0)
                tmp_part(2 * i - 1, 1)
                y_part(2 * i + 1, 1)
                tmp_part(2 * i, 0)
            tmp_part(NT - 1, 1)

            act.wait_ge(var_ready, 1)
            act.activation(row[:, 2, :], row[:, 1, :], ACT.Sqrt).then_inc(gate_std, 1)
            act.wait_ge(gap_ready, 1)
            act.activation(row[:, 5, :], row[:, 4, :], ACT.Exp).then_inc(gate_exp, 1)
            for i in range(2):
                act.wait_ge(tmpw_transposed, i + 1)
                high(tmpw_t[:, 0, i * D:(i + 1) * D], pair[i][:, :], 1.0).then_inc(tmpw_high, 1)

            def store_w(r1, slot):
                act.wait_ge(w_low, NPREP0 + r1 + 1)
                act.dma_start(w1t_rows[ds(r1, 1)].rearrange("a p n -> (a p) n"),
                              w_split[slot].rearrange("p s k c -> p (s k c)")).then_inc(w_stored[slot], 16)

            def layer0(i):
                for s in range(2):
                    t = 2 * i + s
                    for q in range(4):
                        r1 = 4 * t + q
                        act.wait_ge(w_transposed, NPREP0 + r1 + 1)
                        wait_if(act, w_stored[q], 16 * t)
                        high(w_split[q][:, 0], ps8[3], WGT_SCALE).then_inc(w_high, 1)
                        if q > 0:
                            store_w(r1 - 1, q - 1)
                    act.wait_ge(x1_transposed, t + 1)
                    high(act_t[:, 0, :, ds(t * P, P)], ps8[2], ACT_SCALE).then_inc(x1_high, 1)
                    store_w(4 * t + 3, 3)
                    act.dma_start(x1_dram[ds(t * P, P), :], x1_nat[s]).then_inc(x1_stored[s], 16)

            layer0(0)
            with act.Fori(1, NT // 2) as i:
                layer0(i)

            flat = [w.rearrange("a b -> (a b)").rearrange("(p n) -> p n", p=P) for w in (w_gate, w_up, w_down)]

            def load_piece(p, s):
                if not isinstance(p, int):
                    act.wait_ge(stat_done, p - 1)
                for w in range(3):
                    act.dma_start(stat_in[s][:, w, :], flat[w][:, ds(p * PIECE, PIECE)])\
                       .then_inc(stat_loaded[s], 16)

            def copy_z(k, s):
                act.wait_ge(z_done, k + 1)
                high(z_nat[s][:, 0:H], pair[s][:, 0:H], 1.0 / PROD).then_inc(z_copied_a, 1)

            def high_z(k):
                d0 = field(act, F_WRITE, k, WRITE_DUMMY * SEQ)
                d1 = field(act, F_SECOND, k, SECOND_DUMMY * SEQ)
                act.wait_ge(z_transposed, k + 1)
                high(act_t[:, 0, :, ds(d0, SEQ)], ps8[2][:, :, 0:SEQ], ACT_SCALE)
                high(act_t[:, 0, :, ds(d1, SEQ)], ps8[2][:, :, SEQ:P], ACT_SCALE).then_inc(z_high, 1)

            for s in range(4):
                act.wait_ge(w_stored[s], 16 * (NPREP - NPREP0) // 4)
            load_piece(0, 0)
            load_piece(1, 1)
            copy_z(0, 0)

            def layer1(i, more):
                copy_z(2 * i + 1, 1)
                high_z(2 * i)
                if more:
                    load_piece(2 * i + 2, 0)
                copy_z(2 * i + 2, 0)
                high_z(2 * i + 1)
                if more:
                    load_piece(2 * i + 3, 1)

            with act.Fori(0, NPIECE // 2 - 1) as i:
                layer1(i, True)
            for i in range(NPIECE // 2 - 1, NSLOT // 2 - 1):
                layer1(i, False)
            copy_z(NSLOT - 1, 1)
            high_z(NSLOT - 2)
            high_z(NSLOT - 1)

            def store_q(ic):
                for kind in range(3):
                    act.wait_ge(q_transposed, 3 * ic + kind + 1)
                    src = bank16(4 + kind)
                    if kind < 2:
                        dst = (q_gate, q_up)[kind][:, :, ds(ic * P, P)]
                        src = src.rearrange("p (k c) -> p k c", k=KC)
                    else:
                        dst = at(q_down, ic)
                    act.activation(dst, src, ACT.Copy).then_inc(q_stored, 1)

            def inter_part(g, ic, s):
                n = g * IC + ic
                act.wait_ge(gu_done, n + 1)
                wait_if(act, inter_low, n - 1)
                act.activation(gate_s[s], pair[0][:, s * H:(s + 1) * H], ACT.Copy, scale=inter_c[:, 0:1])\
                   .then_inc(gate_scaled, 1)
                act.wait_ge(prod_done, n + 1)
                high(at(inter[:, 0], ic), gate_s[s], 1.0).then_inc(inter_high, 1)

            def widen_gate(g, ic, s):
                if g == 0:
                    act.wait_ge(q_stored, 3 * ic + 1)
                act.activation(chunked(wide[2 * widen_half(g, s)]), q_gate[:, :, ds((ic - 1) * P + P, P)], ACT.Copy)\
                   .then_inc(gate_wide, 1)

            def widen_down(g, ic, c):
                act.activation(wide[down_slot(g, c)], at(q_down, ic), ACT.Copy).then_inc(down_wide[0], 1)

            act.wait_ge(scales_ready, 1)
            store_q(0)
            for g in range(NG):
                wait_if(act, down_step, g * (IC - 2))
                widen_gate(g, 0, 0)
                if g == 0:
                    store_q(1)
                wait_if(act, down_done, TPG * g)
                widen_gate(g, 1, 1)
                inter_part(g, 0, 0)
                with act.Fori(0, IC // 2 - 1) as i:
                    for s in range(2):
                        ic = 2 * i + 1 + s
                        if g == 0:
                            store_q(ic + 1)
                        if g > 0:
                            act.wait_ge(gu_done, g * IC + ic)
                        widen_gate(g, ic + 1, s)
                        inter_part(g, ic, 1 - s)
                if g == 0:
                    act.wait_ge(q_stored, 3 * IC)
                widen_down(g, 0, 0)
                inter_part(g, IC - 1, 1)
                widen_down(g, 2, 2)
                with act.Fori(0, (IC - 6) // 4) as i:
                    for c in (0, 2):
                        act.wait_ge(down_step, g * (IC - 2) + 4 * i + c + 1)
                        widen_down(g, 4 * i + c + 4, c)
                act.wait_ge(down_step, g * (IC - 2) + IC - 5)
                widen_down(g, IC - 2, 0)

        @block.vector
        def _(v):
            ps8 = [p[:, :].rearrange("p (k c) -> p k c", k=KC) for p in pair]

            def low(dst, src, scale, hi):
                return v.scalar_tensor_tensor(out=dst, in0=src, scalar=scale, in1=hi,
                                              op0=ALU.mult, op1=ALU.subtract)

            step = [0]

            def then(instruction):
                step[0] += 1
                instruction.then_inc(index_step, 1)
                v.wait_ge(index_step, step[0])

            def outer(a, n=NB):
                return a.unsqueeze(2).broadcast_to([1, n, NB])

            def inner(a, n=NB):
                return a.unsqueeze(1).broadcast_to([1, n, NB])

            adp, cnd, key, rank, adps, first, since, start, before, grp, nxt, tok, t0, t1, t2, t3 = \
                [ix_a[:, i, :] for i in range(16)]
            num = iota[0:1, :]

            def pick(dst, mask, values, n=NB):
                then(v.tensor_tensor(ix_m[:, 0:n], mask, inner(values, n), ALU.mult))
                then(v.tensor_reduce(dst, ix_m[:, 0:n], X, ALU.add))

            v.wait_ge(consts_ready, 1)
            then(v.tensor_copy(iota[:, :], iota_i[:, :]))
            v.wait_ge(ids_loaded, 32)
            then(v.tensor_copy(adp, ids_i[0:1, 0:NB]))
            then(v.tensor_copy(cnd, ids_i[0:1, NB:2 * NB]))
            then(v.scalar_tensor_tensor(out=key, in0=adp, scalar=float(NB), in1=num, op0=ALU.mult, op1=ALU.add))
            then(v.tensor_tensor(ix_m, inner(key), outer(key), ALU.is_lt))
            then(v.tensor_reduce(rank, ix_m, X, ALU.add))
            then(v.tensor_tensor(ix_o, inner(rank), outer(num), ALU.is_equal))
            pick(ixf[:, F_PERM:F_PERM + NB], ix_o, num)
            pick(ixf[:, F_COND:F_COND + NB], ix_o, cnd)
            v.tensor_copy(ixi[:, 0:F_READ], ixf[:, 0:F_READ]).then_inc(index_ready, 1)
            pick(adps, ix_o, adp)
            then(v.tensor_tensor(ix_m, inner(adps), outer(adps), ALU.is_lt))
            then(v.tensor_reduce(first, ix_m, X, ALU.add))
            then(v.tensor_tensor(since, num, first, ALU.subtract))
            then(v.tensor_copy(ix_i[:, :], since))
            then(v.tensor_scalar(ix_i[:, :], ix_i[:, :], 1, None, ALU.bitwise_and))
            then(v.tensor_copy(t0, ix_i[:, :]))
            then(v.tensor_scalar(start, t0, -1.0, 1.0, ALU.mult, ALU.add))
            then(v.tensor_tensor(ix_o, inner(num), outer(num), ALU.is_lt))
            pick(before, ix_o, start)
            then(v.tensor_scalar(t1, since, 0.0, None, ALU.is_equal))
            then(v.tensor_tensor(ix_o, inner(num), outer(num), ALU.is_le))
            pick(grp, ix_o, t1)
            then(v.tensor_scalar(grp, grp, -1.0, None, ALU.add))
            then(v.tensor_reduce(ixf[:, F_USED:F_USED + 1], t1, X, ALU.add))
            then(v.memset(nxt, 0.0))
            then(v.tensor_tensor(nxt[:, 0:NB - 1], adps[:, 1:NB], adps[:, 0:NB - 1], ALU.is_equal))
            then(v.tensor_scalar(t2, num, float(1 - SECOND_DUMMY), None, ALU.add))
            then(v.tensor_tensor(t2, t2, nxt, ALU.mult))
            then(v.tensor_scalar(t2, t2, float(SECOND_DUMMY), float(SEQ), ALU.add, ALU.mult))
            then(v.tensor_scalar(t3, num, float(SEQ), None, ALU.mult))
            then(v.tensor_tensor(ix_o[:, 0:NSLOT], inner(before, NSLOT), outer(num[:, 0:NSLOT], NSLOT), ALU.is_equal))
            then(v.tensor_tensor(ix_o[:, 0:NSLOT], ix_o[:, 0:NSLOT], inner(start, NSLOT), ALU.mult))
            sl = ix_o[:, 0:NSLOT]
            then(v.tensor_reduce(tok[:, 0:NSLOT], sl, X, ALU.add))
            then(v.tensor_scalar(tok[:, 0:NSLOT], tok[:, 0:NSLOT], -1.0, 1.0, ALU.mult, ALU.add))
            un = tok[:, 0:NSLOT]
            rd, wr, sc, rk = [ixf[:, f:f + NSLOT] for f in (F_READ, F_WRITE, F_SECOND, F_RANK)]
            pick(t0[:, 0:NSLOT], sl, t3, NSLOT)
            then(v.scalar_tensor_tensor(out=rd, in0=un, scalar=float(READ_DUMMY * SEQ), in1=t0[:, 0:NSLOT], op0=ALU.mult, op1=ALU.add))
            then(v.scalar_tensor_tensor(out=wr, in0=un, scalar=float(WRITE_DUMMY * SEQ), in1=t0[:, 0:NSLOT], op0=ALU.mult, op1=ALU.add))
            pick(t0[:, 0:NSLOT], sl, t2, NSLOT)
            then(v.scalar_tensor_tensor(out=sc, in0=un, scalar=float(SECOND_DUMMY * SEQ), in1=t0[:, 0:NSLOT], op0=ALU.mult, op1=ALU.add))
            pick(t0[:, 0:NSLOT], sl, grp, NSLOT)
            then(v.tensor_scalar(t2[:, 0:1], ixf[:, F_USED:F_USED + 1], -1.0, None, ALU.add))
            then(v.scalar_tensor_tensor(out=rk, in0=un, scalar=t2[:, 0:1], in1=t0[:, 0:NSLOT], op0=ALU.mult, op1=ALU.add))
            then(v.tensor_tensor(t0, t1, adps, ALU.mult))
            then(v.tensor_tensor(ix_o[:, 0:NADP], inner(grp, NADP), outer(num[:, 0:NADP], NADP), ALU.is_equal))
            pick(ixf[:, F_ADP:F_ADP + NADP], ix_o[:, 0:NADP], t0, NADP)
            then(v.tensor_tensor(ix_o[:, 0:NADP], inner(grp, NADP), outer(num[:, 0:NADP], NADP), ALU.is_le))
            pick(ixf[:, F_CUM:F_CUM + NADP], ix_o[:, 0:NADP], start, NADP)
            v.tensor_copy(ixi[:, F_READ:NFIELD], ixf[:, F_READ:NFIELD]).then_inc(index_ready, 1)

            v.wait_ge(ag_high, 1)
            low(ag[:, 1, :, ER:ER + GH], pair[3][:, 0:KC * GH].rearrange("p (k c) -> p k c", k=KC),
                WGT_SCALE, ag[:, 0, :, ER:ER + GH]).then_inc(ag_low, 1)
            for r in range(NPREP0):
                v.wait_ge(w_high, r + 1)
                low(w0_t[:, r, 1], ps8[3], WGT_SCALE, w0_t[:, r, 0]).then_inc(w_low, 1)
            v.wait_ge(ag_high, 3)
            low(lb[:, 1, :], lora_b_nat, WGT_SCALE, lb[:, 0, :]).then_inc(ag_low, 1)
            low(ag[:, 1, :, 0:ER], lora_a_nat.rearrange("p k e r -> p k (e r)"), WGT_SCALE,
                ag[:, 0, :, 0:ER]).then_inc(ag_low, 1)

            with v.Fori(0, NT // 2) as i:
                for s in range(2):
                    t = 2 * i + s
                    v.wait_ge(y_high, t + 1)
                    low(act_t[:, 1, :, ds(t * P, P)], ps8[s], ACT_SCALE, act_t[:, 0, :, ds(t * P, P)])\
                        .then_inc(y_low, 1)

            count = [0]

            def gthen(instruction):
                count[0] += 1
                instruction.then_inc(gate_step, 1)
                v.wait_ge(gate_step, count[0])

            def per_channel(a, n=NT):
                return a.unsqueeze(1).broadcast_to([P, n, a.shape[1]])

            def per_token(a, n):
                return a.unsqueeze(2).broadcast_to([P, NT, n])

            total, var, std, rstd, gap, ex, p1, p2 = [row[:, i, :] for i in range(8)]
            gt, one1, one2, gl, is_top, wgt = [gts[:, i] for i in range(6)]
            hd = hid[:, :, :]
            v.wait_ge(small_loaded, 80)
            v.wait_ge(tmp_copied, NT)
            gthen(v.tensor_tensor(hd, tmp[:, :, ER:ER + GH], per_channel(g1b[:, :]), ALU.add))
            gthen(v.tensor_reduce(total, hd, X, ALU.add))
            gthen(v.tensor_scalar(total, total, 1.0 / GH, None, ALU.mult))
            gthen(v.tensor_tensor(hd, hd, per_token(total, GH), ALU.subtract))
            gthen(v.tensor_tensor(hid2, hd, hd, ALU.mult))
            gthen(v.tensor_reduce(var, hid2, X, ALU.add))
            v.tensor_scalar(var, var, 1.0 / GH, LN_EPS, ALU.mult, ALU.add).then_inc(var_ready, 1)
            v.wait_ge(gate_std, 1)
            gthen(v.reciprocal(rstd, std))
            gthen(v.tensor_tensor(gap, rstd, rstd, ALU.mult))
            gthen(v.tensor_tensor(gap, gap, var, ALU.mult))
            gthen(v.tensor_scalar(gap, gap, -0.5, 1.5, ALU.mult, ALU.add))
            gthen(v.tensor_tensor(rstd, rstd, gap, ALU.mult))
            gthen(v.tensor_tensor(hd, hd, per_token(rstd, GH), ALU.mult))
            gthen(v.tensor_tensor(hd, hd, per_channel(lng[:, :]), ALU.mult))
            gthen(v.tensor_tensor(hd, hd, per_channel(lnb[:, :]), ALU.add))
            gthen(v.tensor_scalar(hd, hd, 0.0, None, ALU.max))
            g2 = g2w[:, :].rearrange("p (e h) -> p e h", e=E)
            hf = NT // 2
            for half in range(2):
                for tt in range(hf):
                    v.tensor_tensor(gate_prod[:, tt], hid[:, half * hf + tt, :].unsqueeze(1).broadcast_to([P, E, GH]),
                                    g2, ALU.mult).then_inc(gate_half, 1)
                v.wait_ge(gate_half, hf * (half + 1))
                gthen(v.tensor_reduce(gt[:, half * hf:(half + 1) * hf, :], gate_prod, X, ALU.add))
            gthen(v.tensor_tensor(gt, gt, per_channel(g2b[:, :]), ALU.add))

            def choose(top, one):
                gthen(v.tensor_reduce(top, gt, X, ALU.max))
                gthen(v.tensor_tensor(is_top, gt, per_token(top, E), ALU.is_equal))
                gthen(v.scalar_tensor_tensor(out=gl, in0=is_top, scalar=-float(E), in1=per_channel(iota[:, 0:E]),
                                             op0=ALU.mult, op1=ALU.add))
                gthen(v.tensor_reduce(total, gl, X, ALU.min))
                gthen(v.tensor_tensor(one, gl, per_token(total, E), ALU.is_equal))

            choose(p1, one1)
            gthen(v.scalar_tensor_tensor(out=gt, in0=one1, scalar=-3.0e38, in1=gt, op0=ALU.mult, op1=ALU.add))
            choose(p2, one2)
            v.tensor_tensor(gap, p2, p1, ALU.subtract).then_inc(gap_ready, 1)
            gthen(v.tensor_reduce(cnt[:, 0, :], one1.rearrange("p t e -> p e t"), X, ALU.add))
            v.tensor_reduce(cnt[:, 1, :], one2.rearrange("p t e -> p e t"), X, ALU.add).then_inc(count_ready, 1)
            v.wait_ge(gate_exp, 1)
            gthen(v.tensor_scalar(p1, ex, 1.0, None, ALU.add))
            gthen(v.reciprocal(p1, p1))
            gthen(v.tensor_tensor(p2, ex, p1, ALU.mult))
            v.wait_ge(counted, 1)
            gthen(v.tensor_scalar(okay[:, :, :], pair[2][:, 0:2 * E].rearrange("p (a b) -> p a b", a=2),
                                  float(CAPACITY), None, ALU.is_le))
            gthen(v.tensor_tensor(one1, one1, per_channel(okay[:, 0, :]), ALU.mult))
            gthen(v.tensor_tensor(one2, one2, per_channel(okay[:, 1, :]), ALU.mult))
            gthen(v.tensor_tensor(one1, one1, per_token(p1, E), ALU.mult))
            gthen(v.tensor_tensor(one2, one2, per_token(p2, E), ALU.mult))
            gthen(v.tensor_tensor(wgt, one1, one2, ALU.add))
            for e in range(E):
                ins = v.tensor_tensor(tmpw[:, :, e, :], tmp[:, :, e * R:(e + 1) * R],
                                      wgt[:, :, e].unsqueeze(2).broadcast_to([P, NT, R]), ALU.mult)
            ins.then_inc(tmpw_ready, 1)
            for i in range(2):
                v.wait_ge(tmpw_high, i + 1)
                low(tmpw_t[:, 1, i * D:(i + 1) * D], pair[i][:, :], 1.0, tmpw_t[:, 0, i * D:(i + 1) * D])\
                    .then_inc(acc_released, 1)

            def low_w(t, q):
                v.wait_ge(w_high, NPREP0 + 4 * t + q + 1)
                low(w_split[q][:, 1], ps8[3], WGT_SCALE, w_split[q][:, 0]).then_inc(w_low, 1)

            def layer0(i):
                for s in range(2):
                    t = 2 * i + s
                    for q in range(3):
                        low_w(t, q)
                    v.wait_ge(main_done, t + 1)
                    v.wait_ge(x_loaded[s], 64 * (NT // 2) + 32 * (i + 1))
                    wait_if(v, x1_stored[s], 16 * i)
                    v.scalar_tensor_tensor(out=x1_nat[s], in0=pair[s][:, :], scalar=1.0 / PROD, in1=x_nat[s],
                                           op0=ALU.mult, op1=ALU.add).then_inc(acc_released, 1)
                    low_w(t, 3)
                    v.wait_ge(x1_high, t + 1)
                    cols = act_t[:, :, :, ds(t * P, P)]
                    low(cols[:, 1], ps8[2], ACT_SCALE, cols[:, 0]).then_inc(x1_low, 1)

            layer0(0)
            with v.Fori(1, NT // 2) as i:
                layer0(i)

            def copy_z(k, s):
                v.wait_ge(z_done, k + 1)
                v.tensor_scalar(z_nat[s][:, H:D], pair[s][:, H:D], 1.0 / PROD, None, ALU.mult).then_inc(z_copied_v, 1)

            def low_z(k, last=False):
                d0 = field(v, F_WRITE, k, WRITE_DUMMY * SEQ)
                d1 = field(v, F_SECOND, k, SECOND_DUMMY * SEQ)
                v.wait_ge(z_high, k + 1)
                low(act_t[:, 1, :, ds(d0, SEQ)], ps8[2][:, :, 0:SEQ], ACT_SCALE, act_t[:, 0, :, ds(d0, SEQ)])
                low(act_t[:, 1, :, ds(d1, SEQ)], ps8[2][:, :, SEQ:P], ACT_SCALE, act_t[:, 0, :, ds(d1, SEQ)])\
                    .then_inc(z_low, 1)

            def sum_piece(i, s):
                v.wait_ge(stat_loaded[s], 48 * i + 48)
                v.tensor_reduce(stat[:, :, ds(2 * i + s, 1)].rearrange("p a b -> p (a b)"), stat_in[s], X, ALU.add,
                                apply_absolute_value=True).then_inc(stat_done, 1)

            def layer1(i, sums):
                copy_z(2 * i + 1, 1)
                low_z(2 * i)
                if sums:
                    sum_piece(i, 0)
                copy_z(2 * i + 2, 0)
                low_z(2 * i + 1)
                if sums:
                    sum_piece(i, 1)

            copy_z(0, 0)
            with v.Fori(0, NPIECE // 2) as i:
                layer1(i, True)
            v.wait_ge(stat_done, NPIECE)
            v.tensor_reduce(ssum[:, 0:3], stat[:, :, :], X, ALU.add).then_inc(stat_summed, 1)
            for i in range(NPIECE // 2, NSLOT // 2 - 1):
                layer1(i, False)
            copy_z(NSLOT - 1, 1)
            low_z(NSLOT - 2)
            low_z(NSLOT - 1)

            v.wait_ge(mean_done, 1)
            v.tensor_scalar(mean[:, 0:3], pair[3][:, 0:3], 1.0 / (INNER * D), None, ALU.mult).then_inc(stat_step, 1)
            v.wait_ge(stat_step, 1)
            v.tensor_scalar(thr[:, 0:3], mean[:, 0:3], Q_EPS, 0.5, ALU.add, ALU.mult).then_inc(stat_step, 1)
            v.tensor_scalar(out_c[:, :], mean[:, 2:3], 1.0 / INTER_SCALE, None, ALU.mult).then_inc(stat_step, 1)
            v.scalar_tensor_tensor(out=inter_c[:, :], in0=mean[:, 0:1], scalar=INTER_SCALE / ACT_SCALE ** 2,
                                   in1=mean[:, 1:2], op0=ALU.mult, op1=ALU.mult).then_inc(stat_step, 1)
            v.wait_ge(stat_step, 4)
            v.tensor_scalar(nthr[:, 0:3], thr[:, 0:3], -1.0, None, ALU.mult).then_inc(scales_ready, 1)
            v.wait_ge(scales_ready, 1)

            def ternary(ic, n_load, last=False):
                for kind in range(3):
                    if not isinstance(ic, int) or ic > 0:
                        v.wait_ge(q_transposed, 3 * ic - 2 + kind)
                    if last and kind < 2:
                        v.memset(wq_nat[kind][LAST:P, :], 0.0).then_inc(zeroed, 1)
                    if last and kind == 2:
                        v.memset(wq_nat[2].rearrange("p (t i) -> p t i", t=KC)[:, :, LAST:P], 0.0).then_inc(zeroed, 1)
                    if last:
                        v.wait_ge(zeroed, kind + 1)
                    v.wait_ge(wq_loaded[kind], 16 * n_load)
                    if not isinstance(ic, int) or 3 * ic + kind > 0:
                        v.wait_ge(q_ready, 3 * ic + kind)
                    v.tensor_scalar(le_mask, wq_nat[kind], thr[:, kind:kind + 1], None, ALU.is_le).then_inc(mask_ready, 1)
                    v.wait_ge(mask_ready, 3 * ic + kind + 1)
                    v.scalar_tensor_tensor(out=q16[kind], in0=wq_nat[kind], scalar=nthr[:, kind:kind + 1], in1=le_mask,
                                           op0=ALU.is_ge, op1=ALU.subtract).then_inc(q_ready, 1)

            def product(n, s):
                v.wait_ge(gate_scaled, n + 1)
                v.tensor_tensor(gate_s[s], pair[1][:, s * H:(s + 1) * H], gate_s[s], ALU.mult).then_inc(prod_done, 1)

            def result(g, tt):
                v.wait_ge(down_done, TPG * g + tt + 1)
                v.wait_ge(res_loaded[tt], 16 * g + 16)
                v.scalar_tensor_tensor(out=res[tt], in0=pair[tt][:, :], scalar=out_c[:, 0:1], in1=res[tt],
                                       op0=ALU.mult, op1=ALU.add).then_inc(res_done, 1)

            def widen_down(g, ic, c):
                v.tensor_copy(wide[down_slot(g, c)], at(q_down, ic)).then_inc(down_wide[1], 1)

            def finish(g):
                v.wait_ge(gu_done, g * IC + IC - 1)
                widen_down(g, 1, 1)
                product(g * IC + IC - 1, 1)
                widen_down(g, 3, 3)
                with v.Fori(0, (IC - 6) // 4) as i:
                    for c in (1, 3):
                        v.wait_ge(down_step, g * (IC - 2) + 4 * i + c + 1)
                        widen_down(g, 4 * i + c + 4, c)
                v.wait_ge(down_step, g * (IC - 2) + IC - 4)
                widen_down(g, IC - 1, 1)
                for tt in range(TPG):
                    result(g, tt)

            ternary(0, 1)
            ternary(1, 2)
            with v.Fori(0, IC // 2 - 2) as i:
                for s in range(2):
                    ternary(2 * i + s + 2, 2 * i + s + 3)
                    product(2 * i + s, s)
            ternary(IC - 2, IC - 1)
            product(IC - 4, 0)
            ternary(IC - 1, IC, last=True)
            product(IC - 3, 1)
            product(IC - 2, 0)
            v.wait_ge(q_stored, 3 * IC)
            finish(0)
            for g in range(1, NG):
                with v.Fori(0, IC // 2 - 1) as i:
                    for s in range(2):
                        product(g * IC + 2 * i + s, s)
                product(g * IC + IC - 2, 0)
                finish(g)


_INS = ['x', 'itok_B_3_7', 'itok_B_0_15', 'L0_cond_weights', 'L0_ffn_weight', 'L0_ffn_lora_A', 'L0_ffn_lora_B',
        'L0_ffn_gw1', 'L0_ffn_gb1', 'L0_ffn_ln_gamma', 'L0_ffn_ln_beta', 'L0_ffn_gw2', 'L0_ffn_gb2',
        'L1_cond_weight', 'L1_ffn_w_gate', 'L1_ffn_w_up', 'L1_ffn_w_down']


def kernel(**inputs):
    import numpy as _np
    import concourse.bacc as _bacc
    from concourse import mybir as _mybir
    from concourse.bass_utils import run_bass_kernel_spmd as _run

    nc = _bacc.Bacc("TRN2", target_bir_lowering=False, num_devices=1, dynamic_dma_scratch_size=1024)
    arrays, args = {}, []
    for name in _INS:
        a = _np.ascontiguousarray(inputs[name])
        arrays[f"in_{name}"] = a
        args.append(nc.dram_tensor(f"in_{name}", a.shape, _mybir.dt.from_np(a.dtype), kind="ExternalInput").ap())
    args.append(nc.dram_tensor("out", (NB, SEQ, D), F32, kind="ExternalOutput").ap())
    build_program(nc, *args)
    r = _run(nc, [arrays], core_ids=[0])
    return r.results[0]["out"]
```

```python
from contextlib import ExitStack

import concourse.bass as bass
from concourse import mybir

F32 = mybir.dt.float32
F16 = mybir.dt.float16
I8 = mybir.dt.int8
I32 = mybir.dt.int32
U8 = mybir.dt.uint8
ALU = mybir.AluOpType
ACT = mybir.ActivationFunctionType
X = mybir.AxisListType.X
ds = bass.ds

P = 128
NB, SEQ, D = 32, 64, 1024
NTOK = NB * SEQ
NT = NTOK // P
KC = D // P
H = D // 2
E, R, GH = 8, 16, 32
ER = E * R
CAPACITY = 3 * NTOK // E
NADP = 8
NSLOT = (NB + NADP) // 2
INNER = 2752
IC = (INNER + P - 1) // P
LAST = INNER - (IC - 1) * P
GRP = 512
NG = NTOK // GRP
TPG = GRP // P
READ_DUMMY, WRITE_DUMMY, SECOND_DUMMY = NB, NB + 2, NB + 3
ACT_COLS = (NB + 4) * SEQ

ACT_SCALE = 2.0 ** 4
WGT_SCALE = 2.0 ** 10
PROD = ACT_SCALE * WGT_SCALE
INTER_SCALE = 2.0 ** 6
LN_EPS = 1e-5
Q_EPS = 1e-5

NPIECE = 16
PIECE = INNER * D // P // NPIECE

F_PERM, F_COND, F_READ, F_WRITE, F_SECOND, F_RANK, F_ADP, F_CUM, F_USED = 0, 32, 64, 84, 104, 124, 144, 152, 160
NFIELD = 161


def build_program(nc, x, adapter_id, cond_id, cond_w, w0, lora_a, lora_b, gw1, gb1, ln_g, ln_b, gw2, gb2,
                  w1, w_gate, w_up, w_down, out):
    ctx = ExitStack()
    with ctx:
        def sb(name, shape, dt):
            return ctx.enter_context(nc.sbuf_tensor(name, shape, dt))

        def sem(name):
            return ctx.enter_context(nc.semaphore(name))

        w1t_dram = nc.dram_tensor("w1t_scratch", [NADP, KC, P, 2 * KC * P], F16, kind="Internal").ap()
        x1_dram = nc.dram_tensor("x1_scratch", [NTOK, D], F32, kind="Internal").ap()

        act_t = sb("act_t", [P, 2, KC, ACT_COLS], F16)
        region_q = sb("region_q", [P, 66 * 1024], U8)
        region_w = sb("region_w", [P, 64 * 1024], U8)
        region_s = sb("region_s", [P, 8 * 1024], U8)
        region_g = sb("region_g", [P, 8 * 1024], U8)

        def view(region, kb, dims, dt):
            n = 1
            for d in dims:
                n *= d
            at = int(kb * 1024)
            size = {F32: 4, I32: 4, F16: 2, I8: 1}[dt]
            v = region[:, at:at + n * size].bitcast(dt)
            names = "abcd"[:len(dims)]
            if len(dims) == 1:
                return v
            return v.rearrange(f"p ({' '.join(names)}) -> p {' '.join(names)}", **dict(zip(names, dims)))

        w_nat = [view(region_q, 4 * i, [D], F32) for i in range(4)]
        w_split = [view(region_q, 16 + 4 * i, [2, KC, P], F16) for i in range(4)]
        x_nat = [view(region_q, 32 + 4 * i, [D], F32) for i in range(2)]
        x1_nat = [view(region_q, 40 + 4 * i, [D], F32) for i in range(2)]
        mix_nat = [x_nat[0], x_nat[1], view(region_q, 48, [D], F32), view(region_q, 52, [D], F32)]
        gw1_nat = x1_nat[0]
        tmpw_t = view(region_q, 48, [2, NTOK], F16)
        lora_a_nat = view(region_q, 56, [KC, E, R], F32)
        lora_b_nat = x1_nat[1]
        lb = view(region_q, 60, [2, D], F16)
        gate_prod = view(region_q, 16, [NT // 2, E, GH], F32)
        w0_t = view(region_w, 0, [KC, 2, KC, P], F16)
        cond_bd = view(region_w, 32, [NT, P], F32)
        tmp = view(region_w, 40, [NT, ER + GH], F32)
        ag = view(region_w, 50, [2, KC, ER + GH], F16)
        tmpw = view(region_s, 0, [NT, E, R], F32)
        w1_t = region_w[:, :].bitcast(F16).rearrange("p (b o s k c) -> p b o s k c", b=2, o=KC, s=2, k=KC)
        z_nat = [view(region_q, 58 + 4 * i, [D], F32) for i in range(2)]
        stat_in = [view(region_q, 18 * i, [3, PIECE], F32) for i in range(2)]
        q_gate = view(region_q, 0, [KC, IC * P], I8)
        q_up = view(region_q, 22, [KC, IC * P], I8)
        q_down = view(region_q, 44, [IC, D], I8)
        inter = view(region_w, 0, [2, IC, GRP], F16)
        gate_s = [view(region_w, 44 + 2 * i, [GRP], F32) for i in range(2)]
        res = [view(region_w, 48 + 4 * i, [D], F32) for i in range(TPG)]
        wq_nat = [view(region_w, 48 + 4 * i, [D], F32) for i in range(3)]
        wide = [view(region_g, 2 * i, [D], F16) for i in range(4)]
        wq_early = [view(region_q, 46 + 4 * i, [D], F32) for i in range(3)]
        q16 = [view(region_s, 2 * i, [D], F16) for i in range(3)]
        le_mask = view(region_s, 6, [D], F16)

        ident = sb("ident", [P, P], F32)
        ident16 = sb("ident16", [P, P], F16)
        ones = sb("ones", [P, P], F32)
        g1b = sb("g1b", [P, GH], F32)
        lng = sb("lng", [P, GH], F32)
        lnb = sb("lnb", [P, GH], F32)
        g2w = view(region_q, 64, [E * GH], F32)
        g2b = sb("g2b", [P, E], F32)
        iota_i = sb("iota_i", [P, NB], I32)
        part_i = sb("part_i", [P, 1], I32)
        iota = sb("iota", [P, NB], F32)
        stat = sb("stat", [P, 3, NPIECE], F32)
        ssum = sb("ssum", [P, 4], F32)
        mean = sb("mean", [P, 4], F32)
        thr = sb("thr", [P, 4], F32)
        nthr = sb("nthr", [P, 4], F32)
        inter_c = sb("inter_c", [P, 1], F32)
        out_c = sb("out_c", [P, 1], F32)
        ixi = sb("ixi", [1, NFIELD], I32)
        ids_row_i = view(region_g, 0, [NB], I32)[0:NB]
        ids_col_i = view(region_g, 0.125, [2], I32)[0:NB]
        odd_i = view(region_g, 0.15625, [1], I32)[0:NB]
        ix_rows = view(region_g, 0.25, [12, NB], F32)[0:NB]
        ix_cols = view(region_g, 1.75, [24], F32)[0:NB]
        ix_adp_r, ix_key_r, ix_tmp, ix_onehot, ix_adp_b, ix_lt, ix_le, ix_shift, ix_pair, ix_run, ix_upto = \
            [ix_rows[:, i, :] for i in range(11)]
        ix_pair, ix_run, ix_upto = ix_pair[:, 0:NSLOT], ix_run[:, 0:NADP], ix_upto[:, 0:NADP]
        ix_part, ix_adp, ix_cnd, ix_key, ix_rank, ix_adps, ix_adps1, ix_first, ix_since, ix_start, ix_new, \
            ix_before, ix_gm, ix_nxt, ix_used, ix_last = [ix_cols[:, i:i + 1] for i in range(16)]
        ix_v = [ix_cols[:, 16 + i:17 + i] for i in range(4)]
        hid = view(region_g, 2, [NT, GH], F32)
        hid2 = gate_prod[:, 0:2, :, :].rearrange("p a b c -> p (a b c)").rearrange("p (a b) -> p a b", a=NT)
        row = view(region_g, 4, [8, NT], F32)
        gts = view(region_g, 5, [6, NT, E], F32)
        cnt = sb("cnt", [P, 2, E], F32)
        okay = sb("okay", [P, 2, E], F32)

        pair = [ctx.enter_context(nc.psum_tensor(f"pair{i}", [P, D], F32)) for i in range(4)]

        def q_bank(ic, kind):
            return bank16((6, 7, 6 if isinstance(ic, int) and ic < 2 else 4)[kind])

        ix_ps = pair[0]

        def bank16(i):
            return pair[i // 2][:, (i % 2) * H:(i % 2 + 1) * H].bitcast(F16)

        ids_loaded = sem("ids_loaded")
        small_loaded = sem("small_loaded")
        gw1_loaded = sem("gw1_loaded")
        lora_loaded = sem("lora_loaded")
        w_loaded = [sem(f"w_loaded{i}") for i in range(4)]
        mix_loaded = [sem(f"mix_loaded{i}") for i in range(4)]
        cond_loaded = [sem(f"cond_loaded{i}") for i in range(4)]
        x_loaded = [sem(f"x_loaded{i}") for i in range(2)]
        consts_ready = sem("consts_ready")
        index_step = sem("index_step")
        index_sorted = sem("index_sorted")
        index_sum = sem("index_sum")
        index_ready = sem("index_ready")
        gw1_transposed = sem("gw1_transposed")
        ag_high = sem("ag_high")
        ag_low = sem("ag_low")
        w_transposed = sem("w_transposed")
        w_high = sem("w_high")
        w_low = sem("w_low")
        w_stored = [sem(f"w_stored{i}") for i in range(4)]
        y_done = sem("y_done")
        y_high = sem("y_high")
        y_low = sem("y_low")
        tmp_done = sem("tmp_done")
        tmp_copied = sem("tmp_copied")
        gate_step = sem("gate_step")
        gate_half = sem("gate_half")
        var_ready = sem("var_ready")
        gap_ready = sem("gap_ready")
        count_ready = sem("count_ready")
        tmpw_ready = sem("tmpw_ready")
        gate_std = sem("gate_std")
        gate_exp = sem("gate_exp")
        counted = sem("counted")
        tmpw_transposed = sem("tmpw_transposed")
        tmpw_high = sem("tmpw_high")
        tmpw_low = sem("tmpw_low")
        acc_released = sem("acc_released")
        main_done = sem("main_done")
        x1_transposed = sem("x1_transposed")
        x1_high = sem("x1_high")
        x1_low = sem("x1_low")
        x1_stored = [sem(f"x1_stored{i}") for i in range(2)]
        w1_loaded = sem("w1_loaded")
        stat_loaded = [sem(f"stat_loaded{i}") for i in range(2)]
        stat_done = sem("stat_done")
        stat_summed = sem("stat_summed")
        stat_step = sem("stat_step")
        mean_done = sem("mean_done")
        scales_ready = sem("scales_ready")
        z_done = sem("z_done")
        z_copied_a = sem("z_copied_a")
        z_copied_v = sem("z_copied_v")
        z_transposed = sem("z_transposed")
        z_high = sem("z_high")
        z_low = sem("z_low")
        wq_loaded = [sem(f"wq_loaded{i}") for i in range(3)]
        mask_ready = sem("mask_ready")
        zeroed = sem("zeroed")
        q_ready = sem("q_ready")
        q_transposed = sem("q_transposed")
        q_stored = sem("q_stored")
        gate_wide = sem("gate_wide")
        up_wide = sem("up_wide")
        down_wide = [sem(f"down_wide{i}") for i in range(2)]
        down_step = sem("down_step")
        gu_done = sem("gu_done")
        gate_scaled = sem("gate_scaled")
        prod_done = sem("prod_done")
        inter_high = sem("inter_high")
        inter_low = sem("inter_low")
        down_done = sem("down_done")
        res_loaded = [sem(f"res_loaded{i}") for i in range(TPG)]
        res_done = sem("res_done")
        out_stored = [sem(f"out_stored{i}") for i in range(TPG)]

        x_rows = x.rearrange("b c t -> (b c) t")
        out_rows = out.rearrange("b c t -> (b c) t")
        cond_rows = cond_w.rearrange("b c t -> (b c) t")
        w1_rows = w1.rearrange("a o i -> (a o) i")
        w1t_rows = w1t_dram.rearrange("a o p n -> (a o) p n")

        def loop(eng, start, end):
            return nc.Fori(start, end, engines=bass.OrderedEngineSet([eng.engine]), hint_back_edge=True)

        def wait_if(eng, sem, n):
            if not isinstance(n, int) or n > 0:
                eng.wait_ge(sem, n)

        def at(a, i):
            if isinstance(i, int):
                return a[:, i]
            names = "bcd"[:len(a.shape) - 2]
            return a[:, ds(i, 1)].rearrange(f"p x {' '.join(names)} -> p (x {names[0]}) {' '.join(names[1:])}")

        def widen_half(g, ic):
            return (ic + g) % 2

        def down_slot(g, c):
            return 2 * ((c % 4 // 2 + g) % 2) + c % 2

        def chunked(a):
            return a.rearrange("p (k c) -> p k c", k=KC)

        def field(eng, at, i, hi, least=0):
            return eng.value_load(ixi[0:1, ds(at + i, 1)], min_val=least, max_val=hi)

        NPREP0 = KC
        W0_PAIR = (3, 1, 0, 2)
        INDEX_ALL = 7

        def prep_slot(r1):
            return r1 % 2 if r1 < KC else r1 % 4

        def loads(t, q):
            return 16 * (2 + (KC // 2 if q < 2 else 0) + t - 1)

        def stores(t, q):
            return 16 * ((KC // 2 if q < 2 else 0) + t - 2)

        block = ctx.enter_context(nc.Block())

        @block.sync
        def _(sp):
            def load_w(rows, r, slot):
                wait_if(sp, w_transposed, r - 3)
                sp.dma_start(w_nat[slot], rows).then_inc(w_loaded[slot], 16)

            def load_pair(dst, done, t):
                b0 = field(sp, F_PERM, 2 * t, NB - 1)
                b1 = field(sp, F_PERM, 2 * t + 1, NB - 1)
                sp.dma_start(dst[0:SEQ, :], x_rows[ds(b0 * SEQ, SEQ), :]).then_inc(done, 16)
                sp.dma_start(dst[SEQ:P, :], x_rows[ds(b1 * SEQ, SEQ), :]).then_inc(done, 16)

            def load_mix(t, slot):
                wait_if(sp, y_done, t - 3)
                load_pair(mix_nat[slot], mix_loaded[slot], t)

            wd_view = w_down.rearrange("(t p) i -> p t i", p=P)

            def load_q(ic, place, again, last=False):
                n = LAST if last else P
                for kind, src in enumerate((w_gate, w_up)):
                    if again:
                        sp.wait_ge(q_ready, 3 * ic - 2 + kind)
                    sp.dma_start(place[kind][0:n, :], src[(IC - 1) * P:INNER, :] if last else src[ds(ic * P, P), :])\
                      .then_inc(wq_loaded[kind], 16)
                if again:
                    sp.wait_ge(q_ready, 3 * ic)
                sp.dma_start(place[2].rearrange("p (t i) -> p t i", t=KC)[:, :, 0:n],
                             wd_view[:, :, (IC - 1) * P:INNER] if last else wd_view[:, :, ds((ic - 1) * P + P, P)])\
                  .then_inc(wq_loaded[2], 16)

            sp.dma_start(ids_row_i, adapter_id.partition_broadcast(NB)).then_inc(ids_loaded, 16)
            sp.dma_start(ids_col_i[:, 0:1], adapter_id.unsqueeze(1)).then_inc(ids_loaded, 16)
            sp.dma_start(ids_col_i[:, 1:2], cond_id.unsqueeze(1)).then_inc(ids_loaded, 16)
            sp.dma_start(gw1_nat[0:GH, :], gw1).then_inc(gw1_loaded, 16)
            for r in range(4):
                load_w(w0[r * P:(r + 1) * P, :], r, r)
            sp.wait_ge(index_ready, 1)
            load_mix(0, 0)
            for r in range(4, 6):
                load_w(w0[r * P:(r + 1) * P, :], r, r % 4)
            load_mix(1, 1)
            for r in range(6, NPREP0):
                load_w(w0[r * P:(r + 1) * P, :], r, r % 4)
            for k in range(KC):
                sp.dma_start(lora_a_nat[:, k], lora_a[:, k * P:(k + 1) * P, :].rearrange("e i r -> i e r"))\
                  .then_inc(lora_loaded, 16)
            sp.dma_start(lora_b_nat, lora_b.rearrange("e r o -> (e r) o")).then_inc(lora_loaded, 16)
            for t in range(2, 4):
                load_mix(t, t)
            for dst, src in ((g1b[:, :], gb1), (lng[:, :], ln_g), (lnb[:, :], ln_b),
                             (g2w, gw2.rearrange("e h -> (e h)")), (g2b[:, :], gb2)):
                sp.dma_start(dst, src.partition_broadcast(P)).then_inc(small_loaded, 16)
            sp.wait_ge(index_ready, INDEX_ALL)
            row_0 = field(sp, F_ADP, 0, NADP - 1) * D
            for o in range(2):
                load_w(w1_rows[ds(row_0 + o * P, P), :], NPREP0 + o, o)
            with sp.Fori(1, 4) as i:
                row_0 = field(sp, F_ADP, 0, NADP - 1) * D
                for c in range(4):
                    if c < 2:
                        load_w(w1_rows[ds(row_0 + 2 * i * P + c * P, P), :], NPREP0 + 2 * i + c + 2, c)
                    load_mix(4 * i + c, c)
            for t in range(2):
                sp.wait_ge(y_done, NT)
                load_pair(x_nat[t], x_loaded[t], t)
            sp.wait_ge(w_transposed, NPREP0 + KC)
            with sp.Fori(1, NT // 2) as i:
                for s in range(2):
                    t = 2 * i + s
                    used = field(sp, F_USED, 0, NADP)
                    row_i = field(sp, F_ADP, i, NADP - 1) * D
                    with sp.If(used > i):
                        for q in range(4):
                            load_w(w1_rows[ds(row_i + (4 * s + q) * P, P), :], NPREP0 + 4 * t + q, q)
                    sp.wait_ge(acc_released, t - 1)
                    load_pair(x_nat[s], x_loaded[s], t)

            def load_rank(r):
                sp.dma_start(region_w[:, ((r + 1) % 2) * 32768:((r + 1) % 2 + 1) * 32768].bitcast(F16)
                             .rearrange("p (o n) -> p o n", o=KC),
                             w1t_dram[r].rearrange("o p n -> p o n")).then_inc(w1_loaded, 16)

            sp.wait_ge(tmpw_low, 2)
            for s in range(2):
                sp.wait_ge(w_stored[s], 16 * KC // 2)
            load_rank(0)
            sp.wait_ge(main_done, NT)
            used = field(sp, F_USED, 0, NADP)
            for r in range(1, NADP):
                before = field(sp, F_CUM, r - 2, NSLOT, least=1) if r >= 2 else None
                with sp.If(used > r):
                    for s in range(4):
                        sp.wait_ge(w_stored[s], stores(2 * r + 2, s))
                    sp.wait_ge(w1_loaded, 16 * r)
                    if r >= 2:
                        sp.wait_ge(z_done, before)
                    load_rank(r)
            load_q(0, wq_early, False)
            load_q(1, wq_early, True)
            sp.wait_ge(z_done, NSLOT)
            with sp.Fori(2, IC - 1) as ic:
                load_q(ic, wq_nat, True)
            load_q(IC - 1, wq_nat, True, last=True)

            def load_res(m, slot):
                sp.dma_start(res[slot], x1_dram[ds(m * P, P), :]).then_inc(res_loaded[slot], 16)

            def store_out(m, slot):
                b0 = field(sp, F_PERM, 2 * m, NB - 1)
                b1 = field(sp, F_PERM, 2 * m + 1, NB - 1)
                sp.wait_ge(res_done, m + 1)
                sp.dma_start(out_rows[ds(b0 * SEQ, SEQ), :], res[slot][0:SEQ, :]).then_inc(out_stored[slot], 16)
                sp.dma_start(out_rows[ds(b1 * SEQ, SEQ), :], res[slot][SEQ:P, :]).then_inc(out_stored[slot], 16)

            sp.wait_ge(q_ready, 3 * IC)
            for s in range(2):
                sp.wait_ge(x1_stored[s], 16 * NT // 2)
            for s in range(TPG):
                load_res(s, s)
            for s in range(TPG):
                store_out(s, s)
            with sp.Fori(1, NG) as g:
                for s in range(TPG):
                    sp.wait_ge(out_stored[s], 32 * g)
                    load_res(TPG * g + s, s)
                for s in range(TPG):
                    store_out(TPG * g + s, s)
            for s in range(TPG):
                sp.wait_ge(out_stored[s], 32 * NG)

        @block.gpsimd
        def _(pool):
            pool.iota(iota_i[:, :], pattern=[[1, NB]], base=0, channel_multiplier=0).then_inc(consts_ready, 1)
            pool.iota(part_i[:, :], pattern=[[0, 1]], base=0, channel_multiplier=1).then_inc(consts_ready, 1)
            pool.memset(ones[:, :], 1.0).then_inc(consts_ready, 1)
            pool.memset(ident[:, :], 0.0).then_inc(consts_ready, 1)
            pool.memset(ident16[:, :], 0.0).then_inc(consts_ready, 1)
            pool.wait_ge(consts_ready, 5)
            for m in (ident, ident16):
                pool.affine_select(out=m[:, :], in_=m[:, :], compare_op=ALU.not_equal, fill=1.0, base=0,
                                   pattern=[[-1, P]], channel_multiplier=1).then_inc(consts_ready, 1)
            pool.memset(cond_bd, 0.0).then_inc(consts_ready, 1)

            def load_cond(t, slot):
                c0 = field(pool, F_COND, 2 * t, 15)
                c1 = field(pool, F_COND, 2 * t + 1, 15)
                wait_if(pool, cond_loaded[slot], 8 * (t - slot))
                pool.dma_start(at(cond_bd[0:SEQ], t)[:, 0:SEQ], cond_rows[ds(c0 * SEQ, SEQ), :])\
                    .then_inc(cond_loaded[slot], 16)
                pool.dma_start(at(cond_bd[SEQ:P], t)[:, SEQ:P], cond_rows[ds(c1 * SEQ, SEQ), :])\
                    .then_inc(cond_loaded[slot], 16)

            pool.wait_ge(index_ready, 1)
            pool.wait_ge(consts_ready, 8)
            for t in range(4):
                load_cond(t, t)
            with pool.Fori(1, 4) as i:
                for c in range(4):
                    load_cond(4 * i + c, c)
            pool.memset(act_t[:, :, :, NTOK:ACT_COLS], 0.0).then_inc(consts_ready, 1)

            def widen_up(g, ic, s):
                if g == 0:
                    pool.wait_ge(q_stored, 3 * ic + 2)
                pool.tensor_copy(chunked(wide[2 * widen_half(g, s) + 1]), q_up[:, :, ds(ic * P, P)])\
                    .then_inc(up_wide, 1)

            def low_inter(g, ic, s):
                pool.wait_ge(inter_high, g * IC + ic + 1)
                pool.tensor_tensor(at(inter[:, 1], ic), gate_s[s], at(inter[:, 0], ic), ALU.subtract)\
                    .then_inc(inter_low, 1)

            for g in range(NG):
                wait_if(pool, down_step, g * (IC - 2))
                widen_up(g, 0, 0)
                wait_if(pool, down_done, TPG * g)
                widen_up(g, 1, 1)
                with pool.Fori(0, IC // 2 - 1) as i:
                    for s in range(2):
                        pool.wait_ge(gu_done, g * IC + 2 * i + s + 1)
                        widen_up(g, 2 * i + s + 2, s)
                        low_inter(g, 2 * i + s, s)
                low_inter(g, IC - 2, 0)
                low_inter(g, IC - 1, 1)

        @block.tensor
        def _(pe):
            def transpose8(dst, src, idn):
                for k in range(KC):
                    mm = pe.transpose(dst[:, k * P:(k + 1) * P], src[:, k * P:(k + 1) * P], idn[:, :])
                return mm

            def prep(r, slot, loads, p, free):
                pe.wait_ge(w_loaded[slot], loads)
                wait_if(pe, w_low, free)
                transpose8(pair[p], w_nat[slot], ident).then_inc(w_transposed, 1)

            def ix_sum(dst, lhs, rhs):
                return pe.matmul(dst, lhs, rhs, start=True, stop=True)

            def prep_w0(r):
                if r == 2:
                    pe.wait_ge(index_ready, INDEX_ALL)
                if r == 3:
                    pe.wait_ge(ag_low, 1)
                prep(r, r % 4, 16 * (r // 4 + 1), W0_PAIR[r % 4], r - 3)

            pe.wait_ge(consts_ready, 3)
            pe.wait_ge(index_sorted, 1)
            ix_sum(ix_ps[0:1, 0:NB], ix_part, ix_onehot)
            ix_sum(ix_ps[0:1, NB:2 * NB], ix_cnd, ix_onehot)
            ix_sum(ix_ps[0:NB, 64:96], ix_adp_b, ix_onehot)
            ix_sum(ix_ps[0:NB, 96:97], ix_onehot, ix_adp).then_inc(index_sum, 1)
            pe.wait_ge(consts_ready, 7)
            prep_w0(0)
            pe.wait_ge(index_sorted, 2)
            ix_sum(ix_ps[0:NB, 97:98], ix_lt, ix_start)
            ix_sum(ix_ps[0:NB, 98:99], ix_le, ix_new)
            ix_sum(ix_ps[0:NB, 99:100], ix_shift, ix_adps1)
            ix_sum(ix_ps[0:NB, 100:101], ones[0:NB, 0:NB], ix_new).then_inc(index_sum, 1)
            prep_w0(1)
            pe.wait_ge(index_sorted, 3)
            for f, v_ in ((F_READ, ix_v[0]), (F_WRITE, ix_v[1]), (F_SECOND, ix_v[2]), (F_RANK, ix_v[3])):
                ix_sum(ix_ps[0:1, 128 + f:128 + f + NSLOT], v_, ix_pair)
            ix_sum(ix_ps[0:1, 128 + F_ADP:128 + F_ADP + NADP], ix_adps, ix_run)
            ix_sum(ix_ps[0:1, 128 + F_CUM:128 + F_CUM + NADP], ones[0:NB, 0:1], ix_upto).then_inc(index_sum, 1)

            pe.wait_ge(gw1_loaded, 16)
            for k in range(KC):
                mm = pe.transpose(pair[2][:, k * GH:(k + 1) * GH], gw1_nat[0:GH, k * P:(k + 1) * P],
                                  ident[0:GH, 0:GH])
            mm.then_inc(gw1_transposed, 1)
            for r in range(2, NPREP0):
                prep_w0(r)

            def mix(t, slot, s, loads):
                pe.wait_ge(mix_loaded[slot], loads)
                pe.wait_ge(cond_loaded[slot], loads)
                wait_if(pe, y_low, t - 1)
                for k in range(KC):
                    mm = pe.matmul(pair[s][:, k * P:(k + 1) * P], mix_nat[slot][:, k * P:(k + 1) * P],
                                   at(cond_bd, t), start=True, stop=True)
                mm.then_inc(y_done, 1)

            def gate(t, s):
                pe.wait_ge(y_low, t + 1)
                wait_if(pe, tmp_copied, t - 1)
                dst = pair[2][:, s * H:s * H + ER + GH]
                n = 0
                for k in range(KC):
                    for a, b in ((0, 0), (0, 1), (1, 0)):
                        mm = pe.matmul(dst, act_t[:, a, k, ds(t * P, P)], ag[:, b, k, :],
                                       start=(n == 0), stop=(n == 3 * KC - 1))
                        n += 1
                mm.then_inc(tmp_done, 1)

            pe.wait_ge(w_low, NPREP0 - 1)
            mix(0, 0, 0, 32)
            pe.wait_ge(ag_low, 3)
            for t in range(1, 4):
                mix(t, t, t % 2, 32)
                gate(t - 1, (t - 1) % 2)
                if t % 2 == 1:
                    prep(NPREP0 + t // 2, t // 2, 16 * 3, 3, NPREP0 + t // 2)
            with loop(pe, 1, 4) as i:
                for c in range(4):
                    mix(4 * i + c, c, c % 2, 32 * i + 32)
                    gate(4 * i + c - 1, (c - 1) % 2)
                    if c % 2 == 1:
                        o = 2 * i + c // 2
                        prep(NPREP0 + o, c // 2, 16 * i + 48, 3, NPREP0 + o)
            gate(NT - 1, 1)

            def main(t, s, q):
                if q == 0:
                    wait_if(pe, acc_released, t - 1)
                for k in (2 * q, 2 * q + 1):
                    for a, b in ((0, 0), (0, 1), (1, 0)):
                        for h in range(2):
                            pe.matmul(pair[s][:, h * H:(h + 1) * H], act_t[:, a, k, ds(t * P, P)],
                                      w0_t[:, 4 * h:4 * h + 4, b, k, :],
                                      start=(k == 0 and a + b == 0), stop=False)

            def lora(t, s):
                for a, b in ((0, 0), (0, 1), (1, 0)):
                    for h in range(2):
                        mm = pe.matmul(pair[s][:, h * H:(h + 1) * H], tmpw_t[:, a, ds(t * P, P)],
                                       lb[:, b, h * H:(h + 1) * H], start=False, stop=(a == 1))
                mm.then_inc(main_done, 1)

            def turn_x1(t, s):
                pe.wait_ge(acc_released, t + 1)
                wait_if(pe, x1_low, t)
                transpose8(pair[2], x1_nat[s], ident).then_inc(x1_transposed, 1)

            pe.wait_ge(y_low, NT)
            for t in range(2):
                for q in range(4):
                    main(t, t, q)
            pe.wait_ge(count_ready, 1)
            pe.matmul(pair[3][:, 0:2 * E], ones[:, :], cnt[:, :, :].rearrange("p a b -> p (a b)"),
                      start=True, stop=True).then_inc(counted, 1)
            pe.wait_ge(tmpw_ready, 1)
            pe.wait_ge(tmp_copied, NT)
            for t in range(NT):
                mm = pe.transpose(pair[2 + t // 8][:, (t % 8) * P:(t % 8 + 1) * P],
                                  tmpw[:, t, :, :].rearrange("p a b -> p (a b)"), ident[:, :])
                if t % 8 == 7:
                    mm.then_inc(tmpw_transposed, 1)
            pe.wait_ge(tmpw_low, 2)
            lora(0, 0)
            lora(1, 1)
            turn_x1(0, 0)

            def layer0(i):
                used = field(pe, F_USED, 0, NADP)
                for s in range(2):
                    t = 2 * i + s
                    main(t, s, 0)
                    turn_x1(t - 1, 1 - s)
                    with pe.If(used > i):
                        for q in range(4):
                            prep(NPREP0 + 4 * t + q, q, loads(t, q), 3, NPREP0 + 4 * t + q)
                            if q < 3:
                                main(t, s, q + 1)
                    with pe.If(used <= i):
                        for q in range(1, 4):
                            main(t, s, q)
                    lora(t, s)

            with loop(pe, 1, NT // 2) as i:
                layer0(i)

            def linear(k, s):
                rank = field(pe, F_RANK, k, NADP - 1)
                at = field(pe, F_READ, k, NB * SEQ)
                pe.wait_ge(w1_loaded, rank * 16 + 16)
                wait_if(pe, z_copied_a, k - 1)
                wait_if(pe, z_copied_v, k - 1)
                buf = (rank + 1) % 2
                n = 0
                for c in range(KC):
                    for a, b in ((0, 0), (0, 1), (1, 0)):
                        for h in range(2):
                            mm = pe.matmul(pair[s][:, h * H:(h + 1) * H], act_t[:, a, c, ds(at, P)],
                                           w1_t[:, ds(buf, 1), 4 * h:4 * h + 4, b, c, :].rearrange("p x o c -> p (x o) c"),
                                           start=(n == 0), stop=(n == 3 * KC - 1))
                        n += 1
                mm.then_inc(z_done, 1)

            def linear_t(k, s):
                pe.wait_ge(z_copied_a, k + 1)
                pe.wait_ge(z_copied_v, k + 1)
                pe.wait_ge(x1_low, NT) if isinstance(k, int) and k == 0 else wait_if(pe, z_low, k)
                transpose8(pair[2], z_nat[s], ident).then_inc(z_transposed, 1)

            pe.wait_ge(consts_ready, 9)
            def layer1(i):
                linear(2 * i + 1, 1)
                linear_t(2 * i, 0)
                linear(2 * i + 2, 0)
                linear_t(2 * i + 1, 1)

            pe.wait_ge(x1_low, 2)
            pe.wait_ge(acc_released, NT)
            linear(0, 0)
            turn_x1(NT - 1, 1)
            linear(1, 1)
            linear_t(0, 0)
            pe.wait_ge(x1_low, NT)
            linear(2, 0)
            linear_t(1, 1)
            with loop(pe, 1, NSLOT // 2 - 2) as i:
                layer1(i)

            def turn_q(ic, kinds=(0, 1, 2)):
                for kind in kinds:
                    pe.wait_ge(q_ready, 3 * ic + kind + 1)
                    if isinstance(ic, int) and ic < 2 and kind == 2:
                        pe.wait_ge(q_stored, 3 * ic + 1)
                    elif isinstance(ic, int) and 0 < ic <= 2 and kind == 0:
                        pe.wait_ge(q_stored, 3 * ic)
                    elif not isinstance(ic, int) or ic > 0:
                        pe.wait_ge(q_stored, 3 * ic - 2 + kind)
                    transpose8(q_bank(ic, kind), q16[kind], ident16).then_inc(q_transposed, 1)

            linear(NSLOT - 3, 1)
            pe.wait_ge(stat_summed, 1)
            pe.matmul(pair[3][:, 0:3], ones[:, :], ssum[:, 0:3], start=True, stop=True).then_inc(mean_done, 1)
            linear_t(NSLOT - 4, 0)
            linear(NSLOT - 2, 0)
            turn_q(0, (0, 1))
            linear_t(NSLOT - 3, 1)
            turn_q(0, (2,))
            linear(NSLOT - 1, 1)
            turn_q(1, (0, 1))
            linear_t(NSLOT - 2, 0)
            turn_q(1, (2,))
            linear_t(NSLOT - 1, 1)

            def gate_up(g, ic, s):
                n = g * IC + ic
                pe.wait_ge(gate_wide, n + 1)
                pe.wait_ge(up_wide, n + 1)
                wait_if(pe, prod_done, n - 1)
                half = widen_half(g, s)
                for w, dst in ((wide[2 * half], pair[0]), (wide[2 * half + 1], pair[1])):
                    for k in range(KC):
                        for a in range(2):
                            mm = pe.matmul(dst[:, s * H:(s + 1) * H], w[:, k * P:(k + 1) * P],
                                           act_t[:, a, k, g * GRP:(g + 1) * GRP],
                                           start=(k == 0 and a == 0), stop=(k == KC - 1 and a == 1))
                mm.then_inc(gu_done, 1)

            def down(ic, tt, slot):
                for a in range(2):
                    for h in range(2):
                        mm = pe.matmul(pair[tt][:, h * H:(h + 1) * H], at(inter[:, a], ic)[:, tt * P:(tt + 1) * P],
                                       wide[slot][:, h * H:(h + 1) * H],
                                       start=(isinstance(ic, int) and ic == 0 and a == 0),
                                       stop=(isinstance(ic, int) and ic == IC - 1 and a == 1))
                return mm

            def down_chunk(g, ic, c):
                pe.wait_ge(down_wide[c % 2], IC // 2 * g + (ic - c % 2) // 2 + 1)
                for tt in (2, 3, 0, 1):
                    if g > 0 and isinstance(ic, int) and ic == 0 and tt == 2:
                        pe.wait_ge(res_done, TPG * g)
                    if isinstance(ic, int) and ic == 0 and tt == 0:
                        pe.wait_ge(prod_done, IC * (g + 1))
                    mm = down(ic, tt, down_slot(g, c))
                mm.then_inc(down_step, 1)

            for g in range(NG):
                if g == 0:
                    gate_up(0, 0, 0)
                    pe.wait_ge(z_low, NSLOT)
                    turn_q(2)
                    gate_up(0, 1, 1)
                    with loop(pe, 1, IC // 2 - 1) as i:
                        for s in range(2):
                            turn_q(2 * i + s + 1)
                            gate_up(0, 2 * i + s, s)
                    turn_q(IC - 1)
                    gate_up(0, IC - 2, 0)
                    gate_up(0, IC - 1, 1)
                    pe.wait_ge(q_stored, 3 * IC)
                else:
                    pe.wait_ge(res_done, TPG * (g - 1) + 2)
                    with loop(pe, 0, IC // 2) as i:
                        for s in range(2):
                            gate_up(g, 2 * i + s, s)
                pe.wait_ge(inter_low, IC * (g + 1) - 2)
                for c in range(4):
                    down_chunk(g, c, c)
                with loop(pe, 1, (IC - 2) // 4) as i:
                    for c in range(4):
                        down_chunk(g, 4 * i + c, c)
                for c in range(2):
                    pe.wait_ge(down_wide[c], IC // 2 * (g + 1))
                pe.wait_ge(inter_low, IC * (g + 1))
                for tt in range(TPG):
                    for c in range(2):
                        mm = down(IC - 2 + c, tt, down_slot(g, c))
                    mm.then_inc(down_done, 1)

        @block.scalar
        def _(act):
            def high(dst, src, scale):
                return act.activation(dst, src, ACT.Copy, scale=scale)

            ps8 = [p[:, :].rearrange("p (k c) -> p k c", k=KC) for p in pair]

            def high_w0(r):
                act.wait_ge(w_transposed, r + 1)
                high(w0_t[:, r, 0], ps8[W0_PAIR[r % 4]], WGT_SCALE).then_inc(w_high, 1)

            high_w0(0)
            high_w0(1)
            act.wait_ge(gw1_transposed, 1)
            high(ag[:, 0, :, ER:ER + GH], pair[2][:, 0:KC * GH].rearrange("p (k c) -> p k c", k=KC),
                 WGT_SCALE).then_inc(ag_high, 1)
            for r in range(2, NPREP0):
                high_w0(r)
            act.wait_ge(lora_loaded, 16 * (KC + 1))
            high(ag[:, 0, :, 0:ER], lora_a_nat.rearrange("p k e r -> p k (e r)"), WGT_SCALE).then_inc(ag_high, 1)
            high(lb[:, 0, :], lora_b_nat, WGT_SCALE).then_inc(ag_high, 1)

            def y_part(t, s):
                act.wait_ge(y_done, t + 1)
                high(act_t[:, 0, :, ds(t * P, P)], ps8[s], ACT_SCALE).then_inc(y_high, 1)

            def tmp_part(t, s):
                act.wait_ge(tmp_done, t + 1)
                high(at(tmp, t),
                     pair[2][:, s * H:s * H + ER + GH], 1.0 / PROD).then_inc(tmp_copied, 1)

            def w_part(r1, slot, before):
                act.wait_ge(w_transposed, NPREP0 + r1 + 1)
                wait_if(act, w_stored[slot], before)
                high(w_split[slot][:, 0], ps8[3], WGT_SCALE).then_inc(w_high, 1)

            def store_w(r1, slot):
                act.wait_ge(w_low, NPREP0 + r1 + 1)
                act.dma_start(w1t_rows[ds(r1, 1)].rearrange("a p n -> (a p) n"),
                              w_split[slot].rearrange("p s k c -> p (s k c)")).then_inc(w_stored[slot], 16)

            y_part(0, 0)
            for t in range(1, 4):
                y_part(t, t % 2)
                tmp_part(t - 1, (t - 1) % 2)
                if t % 2 == 1:
                    w_part(t // 2, t // 2, 0)
                else:
                    store_w(t // 2 - 1, t // 2 - 1)
            with act.Fori(1, 4) as i:
                for c in range(4):
                    y_part(4 * i + c, c % 2)
                    tmp_part(4 * i + c - 1, (c - 1) % 2)
                    o = 2 * i + c // 2
                    if c % 2 == 1:
                        w_part(o, c // 2, 16 * i)
                    else:
                        store_w(o - 1, (c // 2 - 1) % 2)
            tmp_part(NT - 1, 1)
            store_w(KC - 1, 1)

            act.wait_ge(var_ready, 1)
            act.activation(row[:, 2, :], row[:, 1, :], ACT.Sqrt).then_inc(gate_std, 1)
            act.wait_ge(gap_ready, 1)
            act.activation(row[:, 5, :], row[:, 4, :], ACT.Exp).then_inc(gate_exp, 1)
            for i in range(2):
                act.wait_ge(tmpw_transposed, i + 1)
                high(tmpw_t[:, 0, i * D:(i + 1) * D], pair[2 + i][:, :], 1.0).then_inc(tmpw_high, 1)

            def x1_part(t, s):
                act.wait_ge(x1_transposed, t + 1)
                high(act_t[:, 0, :, ds(t * P, P)], ps8[2], ACT_SCALE).then_inc(x1_high, 1)
                act.dma_start(x1_dram[ds(t * P, P), :], x1_nat[s]).then_inc(x1_stored[s], 16)

            def layer0(i):
                for s in range(2):
                    t = 2 * i + s
                    x1_part(t - 1, 1 - s)
                    used = field(act, F_USED, 0, NADP)
                    with act.If(used > i):
                        for q in range(4):
                            w_part(4 * t + q, q, stores(t, q))
                            if q > 0:
                                store_w(4 * t + q - 1, q - 1)
                        store_w(4 * t + 3, 3)

            x1_part(0, 0)
            layer0(1)
            with act.Fori(2, NT // 2) as i:
                layer0(i)
            x1_part(NT - 1, 1)

            flat = [w.rearrange("a b -> (a b)").rearrange("(p n) -> p n", p=P) for w in (w_gate, w_up, w_down)]

            def load_piece(p, s):
                if not isinstance(p, int):
                    act.wait_ge(stat_done, p - 1)
                for w in range(3):
                    act.dma_start(stat_in[s][:, w, :], flat[w][:, ds(p * PIECE, PIECE)])\
                       .then_inc(stat_loaded[s], 16)

            def copy_z(k, s):
                act.wait_ge(z_done, k + 1)
                high(z_nat[s][:, 0:H], pair[s][:, 0:H], 1.0 / PROD).then_inc(z_copied_a, 1)

            def high_z(k):
                d0 = field(act, F_WRITE, k, WRITE_DUMMY * SEQ)
                d1 = field(act, F_SECOND, k, SECOND_DUMMY * SEQ)
                act.wait_ge(z_transposed, k + 1)
                high(act_t[:, 0, :, ds(d0, SEQ)], ps8[2][:, :, 0:SEQ], ACT_SCALE)
                high(act_t[:, 0, :, ds(d1, SEQ)], ps8[2][:, :, SEQ:P], ACT_SCALE).then_inc(z_high, 1)

            for s in range(2):
                act.wait_ge(w_stored[s], stores(2, s))
            used = field(act, F_USED, 0, NADP)
            for r in range(1, NADP):
                with act.If(used > r):
                    for s in range(4):
                        act.wait_ge(w_stored[s], stores(2 * r + 2, s))
            load_piece(0, 0)
            load_piece(1, 1)
            copy_z(0, 0)

            def layer1(i, more):
                copy_z(2 * i + 1, 1)
                high_z(2 * i)
                if more:
                    load_piece(2 * i + 2, 0)
                copy_z(2 * i + 2, 0)
                high_z(2 * i + 1)
                if more:
                    load_piece(2 * i + 3, 1)

            with act.Fori(0, NPIECE // 2 - 1) as i:
                layer1(i, True)
            layer1(NPIECE // 2 - 1, False)

            def store_q(ic, kinds=(0, 1, 2)):
                for kind in kinds:
                    act.wait_ge(q_transposed, 3 * ic + kind + 1)
                    src = q_bank(ic, kind)
                    if kind < 2:
                        dst = (q_gate, q_up)[kind][:, :, ds(ic * P, P)]
                        src = src.rearrange("p (k c) -> p k c", k=KC)
                    else:
                        dst = at(q_down, ic)
                    act.activation(dst, src, ACT.Copy).then_inc(q_stored, 1)

            def inter_part(g, ic, s):
                n = g * IC + ic
                act.wait_ge(gu_done, n + 1)
                wait_if(act, inter_low, n - 1)
                act.activation(gate_s[s], pair[0][:, s * H:(s + 1) * H], ACT.Copy, scale=inter_c[:, 0:1])\
                   .then_inc(gate_scaled, 1)
                act.wait_ge(prod_done, n + 1)
                high(at(inter[:, 0], ic), gate_s[s], 1.0).then_inc(inter_high, 1)

            def widen_gate(g, ic, s):
                if g == 0:
                    act.wait_ge(q_stored, 3 * ic + 1)
                act.activation(chunked(wide[2 * widen_half(g, s)]), q_gate[:, :, ds((ic - 1) * P + P, P)], ACT.Copy)\
                   .then_inc(gate_wide, 1)

            def widen_down(g, ic, c):
                act.activation(wide[down_slot(g, c)], at(q_down, ic), ACT.Copy).then_inc(down_wide[0], 1)

            copy_z(NSLOT - 3, 1)
            high_z(NSLOT - 4)
            copy_z(NSLOT - 2, 0)
            for s in range(2):
                act.wait_ge(x1_stored[s], 16 * NT // 2)
            act.wait_ge(scales_ready, 1)
            store_q(0, (0, 1))
            high_z(NSLOT - 3)
            store_q(0, (2,))
            widen_gate(0, 0, 0)
            copy_z(NSLOT - 1, 1)
            store_q(1, (0, 1))
            high_z(NSLOT - 2)
            store_q(1, (2,))
            high_z(NSLOT - 1)
            widen_gate(0, 1, 1)
            for g in range(NG):
                if g > 0:
                    act.wait_ge(down_step, g * (IC - 2))
                    widen_gate(g, 0, 0)
                    act.wait_ge(down_done, TPG * g)
                    widen_gate(g, 1, 1)
                inter_part(g, 0, 0)
                with act.Fori(0, IC // 2 - 1) as i:
                    for s in range(2):
                        ic = 2 * i + 1 + s
                        if g == 0:
                            store_q(ic + 1)
                        if g > 0:
                            act.wait_ge(gu_done, g * IC + ic)
                        widen_gate(g, ic + 1, s)
                        inter_part(g, ic, 1 - s)
                if g == 0:
                    act.wait_ge(q_stored, 3 * IC)
                widen_down(g, 0, 0)
                inter_part(g, IC - 1, 1)
                widen_down(g, 2, 2)
                with act.Fori(0, (IC - 6) // 4) as i:
                    for c in (0, 2):
                        act.wait_ge(down_step, g * (IC - 2) + 4 * i + c + 1)
                        widen_down(g, 4 * i + c + 4, c)
                act.wait_ge(down_step, g * (IC - 2) + IC - 5)
                widen_down(g, IC - 2, 0)

        @block.vector
        def _(v):
            ps8 = [p[:, :].rearrange("p (k c) -> p k c", k=KC) for p in pair]

            def low(dst, src, scale, hi):
                return v.scalar_tensor_tensor(out=dst, in0=src, scalar=scale, in1=hi,
                                              op0=ALU.mult, op1=ALU.subtract)

            step = [0]

            def then(instruction):
                step[0] += 1
                instruction.then_inc(index_step, 1)
                v.wait_ge(index_step, step[0])

            def compare(dst, row, column, op, scale=None):
                if scale is None:
                    return v.tensor_scalar(dst, row, column, None, op)
                return v.tensor_scalar(dst, row, column, scale, op, ALU.mult)

            nums = iota[0:NB, :]
            v.wait_ge(consts_ready, 2)
            then(v.tensor_copy(iota[:, :], iota_i[:, :]))
            then(v.tensor_copy(ix_part, part_i[0:NB, :]))
            v.wait_ge(ids_loaded, 48)
            then(v.tensor_copy(ix_adp, ids_col_i[:, 0:1]))
            then(v.tensor_copy(ix_cnd, ids_col_i[:, 1:2]))
            then(v.tensor_copy(ix_adp_r, ids_row_i))
            then(v.scalar_tensor_tensor(out=ix_key_r, in0=ix_adp_r, scalar=float(NB), in1=nums,
                                        op0=ALU.mult, op1=ALU.add))
            then(v.scalar_tensor_tensor(out=ix_key, in0=ix_adp, scalar=float(NB), in1=ix_part,
                                        op0=ALU.mult, op1=ALU.add))
            then(v.tensor_copy(ix_adp_b, ix_adp.broadcast_to([NB, NB])))
            then(compare(ix_tmp, ix_key_r, ix_key, ALU.is_lt))
            then(v.tensor_reduce(ix_rank, ix_tmp, X, ALU.add))
            compare(ix_onehot, nums, ix_rank, ALU.is_equal).then_inc(index_sorted, 1)
            v.tensor_scalar(ix_lt, nums, ix_part, None, ALU.is_gt).then_inc(index_step, 1)
            v.tensor_scalar(ix_le, nums, ix_part, None, ALU.is_ge).then_inc(index_step, 1)
            v.tensor_scalar(ix_shift, nums, 1.0, ix_part, ALU.add, ALU.is_equal).then_inc(index_step, 1)
            step[0] += 3
            v.wait_ge(index_sum, 1)
            v.tensor_copy(ixi[:, 0:F_READ], ix_ps[0:1, 0:2 * NB]).then_inc(index_ready, 1)
            then(v.tensor_copy(ix_adps, ix_ps[0:NB, 96:97]))
            then(v.tensor_scalar(ix_adps1, ix_adps, 1.0, None, ALU.add))
            then(compare(ix_tmp, ix_ps[0:NB, 64:96], ix_adps, ALU.is_lt))
            then(v.tensor_reduce(ix_first, ix_tmp, X, ALU.add))
            then(v.tensor_tensor(ix_since, ix_part, ix_first, ALU.subtract))
            then(v.tensor_copy(odd_i, ix_since))
            then(v.tensor_scalar(odd_i, odd_i, 1, None, ALU.bitwise_and))
            then(v.tensor_copy(ix_start, odd_i))
            then(v.tensor_scalar(ix_start, ix_start, -1.0, 1.0, ALU.mult, ALU.add))
            v.tensor_scalar(ix_new, ix_since, 0.0, None, ALU.is_equal).then_inc(index_sorted, 1)
            v.wait_ge(index_sum, 2)
            then(v.tensor_copy(ix_before, ix_ps[0:NB, 97:98]))
            then(v.tensor_scalar(ix_gm, ix_ps[0:NB, 98:99], -1.0, None, ALU.add))
            then(v.tensor_tensor(ix_nxt, ix_ps[0:NB, 99:100], ix_adps1, ALU.is_equal))
            then(v.tensor_copy(ix_used, ix_ps[0:NB, 100:101]))
            then(v.tensor_scalar(ix_last, ix_used, -1.0, None, ALU.add))
            then(v.tensor_scalar(ix_v[0], ix_part, float(SEQ), float(-READ_DUMMY * SEQ), ALU.mult, ALU.add))
            then(v.tensor_scalar(ix_v[1], ix_part, float(SEQ), float(-WRITE_DUMMY * SEQ), ALU.mult, ALU.add))
            then(v.tensor_scalar(ix_v[2], ix_part, float(SEQ), float((1 - SECOND_DUMMY) * SEQ), ALU.mult, ALU.add))
            then(v.tensor_tensor(ix_v[2], ix_v[2], ix_nxt, ALU.mult))
            then(v.tensor_tensor(ix_v[3], ix_gm, ix_last, ALU.subtract))
            then(compare(ix_pair, nums[:, 0:NSLOT], ix_before, ALU.is_equal, ix_start))
            then(compare(ix_run, nums[:, 0:NADP], ix_gm, ALU.is_equal, ix_new))
            compare(ix_upto, nums[:, 0:NADP], ix_gm, ALU.is_ge, ix_start).then_inc(index_sorted, 1)
            v.wait_ge(index_sum, 3)
            for f, dummy in ((F_READ, float(READ_DUMMY * SEQ)), (F_WRITE, float(WRITE_DUMMY * SEQ)),
                             (F_SECOND, float(SECOND_DUMMY * SEQ)), (F_RANK, ix_last[0:1])):
                v.tensor_scalar(ixi[:, f:f + NSLOT], ix_ps[0:1, 128 + f:128 + f + NSLOT], dummy, None, ALU.add)\
                 .then_inc(index_ready, 1)
            v.tensor_copy(ixi[:, F_ADP:F_USED], ix_ps[0:1, 128 + F_ADP:128 + F_USED]).then_inc(index_ready, 1)
            v.tensor_copy(ixi[:, F_USED:NFIELD], ix_used[0:1]).then_inc(index_ready, 1)

            def low_w0(r):
                v.wait_ge(w_high, r + 1)
                low(w0_t[:, r, 1], ps8[W0_PAIR[r % 4]], WGT_SCALE, w0_t[:, r, 0]).then_inc(w_low, 1)

            low_w0(0)
            low_w0(1)
            v.wait_ge(ag_high, 1)
            low(ag[:, 1, :, ER:ER + GH], pair[2][:, 0:KC * GH].rearrange("p (k c) -> p k c", k=KC),
                WGT_SCALE, ag[:, 0, :, ER:ER + GH]).then_inc(ag_low, 1)
            for r in range(2, NPREP0):
                low_w0(r)
            v.wait_ge(ag_high, 3)
            low(lb[:, 1, :], lora_b_nat, WGT_SCALE, lb[:, 0, :]).then_inc(ag_low, 1)
            low(ag[:, 1, :, 0:ER], lora_a_nat.rearrange("p k e r -> p k (e r)"), WGT_SCALE,
                ag[:, 0, :, 0:ER]).then_inc(ag_low, 1)

            def low_y(t, s):
                v.wait_ge(y_high, t + 1)
                low(act_t[:, 1, :, ds(t * P, P)], ps8[s], ACT_SCALE, act_t[:, 0, :, ds(t * P, P)])\
                    .then_inc(y_low, 1)

            def low_w(r1, slot):
                v.wait_ge(w_high, NPREP0 + r1 + 1)
                low(w_split[slot][:, 1], ps8[3], WGT_SCALE, w_split[slot][:, 0]).then_inc(w_low, 1)

            for t in range(4):
                low_y(t, t % 2)
                if t % 2 == 1:
                    low_w(t // 2, t // 2)
            with v.Fori(1, 4) as i:
                for c in range(4):
                    low_y(4 * i + c, c % 2)
                    if c % 2 == 1:
                        low_w(2 * i + c // 2, c // 2)

            count = [0]

            def gthen(instruction):
                count[0] += 1
                instruction.then_inc(gate_step, 1)
                v.wait_ge(gate_step, count[0])

            def per_channel(a, n=NT):
                return a.unsqueeze(1).broadcast_to([P, n, a.shape[1]])

            def per_token(a, n):
                return a.unsqueeze(2).broadcast_to([P, NT, n])

            total, var, std, rstd, gap, ex, p1, p2 = [row[:, i, :] for i in range(8)]
            gt, one1, one2, gl, is_top, wgt = [gts[:, i] for i in range(6)]
            hd = hid[:, :, :]
            v.wait_ge(small_loaded, 80)
            v.wait_ge(tmp_copied, NT)
            for s in range(2):
                v.wait_ge(w_stored[s], 16 * KC // 2)
            gthen(v.tensor_tensor(hd, tmp[:, :, ER:ER + GH], per_channel(g1b[:, :]), ALU.add))
            gthen(v.tensor_reduce(total, hd, X, ALU.add))
            gthen(v.tensor_scalar(total, total, 1.0 / GH, None, ALU.mult))
            gthen(v.tensor_tensor(hd, hd, per_token(total, GH), ALU.subtract))
            gthen(v.tensor_tensor(hid2, hd, hd, ALU.mult))
            gthen(v.tensor_reduce(var, hid2, X, ALU.add))
            v.tensor_scalar(var, var, 1.0 / GH, LN_EPS, ALU.mult, ALU.add).then_inc(var_ready, 1)
            v.wait_ge(gate_std, 1)
            gthen(v.reciprocal(rstd, std))
            gthen(v.tensor_tensor(gap, rstd, rstd, ALU.mult))
            gthen(v.tensor_tensor(gap, gap, var, ALU.mult))
            gthen(v.tensor_scalar(gap, gap, -0.5, 1.5, ALU.mult, ALU.add))
            gthen(v.tensor_tensor(rstd, rstd, gap, ALU.mult))
            gthen(v.tensor_tensor(hd, hd, per_token(rstd, GH), ALU.mult))
            gthen(v.tensor_tensor(hd, hd, per_channel(lng[:, :]), ALU.mult))
            gthen(v.tensor_tensor(hd, hd, per_channel(lnb[:, :]), ALU.add))
            gthen(v.tensor_scalar(hd, hd, 0.0, None, ALU.max))
            g2 = g2w[:, :].rearrange("p (e h) -> p e h", e=E)
            hf = NT // 2
            for half in range(2):
                for tt in range(hf):
                    v.tensor_tensor(gate_prod[:, tt], hid[:, half * hf + tt, :].unsqueeze(1).broadcast_to([P, E, GH]),
                                    g2, ALU.mult).then_inc(gate_half, 1)
                v.wait_ge(gate_half, hf * (half + 1))
                gthen(v.tensor_reduce(gt[:, half * hf:(half + 1) * hf, :], gate_prod, X, ALU.add))
            gthen(v.tensor_tensor(gt, gt, per_channel(g2b[:, :]), ALU.add))

            def choose(top, one):
                gthen(v.tensor_reduce(top, gt, X, ALU.max))
                gthen(v.tensor_tensor(is_top, gt, per_token(top, E), ALU.is_equal))
                gthen(v.scalar_tensor_tensor(out=gl, in0=is_top, scalar=-float(E), in1=per_channel(iota[:, 0:E]),
                                             op0=ALU.mult, op1=ALU.add))
                gthen(v.tensor_reduce(total, gl, X, ALU.min))
                gthen(v.tensor_tensor(one, gl, per_token(total, E), ALU.is_equal))

            choose(p1, one1)
            gthen(v.scalar_tensor_tensor(out=gt, in0=one1, scalar=-3.0e38, in1=gt, op0=ALU.mult, op1=ALU.add))
            choose(p2, one2)
            v.tensor_tensor(gap, p2, p1, ALU.subtract).then_inc(gap_ready, 1)
            gthen(v.tensor_reduce(cnt[:, 0, :], one1.rearrange("p t e -> p e t"), X, ALU.add))
            v.tensor_reduce(cnt[:, 1, :], one2.rearrange("p t e -> p e t"), X, ALU.add).then_inc(count_ready, 1)
            v.wait_ge(gate_exp, 1)
            gthen(v.tensor_scalar(p1, ex, 1.0, None, ALU.add))
            gthen(v.reciprocal(p1, p1))
            gthen(v.tensor_tensor(p2, ex, p1, ALU.mult))
            v.wait_ge(counted, 1)
            gthen(v.tensor_scalar(okay[:, :, :], pair[3][:, 0:2 * E].rearrange("p (a b) -> p a b", a=2),
                                  float(CAPACITY), None, ALU.is_le))
            gthen(v.tensor_tensor(one1, one1, per_channel(okay[:, 0, :]), ALU.mult))
            gthen(v.tensor_tensor(one2, one2, per_channel(okay[:, 1, :]), ALU.mult))
            gthen(v.tensor_tensor(one1, one1, per_token(p1, E), ALU.mult))
            gthen(v.tensor_tensor(one2, one2, per_token(p2, E), ALU.mult))
            gthen(v.tensor_tensor(wgt, one1, one2, ALU.add))
            for e in range(E):
                ins = v.tensor_tensor(tmpw[:, :, e, :], tmp[:, :, e * R:(e + 1) * R],
                                      wgt[:, :, e].unsqueeze(2).broadcast_to([P, NT, R]), ALU.mult)
            ins.then_inc(tmpw_ready, 1)
            for i in range(2):
                v.wait_ge(tmpw_high, i + 1)
                low(tmpw_t[:, 1, i * D:(i + 1) * D], pair[2 + i][:, :], 1.0, tmpw_t[:, 0, i * D:(i + 1) * D])\
                    .then_inc(tmpw_low, 1)

            def residual(t, s):
                v.wait_ge(main_done, t + 1)
                v.wait_ge(x_loaded[s], 32 * (t // 2 + 1) if isinstance(t, int) else 16 * t + 32 - 16 * s)
                wait_if(v, x1_stored[s], 8 * (t - s))
                v.scalar_tensor_tensor(out=x1_nat[s], in0=pair[s][:, :], scalar=1.0 / PROD, in1=x_nat[s],
                                       op0=ALU.mult, op1=ALU.add).then_inc(acc_released, 1)

            def low_x1(t):
                v.wait_ge(x1_high, t + 1)
                low(act_t[:, 1, :, ds(t * P, P)], ps8[2], ACT_SCALE, act_t[:, 0, :, ds(t * P, P)])\
                    .then_inc(x1_low, 1)

            residual(0, 0)
            residual(1, 1)
            low_x1(0)
            with v.Fori(1, NT // 2) as i:
                for s in range(2):
                    t = 2 * i + s
                    low_x1(t - 1)
                    used = field(v, F_USED, 0, NADP)
                    with v.If(used > i):
                        for q in range(4):
                            low_w(4 * t + q, q)
                    residual(t, s)
            low_x1(NT - 1)

            def copy_z(k, s):
                v.wait_ge(z_done, k + 1)
                v.tensor_scalar(z_nat[s][:, H:D], pair[s][:, H:D], 1.0 / PROD, None, ALU.mult).then_inc(z_copied_v, 1)

            def low_z(k, last=False):
                d0 = field(v, F_WRITE, k, WRITE_DUMMY * SEQ)
                d1 = field(v, F_SECOND, k, SECOND_DUMMY * SEQ)
                v.wait_ge(z_high, k + 1)
                low(act_t[:, 1, :, ds(d0, SEQ)], ps8[2][:, :, 0:SEQ], ACT_SCALE, act_t[:, 0, :, ds(d0, SEQ)])
                low(act_t[:, 1, :, ds(d1, SEQ)], ps8[2][:, :, SEQ:P], ACT_SCALE, act_t[:, 0, :, ds(d1, SEQ)])\
                    .then_inc(z_low, 1)

            def sum_piece(i, s):
                v.wait_ge(stat_loaded[s], 48 * i + 48)
                v.tensor_reduce(stat[:, :, ds(2 * i + s, 1)].rearrange("p a b -> p (a b)"), stat_in[s], X, ALU.add,
                                apply_absolute_value=True).then_inc(stat_done, 1)

            def layer1(i, sums):
                copy_z(2 * i + 1, 1)
                low_z(2 * i)
                if sums:
                    sum_piece(i, 0)
                copy_z(2 * i + 2, 0)
                low_z(2 * i + 1)
                if sums:
                    sum_piece(i, 1)

            copy_z(0, 0)
            with v.Fori(0, NPIECE // 2) as i:
                layer1(i, True)
            v.wait_ge(stat_done, NPIECE)
            v.tensor_reduce(ssum[:, 0:3], stat[:, :, :], X, ALU.add).then_inc(stat_summed, 1)
            def ternary(ic, n_load, last=False):
                place = wq_early if isinstance(ic, int) and ic < 2 else wq_nat
                for kind in range(3):
                    if not isinstance(ic, int) or ic > 0:
                        v.wait_ge(q_transposed, 3 * ic - 2 + kind)
                    if last and kind < 2:
                        v.memset(place[kind][LAST:P, :], 0.0).then_inc(zeroed, 1)
                    if last and kind == 2:
                        v.memset(chunked(place[2])[:, :, LAST:P], 0.0).then_inc(zeroed, 1)
                    if last:
                        v.wait_ge(zeroed, kind + 1)
                    v.wait_ge(wq_loaded[kind], 16 * n_load)
                    if not isinstance(ic, int) or 3 * ic + kind > 0:
                        v.wait_ge(q_ready, 3 * ic + kind)
                    v.tensor_scalar(le_mask, place[kind], thr[:, kind:kind + 1], None, ALU.is_le).then_inc(mask_ready, 1)
                    v.wait_ge(mask_ready, 3 * ic + kind + 1)
                    v.scalar_tensor_tensor(out=q16[kind], in0=place[kind], scalar=nthr[:, kind:kind + 1], in1=le_mask,
                                           op0=ALU.is_ge, op1=ALU.subtract).then_inc(q_ready, 1)

            def product(n, s):
                v.wait_ge(gate_scaled, n + 1)
                v.tensor_tensor(gate_s[s], pair[1][:, s * H:(s + 1) * H], gate_s[s], ALU.mult).then_inc(prod_done, 1)

            def result(g, tt):
                v.wait_ge(down_done, TPG * g + tt + 1)
                v.wait_ge(res_loaded[tt], 16 * g + 16)
                v.scalar_tensor_tensor(out=res[tt], in0=pair[tt][:, :], scalar=out_c[:, 0:1], in1=res[tt],
                                       op0=ALU.mult, op1=ALU.add).then_inc(res_done, 1)

            def widen_down(g, ic, c):
                v.tensor_copy(wide[down_slot(g, c)], at(q_down, ic)).then_inc(down_wide[1], 1)

            def finish(g):
                v.wait_ge(gu_done, g * IC + IC - 1)
                widen_down(g, 1, 1)
                product(g * IC + IC - 1, 1)
                widen_down(g, 3, 3)
                with v.Fori(0, (IC - 6) // 4) as i:
                    for c in (1, 3):
                        v.wait_ge(down_step, g * (IC - 2) + 4 * i + c + 1)
                        widen_down(g, 4 * i + c + 4, c)
                v.wait_ge(down_step, g * (IC - 2) + IC - 4)
                widen_down(g, IC - 1, 1)
                for tt in range(TPG):
                    result(g, tt)

            copy_z(NSLOT - 3, 1)
            low_z(NSLOT - 4)
            v.wait_ge(mean_done, 1)
            v.tensor_scalar(mean[:, 0:3], pair[3][:, 0:3], 1.0 / (INNER * D), None, ALU.mult).then_inc(stat_step, 1)
            v.wait_ge(stat_step, 1)
            v.tensor_scalar(thr[:, 0:3], mean[:, 0:3], Q_EPS, 0.5, ALU.add, ALU.mult).then_inc(stat_step, 1)
            v.tensor_scalar(out_c[:, :], mean[:, 2:3], 1.0 / INTER_SCALE, None, ALU.mult).then_inc(stat_step, 1)
            v.scalar_tensor_tensor(out=inter_c[:, :], in0=mean[:, 0:1], scalar=INTER_SCALE / ACT_SCALE ** 2,
                                   in1=mean[:, 1:2], op0=ALU.mult, op1=ALU.mult).then_inc(stat_step, 1)
            v.wait_ge(stat_step, 4)
            v.tensor_scalar(nthr[:, 0:3], thr[:, 0:3], -1.0, None, ALU.mult).then_inc(scales_ready, 1)
            v.wait_ge(scales_ready, 1)
            ternary(0, 1)
            copy_z(NSLOT - 2, 0)
            low_z(NSLOT - 3)
            ternary(1, 2)
            copy_z(NSLOT - 1, 1)
            low_z(NSLOT - 2)
            low_z(NSLOT - 1)
            with v.Fori(0, IC // 2 - 2) as i:
                for s in range(2):
                    ternary(2 * i + s + 2, 2 * i + s + 3)
                    product(2 * i + s, s)
            ternary(IC - 2, IC - 1)
            product(IC - 4, 0)
            ternary(IC - 1, IC, last=True)
            product(IC - 3, 1)
            product(IC - 2, 0)
            v.wait_ge(q_stored, 3 * IC)
            finish(0)
            for g in range(1, NG):
                with v.Fori(0, IC // 2 - 1) as i:
                    for s in range(2):
                        product(g * IC + 2 * i + s, s)
                product(g * IC + IC - 2, 0)
                finish(g)


_INS = ['x', 'itok_B_3_7', 'itok_B_0_15', 'L0_cond_weights', 'L0_ffn_weight', 'L0_ffn_lora_A', 'L0_ffn_lora_B',
        'L0_ffn_gw1', 'L0_ffn_gb1', 'L0_ffn_ln_gamma', 'L0_ffn_ln_beta', 'L0_ffn_gw2', 'L0_ffn_gb2',
        'L1_cond_weight', 'L1_ffn_w_gate', 'L1_ffn_w_up', 'L1_ffn_w_down']


def kernel(**inputs):
    import numpy as _np
    import concourse.bacc as _bacc
    from concourse import mybir as _mybir
    from concourse.bass_utils import run_bass_kernel_spmd as _run

    nc = _bacc.Bacc("TRN2", target_bir_lowering=False, num_devices=1, dynamic_dma_scratch_size=1024)
    arrays, args = {}, []
    for name in _INS:
        a = _np.ascontiguousarray(inputs[name])
        arrays[f"in_{name}"] = a
        args.append(nc.dram_tensor(f"in_{name}", a.shape, _mybir.dt.from_np(a.dtype), kind="ExternalInput").ap())
    args.append(nc.dram_tensor("out", (NB, SEQ, D), F32, kind="ExternalOutput").ap())
    build_program(nc, *args)
    r = _run(nc, [arrays], core_ids=[0])
    return r.results[0]["out"]
```

```python
from contextlib import ExitStack

import concourse.bass as bass
from concourse import mybir

F32 = mybir.dt.float32
F16 = mybir.dt.float16
I8 = mybir.dt.int8
I32 = mybir.dt.int32
U8 = mybir.dt.uint8
ALU = mybir.AluOpType
ACT = mybir.ActivationFunctionType
X = mybir.AxisListType.X
ds = bass.ds

P = 128
NB, SEQ, D = 32, 64, 1024
NTOK = NB * SEQ
NT = NTOK // P
KC = D // P
H = D // 2
E, R, GH = 8, 16, 32
ER = E * R
CAPACITY = 3 * NTOK // E
NADP = 8
NSLOT = (NB + NADP) // 2
INNER = 2752
IC = (INNER + P - 1) // P
LAST = INNER - (IC - 1) * P
GRP = 512
NG = NTOK // GRP
TPG = GRP // P
READ_DUMMY, WRITE_DUMMY, SECOND_DUMMY = NB, NB + 2, NB + 3
ACT_COLS = (NB + 4) * SEQ

ACT_SCALE = 2.0 ** 4
WGT_SCALE = 2.0 ** 10
PROD = ACT_SCALE * WGT_SCALE
INTER_SCALE = 2.0 ** 6
LN_EPS = 1e-5
Q_EPS = 1e-5

NPIECE_G = 16
PIECE_G = INNER * D // P // NPIECE_G
NPIECE = 12
PIECE = -(-INNER * D // P // NPIECE)

F_PERM, F_COND, F_READ, F_WRITE, F_SECOND, F_RANK, F_ADP, F_CUM, F_USED = 0, 32, 64, 84, 104, 124, 144, 152, 160
NFIELD = 161


def build_program(nc, x, adapter_id, cond_id, cond_w, w0, lora_a, lora_b, gw1, gb1, ln_g, ln_b, gw2, gb2,
                  w1, w_gate, w_up, w_down, out):
    ctx = ExitStack()
    with ctx:
        def sb(name, shape, dt):
            return ctx.enter_context(nc.sbuf_tensor(name, shape, dt))

        def sem(name):
            return ctx.enter_context(nc.semaphore(name))

        w1t_dram = nc.dram_tensor("w1t_scratch", [NADP, KC, P, 2 * KC * P], F16, kind="Internal").ap()
        x1_dram = nc.dram_tensor("x1_scratch", [NTOK, D], F32, kind="Internal").ap()

        act_t = sb("act_t", [P, 2, KC, ACT_COLS], F16)
        region_q = sb("region_q", [P, 66 * 1024], U8)
        region_w = sb("region_w", [P, 64 * 1024], U8)
        region_s = sb("region_s", [P, 8 * 1024], U8)
        region_g = sb("region_g", [P, 8 * 1024], U8)

        def view(region, kb, dims, dt):
            n = 1
            for d in dims:
                n *= d
            at = int(kb * 1024)
            size = {F32: 4, I32: 4, F16: 2, I8: 1}[dt]
            v = region[:, at:at + n * size].bitcast(dt)
            names = "abcd"[:len(dims)]
            if len(dims) == 1:
                return v
            return v.rearrange(f"p ({' '.join(names)}) -> p {' '.join(names)}", **dict(zip(names, dims)))

        w_nat = [view(region_q, 4 * i, [D], F32) for i in range(4)]
        w_split = [view(region_q, 16 + 4 * i, [2, KC, P], F16) for i in range(4)]
        x_nat = [view(region_q, 32 + 4 * i, [D], F32) for i in range(2)]
        x1_nat = [view(region_q, 40 + 4 * i, [D], F32) for i in range(2)]
        mix_nat = [x_nat[0], x_nat[1], view(region_q, 48, [D], F32), view(region_q, 52, [D], F32)]
        gw1_nat = x1_nat[0]
        tmpw_t = view(region_q, 48, [2, NTOK], F16)
        lora_a_nat = view(region_q, 56, [KC, E, R], F32)
        lora_b_nat = x1_nat[1]
        lb = view(region_q, 60, [2, D], F16)
        gate_prod = view(region_q, 16, [NT // 2, E, GH], F32)
        w0_t = view(region_w, 0, [KC, 2, KC, P], F16)
        cond_bd = view(region_w, 32, [NT, P], F32)
        tmp = view(region_w, 40, [NT, ER + GH], F32)
        ag = view(region_w, 50, [2, KC, ER + GH], F16)
        tmpw = view(region_s, 0, [NT, E, R], F32)
        w1_t = region_w[:, :].bitcast(F16).rearrange("p (b o s k c) -> p b o s k c", b=2, o=KC, s=2, k=KC)
        z_nat = [view(region_q, 58 + 4 * i, [D], F32) for i in range(2)]
        stat_in = [view(region_q, 15 * i, [2, PIECE], F32) for i in range(2)]
        stat_gate = [view(r, 0, [PIECE_G], F32) for r in (region_s, region_g)]
        q_gate = view(region_q, 0, [KC, IC * P], I8)
        q_up = view(region_q, 22, [KC, IC * P], I8)
        q_down = view(region_q, 44, [IC, D], I8)
        inter = view(region_w, 0, [2, IC, GRP], F16)
        gate_s = [view(region_w, 44 + 2 * i, [GRP], F32) for i in range(2)]
        res = [view(region_w, 48 + 4 * i, [D], F32) for i in range(TPG)]
        wq_nat = [view(region_w, 48 + 4 * i, [D], F32) for i in range(3)]
        wide = [view(region_g, 2 * i, [D], F16) for i in range(4)]
        wq_early = [view(region_q, 46 + 4 * i, [D], F32) for i in range(3)]
        q16 = [view(region_s, 2 * i, [D], F16) for i in range(3)]
        le_mask = view(region_s, 6, [D], F16)

        ident = sb("ident", [P, P], F32)
        ident16 = sb("ident16", [P, P], F16)
        ones = sb("ones", [P, P], F32)
        g1b = sb("g1b", [P, GH], F32)
        lng = sb("lng", [P, GH], F32)
        lnb = sb("lnb", [P, GH], F32)
        g2w = view(region_q, 64, [E * GH], F32)
        g2b = sb("g2b", [P, E], F32)
        iota_i = sb("iota_i", [P, NB], I32)
        part_i = sb("part_i", [P, 1], I32)
        iota = sb("iota", [P, NB], F32)
        stat_g = sb("stat_g", [P, NPIECE_G], F32)
        stat = sb("stat", [P, 2, NPIECE], F32)
        ssum = sb("ssum", [P, 4], F32)
        mean = sb("mean", [P, 4], F32)
        thr = sb("thr", [P, 4], F32)
        nthr = sb("nthr", [P, 4], F32)
        inter_c = sb("inter_c", [P, 1], F32)
        out_c = sb("out_c", [P, 1], F32)
        ixi = sb("ixi", [1, NFIELD], I32)
        ids_row_i = view(region_g, 0, [NB], I32)[0:NB]
        ids_col_i = view(region_g, 0.125, [2], I32)[0:NB]
        odd_i = view(region_g, 0.15625, [1], I32)[0:NB]
        ix_rows = view(region_g, 0.25, [12, NB], F32)[0:NB]
        ix_cols = view(region_g, 1.75, [24], F32)[0:NB]
        ix_adp_r, ix_key_r, ix_tmp, ix_onehot, ix_adp_b, ix_lt, ix_le, ix_shift, ix_pair, ix_run, ix_upto = \
            [ix_rows[:, i, :] for i in range(11)]
        ix_pair, ix_run, ix_upto = ix_pair[:, 0:NSLOT], ix_run[:, 0:NADP], ix_upto[:, 0:NADP]
        ix_part, ix_adp, ix_cnd, ix_key, ix_rank, ix_adps, ix_adps1, ix_first, ix_since, ix_start, ix_new, \
            ix_before, ix_gm, ix_nxt, ix_used, ix_last = [ix_cols[:, i:i + 1] for i in range(16)]
        ix_v = [ix_cols[:, 16 + i:17 + i] for i in range(4)]
        hid = view(region_g, 2, [NT, GH], F32)
        hid2 = view(region_q, 24, [NT, GH], F32)
        row = view(region_g, 4, [8, NT], F32)
        gts = view(region_g, 5, [6, NT, E], F32)
        cnt = sb("cnt", [P, 2, E], F32)
        okay = sb("okay", [P, 2, E], F32)

        pair = [ctx.enter_context(nc.psum_tensor(f"pair{i}", [P, D], F32)) for i in range(4)]

        def q_bank(ic, kind):
            return bank16((6, 7, 6 if isinstance(ic, int) and ic < 2 else 4)[kind])

        ix_ps = pair[0]

        def bank16(i):
            return pair[i // 2][:, (i % 2) * H:(i % 2 + 1) * H].bitcast(F16)

        ids_loaded = sem("ids_loaded")
        small_loaded = sem("small_loaded")
        gw1_loaded = sem("gw1_loaded")
        lora_loaded = sem("lora_loaded")
        w_loaded = [sem(f"w_loaded{i}") for i in range(4)]
        mix_loaded = [sem(f"mix_loaded{i}") for i in range(4)]
        cond_loaded = [sem(f"cond_loaded{i}") for i in range(4)]
        x_loaded = [sem(f"x_loaded{i}") for i in range(2)]
        consts_ready = sem("consts_ready")
        index_step = sem("index_step")
        index_sorted = sem("index_sorted")
        index_sum = sem("index_sum")
        index_ready = sem("index_ready")
        gw1_transposed = sem("gw1_transposed")
        ag_high = sem("ag_high")
        ag_low = sem("ag_low")
        w_transposed = sem("w_transposed")
        w_high = sem("w_high")
        w_low = sem("w_low")
        w_stored = [sem(f"w_stored{i}") for i in range(4)]
        y_done = sem("y_done")
        y_high = sem("y_high")
        y_low = sem("y_low")
        tmp_done = sem("tmp_done")
        tmp_copied = sem("tmp_copied")
        gate_step = sem("gate_step")
        gate_half = sem("gate_half")
        var_ready = sem("var_ready")
        gap_ready = sem("gap_ready")
        count_ready = sem("count_ready")
        tmpw_ready = sem("tmpw_ready")
        gate_std = sem("gate_std")
        gate_exp = sem("gate_exp")
        counted = sem("counted")
        tmpw_transposed = sem("tmpw_transposed")
        tmpw_high = sem("tmpw_high")
        tmpw_low = sem("tmpw_low")
        acc_released = sem("acc_released")
        main_done = sem("main_done")
        x1_transposed = sem("x1_transposed")
        x1_high = sem("x1_high")
        x1_low = sem("x1_low")
        x1_stored = [sem(f"x1_stored{i}") for i in range(2)]
        w1_loaded = sem("w1_loaded")
        stat_loaded = [sem(f"stat_loaded{i}") for i in range(2)]
        stat_done = sem("stat_done")
        gate_loaded = [sem(f"gate_loaded{i}") for i in range(2)]
        gate_summed = sem("gate_summed")
        stat_summed = sem("stat_summed")
        stat_step = sem("stat_step")
        mean_done = sem("mean_done")
        scales_ready = sem("scales_ready")
        z_done = sem("z_done")
        z_copied_a = sem("z_copied_a")
        z_copied_v = sem("z_copied_v")
        z_transposed = sem("z_transposed")
        z_high = sem("z_high")
        z_low = sem("z_low")
        wq_loaded = [sem(f"wq_loaded{i}") for i in range(3)]
        mask_ready = sem("mask_ready")
        zeroed = sem("zeroed")
        q_ready = sem("q_ready")
        q_transposed = sem("q_transposed")
        q_stored = sem("q_stored")
        gate_wide = sem("gate_wide")
        up_wide = sem("up_wide")
        down_wide = [sem(f"down_wide{i}") for i in range(2)]
        down_step = sem("down_step")
        gu_done = sem("gu_done")
        gate_scaled = sem("gate_scaled")
        prod_done = sem("prod_done")
        tail_zeroed = sem("tail_zeroed")
        inter_high = sem("inter_high")
        inter_low = sem("inter_low")
        down_done = sem("down_done")
        res_loaded = [sem(f"res_loaded{i}") for i in range(TPG)]
        res_done = sem("res_done")
        out_stored = [sem(f"out_stored{i}") for i in range(TPG)]

        x_rows = x.rearrange("b c t -> (b c) t")
        out_rows = out.rearrange("b c t -> (b c) t")
        cond_rows = cond_w.rearrange("b c t -> (b c) t")
        w1_rows = w1.rearrange("a o i -> (a o) i")
        w1t_rows = w1t_dram.rearrange("a o p n -> (a o) p n")

        def loop(eng, start, end):
            return nc.Fori(start, end, engines=bass.OrderedEngineSet([eng.engine]), hint_back_edge=True)

        def wait_if(eng, sem, n):
            if not isinstance(n, int) or n > 0:
                eng.wait_ge(sem, n)

        def at(a, i):
            if isinstance(i, int):
                return a[:, i]
            names = "bcd"[:len(a.shape) - 2]
            return a[:, ds(i, 1)].rearrange(f"p x {' '.join(names)} -> p (x {names[0]}) {' '.join(names[1:])}")

        def widen_half(g, ic):
            return (ic + g) % 2

        def down_slot(g, c):
            return 2 * ((c % 4 // 2 + g) % 2) + c % 2

        def chunked(a):
            return a.rearrange("p (k c) -> p k c", k=KC)

        def field(eng, at, i, hi, least=0):
            return eng.value_load(ixi[0:1, ds(at + i, 1)], min_val=least, max_val=hi)

        wd_view = w_down.rearrange("(t p) i -> p t i", p=P)

        def load_q(eng, ic, place, again, last=False):
            n = LAST if last else P
            for kind, src in enumerate((w_gate, w_up)):
                if again:
                    eng.wait_ge(q_ready, 3 * ic - 2 + kind)
                eng.dma_start(place[kind][0:n, :], src[(IC - 1) * P:INNER, :] if last else src[ds(ic * P, P), :])\
                   .then_inc(wq_loaded[kind], 16)
                if last and kind == 0:
                    eng.dma_start(place[0][LAST:2 * LAST, :], w_up[(IC - 1) * P:INNER, :]).then_inc(wq_loaded[0], 16)
            if again:
                eng.wait_ge(q_ready, 3 * ic)
            eng.dma_start(place[2].rearrange("p (t i) -> p t i", t=KC)[:, :, 0:n],
                          wd_view[:, :, (IC - 1) * P:INNER] if last else wd_view[:, :, ds((ic - 1) * P + P, P)])\
               .then_inc(wq_loaded[2], 16)

        NPREP0 = KC
        W0_PAIR = (3, 1, 0, 2)
        INDEX_ALL = 7
        FIRST_OPTIONAL = NSLOT - 3

        def loads(t, q):
            return 16 * (2 + (KC // 2 if q < 2 else 0) + t - 1)

        def stores(t, q):
            return 16 * ((KC // 2 if q < 2 else 0) + t - 2)

        block = ctx.enter_context(nc.Block())

        @block.sync
        def _(sp):
            def load_w(rows, r, slot):
                wait_if(sp, w_transposed, r - 3)
                sp.dma_start(w_nat[slot], rows).then_inc(w_loaded[slot], 16)

            def load_pair(dst, done, t):
                b0 = field(sp, F_PERM, 2 * t, NB - 1)
                b1 = field(sp, F_PERM, 2 * t + 1, NB - 1)
                sp.dma_start(dst[0:SEQ, :], x_rows[ds(b0 * SEQ, SEQ), :]).then_inc(done, 16)
                sp.dma_start(dst[SEQ:P, :], x_rows[ds(b1 * SEQ, SEQ), :]).then_inc(done, 16)

            def load_mix(t, slot):
                wait_if(sp, y_done, t - 3)
                load_pair(mix_nat[slot], mix_loaded[slot], t)

            gate_flat = w_gate.rearrange("a b -> (a b)").rearrange("(p n) -> p n", p=P)

            def load_gate(p, s):
                wait_if(sp, gate_summed, p - 1)
                sp.dma_start(stat_gate[s], gate_flat[:, ds(p * PIECE_G, PIECE_G)]).then_inc(gate_loaded[s], 16)

            sp.dma_start(ids_row_i, adapter_id.partition_broadcast(NB)).then_inc(ids_loaded, 16)
            sp.dma_start(ids_col_i[:, 0:1], adapter_id.unsqueeze(1)).then_inc(ids_loaded, 16)
            sp.dma_start(ids_col_i[:, 1:2], cond_id.unsqueeze(1)).then_inc(ids_loaded, 16)
            sp.dma_start(gw1_nat[0:GH, :], gw1).then_inc(gw1_loaded, 16)
            for r in range(4):
                load_w(w0[r * P:(r + 1) * P, :], r, r)
            sp.wait_ge(index_ready, 1)
            load_mix(0, 0)
            for r in range(4, 6):
                load_w(w0[r * P:(r + 1) * P, :], r, r % 4)
            load_mix(1, 1)
            for r in range(6, NPREP0):
                load_w(w0[r * P:(r + 1) * P, :], r, r % 4)
            for k in range(KC):
                sp.dma_start(lora_a_nat[:, k], lora_a[:, k * P:(k + 1) * P, :].rearrange("e i r -> i e r"))\
                  .then_inc(lora_loaded, 16)
            sp.dma_start(lora_b_nat, lora_b.rearrange("e r o -> (e r) o")).then_inc(lora_loaded, 16)
            for t in range(2, 4):
                load_mix(t, t)
            for dst, src in ((g1b[:, :], gb1), (lng[:, :], ln_g), (lnb[:, :], ln_b),
                             (g2w, gw2.rearrange("e h -> (e h)")), (g2b[:, :], gb2)):
                sp.dma_start(dst, src.partition_broadcast(P)).then_inc(small_loaded, 16)
            sp.wait_ge(index_ready, INDEX_ALL)
            row_0 = field(sp, F_ADP, 0, NADP - 1) * D
            for p in range(2):
                load_gate(p, p)
            for o in range(2):
                load_w(w1_rows[ds(row_0 + o * P, P), :], NPREP0 + o, o)
            with sp.Fori(1, 4) as i:
                row_0 = field(sp, F_ADP, 0, NADP - 1) * D
                for c in range(4):
                    load_mix(4 * i + c, c)
                    if c % 2 == 1:
                        load_w(w1_rows[ds(row_0 + 2 * i * P + c // 2 * P, P), :], NPREP0 + 2 * i + c // 2 + 2, c // 2)
                    if c < 2:
                        load_gate(2 * i + c, c)
            for t in range(2):
                sp.wait_ge(y_done, NT)
                load_pair(x_nat[t], x_loaded[t], t)
            sp.wait_ge(w_transposed, NPREP0 + KC)
            def layer0(i, pieces):
                for s in range(2):
                    t = 2 * i + s
                    used = field(sp, F_USED, 0, NADP)
                    row_i = field(sp, F_ADP, i, NADP - 1) * D
                    with sp.If(used > i):
                        for q in range(4):
                            load_w(w1_rows[ds(row_i + (4 * s + q) * P, P), :], NPREP0 + 4 * t + q, q)
                    sp.wait_ge(acc_released, t - 1)
                    load_pair(x_nat[s], x_loaded[s], t)
                    if pieces:
                        load_gate(t, s)

            with sp.Fori(1, NT // 4) as i:
                layer0(i, False)
            with sp.Fori(NT // 4, NT // 2) as i:
                layer0(i, True)

            def load_rank(r):
                sp.dma_start(region_w[:, ((r + 1) % 2) * 32768:((r + 1) % 2 + 1) * 32768].bitcast(F16)
                             .rearrange("p (o n) -> p o n", o=KC),
                             w1t_dram[r].rearrange("o p n -> p o n")).then_inc(w1_loaded, 16)

            sp.wait_ge(tmpw_low, 2)
            for s in range(2):
                sp.wait_ge(w_stored[s], 16 * KC // 2)
            load_rank(0)
            sp.wait_ge(main_done, NT)
            used = field(sp, F_USED, 0, NADP)
            for r in range(1, NADP):
                before = field(sp, F_CUM, r - 2, NSLOT, least=1) if r >= 2 else None
                with sp.If(used > r):
                    for s in range(4):
                        sp.wait_ge(w_stored[s], stores(2 * r + 2, s))
                    sp.wait_ge(w1_loaded, 16 * r)
                    if r >= 2:
                        sp.wait_ge(z_done, before)
                    load_rank(r)
            sp.wait_ge(z_done, NSLOT)
            with sp.Fori(2, IC - 1) as ic:
                load_q(sp, ic, wq_nat, True)
            load_q(sp, IC - 1, wq_nat, True, last=True)

            def load_res(m, slot):
                sp.dma_start(res[slot], x1_dram[ds(m * P, P), :]).then_inc(res_loaded[slot], 16)

            def store_out(m, slot):
                b0 = field(sp, F_PERM, 2 * m, NB - 1)
                b1 = field(sp, F_PERM, 2 * m + 1, NB - 1)
                sp.wait_ge(res_done, m + 1)
                sp.dma_start(out_rows[ds(b0 * SEQ, SEQ), :], res[slot][0:SEQ, :]).then_inc(out_stored[slot], 16)
                sp.dma_start(out_rows[ds(b1 * SEQ, SEQ), :], res[slot][SEQ:P, :]).then_inc(out_stored[slot], 16)

            sp.wait_ge(q_ready, 3 * IC)
            for s in range(2):
                sp.wait_ge(x1_stored[s], 16 * NT // 2)
            for s in range(TPG):
                load_res(s, s)
            for s in range(TPG):
                store_out(s, s)
            with sp.Fori(1, NG) as g:
                for s in range(TPG):
                    sp.wait_ge(out_stored[s], 32 * g)
                    load_res(TPG * g + s, s)
                for s in range(TPG):
                    store_out(TPG * g + s, s)
            for s in range(TPG):
                sp.wait_ge(out_stored[s], 32 * NG)

        @block.gpsimd
        def _(pool):
            pool.iota(iota_i[:, :], pattern=[[1, NB]], base=0, channel_multiplier=0).then_inc(consts_ready, 1)
            pool.iota(part_i[:, :], pattern=[[0, 1]], base=0, channel_multiplier=1).then_inc(consts_ready, 1)
            pool.memset(ones[:, :], 1.0).then_inc(consts_ready, 1)
            pool.memset(ident[:, :], 0.0).then_inc(consts_ready, 1)
            pool.memset(ident16[:, :], 0.0).then_inc(consts_ready, 1)
            pool.wait_ge(consts_ready, 5)
            for m in (ident, ident16):
                pool.affine_select(out=m[:, :], in_=m[:, :], compare_op=ALU.not_equal, fill=1.0, base=0,
                                   pattern=[[-1, P]], channel_multiplier=1).then_inc(consts_ready, 1)
            pool.memset(cond_bd, 0.0).then_inc(consts_ready, 1)

            def load_cond(t, slot):
                c0 = field(pool, F_COND, 2 * t, 15)
                c1 = field(pool, F_COND, 2 * t + 1, 15)
                wait_if(pool, cond_loaded[slot], 8 * (t - slot))
                pool.dma_start(at(cond_bd[0:SEQ], t)[:, 0:SEQ], cond_rows[ds(c0 * SEQ, SEQ), :])\
                    .then_inc(cond_loaded[slot], 16)
                pool.dma_start(at(cond_bd[SEQ:P], t)[:, SEQ:P], cond_rows[ds(c1 * SEQ, SEQ), :])\
                    .then_inc(cond_loaded[slot], 16)

            pool.wait_ge(index_ready, 1)
            pool.wait_ge(consts_ready, 8)
            for t in range(4):
                load_cond(t, t)
            with pool.Fori(1, 4) as i:
                for c in range(4):
                    load_cond(4 * i + c, c)
            pool.memset(act_t[:, :, :, NTOK:ACT_COLS], 0.0).then_inc(consts_ready, 1)

            def widen_up(g, ic, s):
                if g == 0:
                    pool.wait_ge(q_stored, 3 * ic + 2)
                pool.tensor_copy(chunked(wide[2 * widen_half(g, s) + 1]), q_up[:, :, ds(ic * P, P)])\
                    .then_inc(up_wide, 1)

            def low_inter(g, ic, s, last=False):
                part = slice(0, LAST) if last else slice(0, P)
                pool.wait_ge(inter_high, g * IC + ic + 1)
                pool.tensor_tensor(at(inter[:, 1], ic)[part], gate_s[s][part], at(inter[:, 0], ic)[part], ALU.subtract)\
                    .then_inc(inter_low, 1)

            for g in range(NG):
                wait_if(pool, down_step, g * (IC - 2))
                widen_up(g, 0, 0)
                wait_if(pool, down_done, TPG * g)
                widen_up(g, 1, 1)
                if g == 0:
                    pool.wait_ge(z_done, NSLOT)
                    pool.wait_ge(up_wide, 2)
                    pool.memset(inter[LAST:P, :, IC - 1, :], 0.0).then_inc(tail_zeroed, 1)
                    pool.wait_ge(tail_zeroed, 1)
                with pool.Fori(0, IC // 2 - 1) as i:
                    for s in range(2):
                        pool.wait_ge(gu_done, g * IC + 2 * i + s + 1)
                        widen_up(g, 2 * i + s + 2, s)
                        low_inter(g, 2 * i + s, s)
                low_inter(g, IC - 2, 0)
                low_inter(g, IC - 1, 1, last=True)

        @block.tensor
        def _(pe):
            def transpose8(dst, src, idn):
                for k in range(KC):
                    mm = pe.transpose(dst[:, k * P:(k + 1) * P], src[:, k * P:(k + 1) * P], idn[:, :])
                return mm

            def prep(r, slot, loads, p, free):
                pe.wait_ge(w_loaded[slot], loads)
                wait_if(pe, w_low, free)
                transpose8(pair[p], w_nat[slot], ident).then_inc(w_transposed, 1)

            def ix_sum(dst, lhs, rhs):
                return pe.matmul(dst, lhs, rhs, start=True, stop=True)

            def prep_w0(r):
                if r == 2:
                    pe.wait_ge(index_ready, INDEX_ALL)
                if r == 3:
                    pe.wait_ge(ag_low, 1)
                prep(r, r % 4, 16 * (r // 4 + 1), W0_PAIR[r % 4], r - 3)

            pe.wait_ge(consts_ready, 3)
            pe.wait_ge(index_sorted, 1)
            ix_sum(ix_ps[0:1, 0:NB], ix_part, ix_onehot)
            ix_sum(ix_ps[0:1, NB:2 * NB], ix_cnd, ix_onehot)
            ix_sum(ix_ps[0:NB, 64:96], ix_adp_b, ix_onehot)
            ix_sum(ix_ps[0:NB, 96:97], ix_onehot, ix_adp).then_inc(index_sum, 1)
            pe.wait_ge(consts_ready, 7)
            prep_w0(0)
            pe.wait_ge(index_sorted, 2)
            ix_sum(ix_ps[0:NB, 97:98], ix_lt, ix_start)
            ix_sum(ix_ps[0:NB, 98:99], ix_le, ix_new)
            ix_sum(ix_ps[0:NB, 99:100], ix_shift, ix_adps1)
            ix_sum(ix_ps[0:NB, 100:101], ones[0:NB, 0:NB], ix_new).then_inc(index_sum, 1)
            prep_w0(1)
            pe.wait_ge(index_sorted, 3)
            for f, v_ in ((F_READ, ix_v[0]), (F_WRITE, ix_v[1]), (F_SECOND, ix_v[2]), (F_RANK, ix_v[3])):
                ix_sum(ix_ps[0:1, 128 + f:128 + f + NSLOT], v_, ix_pair)
            ix_sum(ix_ps[0:1, 128 + F_ADP:128 + F_ADP + NADP], ix_adps, ix_run)
            ix_sum(ix_ps[0:1, 128 + F_CUM:128 + F_CUM + NADP], ones[0:NB, 0:1], ix_upto).then_inc(index_sum, 1)

            pe.wait_ge(gw1_loaded, 16)
            for k in range(KC):
                mm = pe.transpose(pair[2][:, k * GH:(k + 1) * GH], gw1_nat[0:GH, k * P:(k + 1) * P],
                                  ident[0:GH, 0:GH])
            mm.then_inc(gw1_transposed, 1)
            for r in range(2, NPREP0):
                prep_w0(r)

            def mix(t, slot, s, loads):
                pe.wait_ge(mix_loaded[slot], loads)
                pe.wait_ge(cond_loaded[slot], loads)
                wait_if(pe, y_low, t - 1)
                for k in range(KC):
                    mm = pe.matmul(pair[s][:, k * P:(k + 1) * P], mix_nat[slot][:, k * P:(k + 1) * P],
                                   at(cond_bd, t), start=True, stop=True)
                mm.then_inc(y_done, 1)

            def gate(t, s):
                pe.wait_ge(y_low, t + 1)
                wait_if(pe, tmp_copied, t - 1)
                dst = pair[2][:, s * H:s * H + ER + GH]
                n = 0
                for k in range(KC):
                    for a, b in ((0, 0), (0, 1), (1, 0)):
                        mm = pe.matmul(dst, act_t[:, a, k, ds(t * P, P)], ag[:, b, k, :],
                                       start=(n == 0), stop=(n == 3 * KC - 1))
                        n += 1
                mm.then_inc(tmp_done, 1)

            pe.wait_ge(w_low, NPREP0 - 1)
            mix(0, 0, 0, 32)
            pe.wait_ge(ag_low, 3)
            for t in range(1, 4):
                mix(t, t, t % 2, 32)
                gate(t - 1, (t - 1) % 2)
                if t % 2 == 1:
                    prep(NPREP0 + t // 2, t // 2, 16 * 3, 3, NPREP0 + t // 2)
            with loop(pe, 1, 4) as i:
                for c in range(4):
                    mix(4 * i + c, c, c % 2, 32 * i + 32)
                    gate(4 * i + c - 1, (c - 1) % 2)
                    if c % 2 == 1:
                        o = 2 * i + c // 2
                        prep(NPREP0 + o, c // 2, 16 * i + 48, 3, NPREP0 + o)
            gate(NT - 1, 1)

            def main(t, s, q):
                if q == 0:
                    wait_if(pe, acc_released, t - 1)
                for k in (2 * q, 2 * q + 1):
                    for a, b in ((0, 0), (0, 1), (1, 0)):
                        for h in range(2):
                            pe.matmul(pair[s][:, h * H:(h + 1) * H], act_t[:, a, k, ds(t * P, P)],
                                      w0_t[:, 4 * h:4 * h + 4, b, k, :],
                                      start=(k == 0 and a + b == 0), stop=False)

            def lora(t, s):
                for a, b in ((0, 0), (0, 1), (1, 0)):
                    for h in range(2):
                        mm = pe.matmul(pair[s][:, h * H:(h + 1) * H], tmpw_t[:, a, ds(t * P, P)],
                                       lb[:, b, h * H:(h + 1) * H], start=False, stop=(a == 1))
                mm.then_inc(main_done, 1)

            def turn_x1(t, s):
                pe.wait_ge(acc_released, t + 1)
                wait_if(pe, x1_low, t)
                transpose8(pair[2], x1_nat[s], ident).then_inc(x1_transposed, 1)

            pe.wait_ge(y_low, NT)
            for t in range(2):
                for q in range(4):
                    main(t, t, q)
            pe.wait_ge(count_ready, 1)
            pe.matmul(pair[3][:, 0:2 * E], ones[:, :], cnt[:, :, :].rearrange("p a b -> p (a b)"),
                      start=True, stop=True).then_inc(counted, 1)
            pe.wait_ge(tmpw_ready, 1)
            pe.wait_ge(tmp_copied, NT)
            for t in range(NT):
                mm = pe.transpose(pair[2 + t // 8][:, (t % 8) * P:(t % 8 + 1) * P],
                                  tmpw[:, t, :, :].rearrange("p a b -> p (a b)"), ident[:, :])
                if t % 8 == 7:
                    mm.then_inc(tmpw_transposed, 1)
            pe.wait_ge(tmpw_low, 2)
            lora(0, 0)
            lora(1, 1)
            turn_x1(0, 0)

            def layer0(i):
                used = field(pe, F_USED, 0, NADP)
                for s in range(2):
                    t = 2 * i + s
                    main(t, s, 0)
                    turn_x1(t - 1, 1 - s)
                    with pe.If(used > i):
                        for q in range(4):
                            prep(NPREP0 + 4 * t + q, q, loads(t, q), 3, NPREP0 + 4 * t + q)
                            if q < 3:
                                main(t, s, q + 1)
                    with pe.If(used <= i):
                        for q in range(1, 4):
                            main(t, s, q)
                    lora(t, s)

            with loop(pe, 1, NT // 2) as i:
                layer0(i)

            def linear(k, s):
                rank = field(pe, F_RANK, k, NADP - 1)
                at = field(pe, F_READ, k, NB * SEQ)
                if isinstance(k, int) and k == 0:
                    pe.wait_ge(x1_low, 2)
                    pe.wait_ge(acc_released, NT)
                pe.wait_ge(w1_loaded, rank * 16 + 16)
                wait_if(pe, z_copied_a, k - 1)
                wait_if(pe, z_copied_v, k - 1)
                buf = (rank + 1) % 2
                n = 0
                for c in range(KC):
                    for a, b in ((0, 0), (0, 1), (1, 0)):
                        for h in range(2):
                            mm = pe.matmul(pair[s][:, h * H:(h + 1) * H], act_t[:, a, c, ds(at, P)],
                                           w1_t[:, ds(buf, 1), 4 * h:4 * h + 4, b, c, :].rearrange("p x o c -> p (x o) c"),
                                           start=(n == 0), stop=(n == 3 * KC - 1))
                        n += 1
                mm.then_inc(z_done, 1)

            def linear_t(k, s):
                pe.wait_ge(z_copied_a, k + 1)
                pe.wait_ge(z_copied_v, k + 1)
                if isinstance(k, int) and k == 0:
                    pe.wait_ge(x1_low, NT)
                else:
                    pe.wait_ge(z_low, k)
                transpose8(pair[2], z_nat[s], ident).then_inc(z_transposed, 1)

            pe.wait_ge(consts_ready, 9)

            def layer1(i):
                linear(2 * i + 1, 1)
                linear_t(2 * i, 0)
                linear(2 * i + 2, 0)
                linear_t(2 * i + 1, 1)

            linear(0, 0)
            turn_x1(NT - 1, 1)
            linear(1, 1)
            linear_t(0, 0)
            pe.wait_ge(x1_low, NT)
            linear(2, 0)
            linear_t(1, 1)
            with loop(pe, 1, NSLOT // 2 - 4) as i:
                layer1(i)

            def turn_q(ic, kinds=(0, 1, 2)):
                for kind in kinds:
                    pe.wait_ge(q_ready, 3 * ic + kind + 1)
                    if isinstance(ic, int) and ic < 2 and kind == 2:
                        pe.wait_ge(q_stored, 3 * ic + 1)
                    elif isinstance(ic, int) and 0 < ic <= 2 and kind == 0:
                        pe.wait_ge(q_stored, 3 * ic)
                    elif not isinstance(ic, int) or ic > 0:
                        pe.wait_ge(q_stored, 3 * ic - 2 + kind)
                    transpose8(q_bank(ic, kind), q16[kind], ident16).then_inc(q_transposed, 1)

            def linear_opt(k, s):
                pairs = field(pe, F_CUM, NADP - 1, NSLOT)
                with pe.If(pairs > k):
                    linear(k, s)
                with pe.If(pairs <= k):
                    pe.wait_ge(z_copied_a, k - 1)
                    pe.wait_ge(z_copied_v, k - 1)
                    pe.transpose(pair[s][:, 0:P], ident[:, :], ident[:, :]).then_inc(z_done, 1)

            def linear_t_opt(k, s):
                pairs = field(pe, F_CUM, NADP - 1, NSLOT)
                with pe.If(pairs > k):
                    linear_t(k, s)
                with pe.If(pairs <= k):
                    pe.wait_ge(z_copied_a, k + 1)
                    pe.wait_ge(z_copied_v, k + 1)
                    pe.wait_ge(z_low, k)
                    pe.transpose(pair[2][:, 0:P], ident[:, :], ident[:, :]).then_inc(z_transposed, 1)

            k = FIRST_OPTIONAL
            linear(k - 4, 1)
            pe.wait_ge(stat_summed, 2)
            pe.matmul(pair[3][:, 0:3], ones[:, :], ssum[:, 0:3], start=True, stop=True).then_inc(mean_done, 1)
            linear_t(k - 5, 0)
            linear(k - 3, 0)
            turn_q(0, (0, 1))
            linear_t(k - 4, 1)
            turn_q(0, (2,))
            linear(k - 2, 1)
            linear_t(k - 3, 0)
            linear(k - 1, 0)
            turn_q(1, (0, 1))
            linear_t(k - 2, 1)
            turn_q(1, (2,))
            linear_opt(k, 1)
            linear_t(k - 1, 0)
            linear_opt(k + 1, 0)
            linear_t_opt(k, 1)
            linear_opt(k + 2, 1)
            linear_t_opt(k + 1, 0)
            linear_t_opt(k + 2, 1)

            def gate_up(g, ic, s, last=False):
                n = g * IC + ic
                pe.wait_ge(gate_wide, n + 1)
                pe.wait_ge(up_wide, n + 1)
                wait_if(pe, prod_done, n - 1)
                half = widen_half(g, s)
                both = ((wide[2 * half], pair[0]), (wide[2 * half + 1], pair[1]))
                for w, dst in both[:1] if last else both:
                    for k in range(KC):
                        for a in range(2):
                            mm = pe.matmul(dst[:, s * H:(s + 1) * H], w[:, k * P:(k + 1) * P],
                                           act_t[:, a, k, g * GRP:(g + 1) * GRP],
                                           start=(k == 0 and a == 0), stop=(k == KC - 1 and a == 1))
                mm.then_inc(gu_done, 1)

            def down(ic, tt, slot):
                for a in range(2):
                    for h in range(2):
                        mm = pe.matmul(pair[tt][:, h * H:(h + 1) * H], at(inter[:, a], ic)[:, tt * P:(tt + 1) * P],
                                       wide[slot][:, h * H:(h + 1) * H],
                                       start=(isinstance(ic, int) and ic == 0 and a == 0),
                                       stop=(isinstance(ic, int) and ic == IC - 1 and a == 1))
                return mm

            def down_chunk(g, ic, c):
                pe.wait_ge(down_wide[c % 2], IC // 2 * g + (ic - c % 2) // 2 + 1)
                for tt in (2, 3, 0, 1):
                    if g > 0 and isinstance(ic, int) and ic == 0 and tt == 2:
                        pe.wait_ge(res_done, TPG * g)
                    if isinstance(ic, int) and ic == 0 and tt == 0:
                        pe.wait_ge(prod_done, IC * (g + 1))
                    mm = down(ic, tt, down_slot(g, c))
                mm.then_inc(down_step, 1)

            for g in range(NG):
                if g == 0:
                    gate_up(0, 0, 0)
                    pe.wait_ge(z_low, NSLOT)
                    turn_q(2)
                    gate_up(0, 1, 1)
                    with loop(pe, 1, IC // 2 - 1) as i:
                        for s in range(2):
                            turn_q(2 * i + s + 1)
                            gate_up(0, 2 * i + s, s)
                    turn_q(IC - 1)
                    gate_up(0, IC - 2, 0)
                    gate_up(0, IC - 1, 1, last=True)
                    pe.wait_ge(q_stored, 3 * IC)
                else:
                    pe.wait_ge(res_done, TPG * (g - 1) + 2)
                    with loop(pe, 0, IC // 2 - 1) as i:
                        for s in range(2):
                            gate_up(g, 2 * i + s, s)
                    gate_up(g, IC - 2, 0)
                    gate_up(g, IC - 1, 1, last=True)
                pe.wait_ge(inter_low, IC * (g + 1) - 2)
                for c in range(4):
                    down_chunk(g, c, c)
                with loop(pe, 1, (IC - 2) // 4) as i:
                    for c in range(4):
                        down_chunk(g, 4 * i + c, c)
                for c in range(2):
                    pe.wait_ge(down_wide[c], IC // 2 * (g + 1))
                pe.wait_ge(inter_low, IC * (g + 1))
                pe.wait_ge(tail_zeroed, 1)
                for tt in range(TPG):
                    for c in range(2):
                        mm = down(IC - 2 + c, tt, down_slot(g, c))
                    mm.then_inc(down_done, 1)

        @block.scalar
        def _(act):
            def high(dst, src, scale):
                return act.activation(dst, src, ACT.Copy, scale=scale)

            ps8 = [p[:, :].rearrange("p (k c) -> p k c", k=KC) for p in pair]

            def high_w0(r):
                act.wait_ge(w_transposed, r + 1)
                high(w0_t[:, r, 0], ps8[W0_PAIR[r % 4]], WGT_SCALE).then_inc(w_high, 1)

            high_w0(0)
            high_w0(1)
            act.wait_ge(gw1_transposed, 1)
            high(ag[:, 0, :, ER:ER + GH], pair[2][:, 0:KC * GH].rearrange("p (k c) -> p k c", k=KC),
                 WGT_SCALE).then_inc(ag_high, 1)
            for r in range(2, NPREP0):
                high_w0(r)
            act.wait_ge(lora_loaded, 16 * (KC + 1))
            high(ag[:, 0, :, 0:ER], lora_a_nat.rearrange("p k e r -> p k (e r)"), WGT_SCALE).then_inc(ag_high, 1)
            high(lb[:, 0, :], lora_b_nat, WGT_SCALE).then_inc(ag_high, 1)

            def y_part(t, s):
                act.wait_ge(y_done, t + 1)
                high(act_t[:, 0, :, ds(t * P, P)], ps8[s], ACT_SCALE).then_inc(y_high, 1)

            def tmp_part(t, s):
                act.wait_ge(tmp_done, t + 1)
                high(at(tmp, t),
                     pair[2][:, s * H:s * H + ER + GH], 1.0 / PROD).then_inc(tmp_copied, 1)

            def w_part(r1, slot, before):
                act.wait_ge(w_transposed, NPREP0 + r1 + 1)
                wait_if(act, w_stored[slot], before)
                high(w_split[slot][:, 0], ps8[3], WGT_SCALE).then_inc(w_high, 1)

            def store_w(r1, slot):
                act.wait_ge(w_low, NPREP0 + r1 + 1)
                act.dma_start(w1t_rows[ds(r1, 1)].rearrange("a p n -> (a p) n"),
                              w_split[slot].rearrange("p s k c -> p (s k c)")).then_inc(w_stored[slot], 16)

            y_part(0, 0)
            for t in range(1, 4):
                y_part(t, t % 2)
                tmp_part(t - 1, (t - 1) % 2)
                if t % 2 == 1:
                    w_part(t // 2, t // 2, 0)
                else:
                    store_w(t // 2 - 1, t // 2 - 1)
            with act.Fori(1, 4) as i:
                for c in range(4):
                    y_part(4 * i + c, c % 2)
                    tmp_part(4 * i + c - 1, (c - 1) % 2)
                    o = 2 * i + c // 2
                    if c % 2 == 1:
                        w_part(o, c // 2, 16 * i)
                    else:
                        store_w(o - 1, (c // 2 - 1) % 2)
            tmp_part(NT - 1, 1)
            store_w(KC - 1, 1)

            act.wait_ge(var_ready, 1)
            act.activation(row[:, 2, :], row[:, 1, :], ACT.Sqrt).then_inc(gate_std, 1)
            act.wait_ge(gap_ready, 1)
            act.activation(row[:, 5, :], row[:, 4, :], ACT.Exp).then_inc(gate_exp, 1)
            for i in range(2):
                act.wait_ge(tmpw_transposed, i + 1)
                high(tmpw_t[:, 0, i * D:(i + 1) * D], pair[2 + i][:, :], 1.0).then_inc(tmpw_high, 1)

            def x1_part(t, s):
                act.wait_ge(x1_transposed, t + 1)
                high(act_t[:, 0, :, ds(t * P, P)], ps8[2], ACT_SCALE).then_inc(x1_high, 1)
                act.dma_start(x1_dram[ds(t * P, P), :], x1_nat[s]).then_inc(x1_stored[s], 16)

            def layer0(i):
                for s in range(2):
                    t = 2 * i + s
                    x1_part(t - 1, 1 - s)
                    used = field(act, F_USED, 0, NADP)
                    with act.If(used > i):
                        for q in range(4):
                            w_part(4 * t + q, q, stores(t, q))
                            if q > 0:
                                store_w(4 * t + q - 1, q - 1)
                        store_w(4 * t + 3, 3)

            x1_part(0, 0)
            layer0(1)
            with act.Fori(2, NT // 2) as i:
                layer0(i)
            x1_part(NT - 1, 1)

            flat = [w.rearrange("a b -> (a b)").rearrange("(p n) -> p n", p=P) for w in (w_up, w_down)]

            def load_piece(p, s, last=False):
                wait_if(act, stat_done, p - 1)
                n = PIECE if not last else INNER * D // P - (NPIECE - 1) * PIECE
                for w in range(2):
                    act.dma_start(stat_in[s][:, w, 0:n], flat[w][:, ds(p * PIECE, n)])\
                       .then_inc(stat_loaded[s], 16)

            def copy_z(k, s):
                act.wait_ge(z_done, k + 1)
                high(z_nat[s][:, 0:H], pair[s][:, 0:H], 1.0 / PROD).then_inc(z_copied_a, 1)

            def high_z(k):
                d0 = field(act, F_WRITE, k, WRITE_DUMMY * SEQ)
                d1 = field(act, F_SECOND, k, SECOND_DUMMY * SEQ)
                act.wait_ge(z_transposed, k + 1)
                high(act_t[:, 0, :, ds(d0, SEQ)], ps8[2][:, :, 0:SEQ], ACT_SCALE)
                high(act_t[:, 0, :, ds(d1, SEQ)], ps8[2][:, :, SEQ:P], ACT_SCALE).then_inc(z_high, 1)

            for s in range(2):
                act.wait_ge(w_stored[s], stores(2, s))
            used = field(act, F_USED, 0, NADP)
            for r in range(1, NADP):
                with act.If(used > r):
                    for s in range(4):
                        act.wait_ge(w_stored[s], stores(2 * r + 2, s))
            load_piece(0, 0)
            load_piece(1, 1)
            copy_z(0, 0)

            def layer1(i, more, last=False):
                copy_z(2 * i + 1, 1)
                high_z(2 * i)
                if more:
                    load_piece(2 * i + 2, 0)
                copy_z(2 * i + 2, 0)
                high_z(2 * i + 1)
                if more:
                    load_piece(2 * i + 3, 1, last)

            with act.Fori(0, NPIECE // 2 - 2) as i:
                layer1(i, True)
            layer1(NPIECE // 2 - 2, True, last=True)
            load_q(act, 0, wq_early, False)
            layer1(NPIECE // 2 - 1, False)

            def store_q(ic, kinds=(0, 1, 2)):
                for kind in kinds:
                    act.wait_ge(q_transposed, 3 * ic + kind + 1)
                    src = q_bank(ic, kind)
                    if kind < 2:
                        dst = (q_gate, q_up)[kind][:, :, ds(ic * P, P)]
                        src = src.rearrange("p (k c) -> p k c", k=KC)
                    else:
                        dst = at(q_down, ic)
                    act.activation(dst, src, ACT.Copy).then_inc(q_stored, 1)

            def inter_part(g, ic, s, last=False):
                lower = slice(0, LAST) if last else slice(0, P)
                upper = slice(LAST, 2 * LAST) if last else slice(0, P)
                n = g * IC + ic
                act.wait_ge(gu_done, n + 1)
                wait_if(act, inter_low, n - 1)
                act.activation(gate_s[s][upper], pair[0][lower, s * H:(s + 1) * H], ACT.Copy,
                               scale=inter_c[lower, 0:1])\
                   .then_inc(gate_scaled, 1)
                act.wait_ge(prod_done, n + 1)
                high(at(inter[:, 0], ic)[lower], gate_s[s][lower], 1.0).then_inc(inter_high, 1)

            def widen_gate(g, ic, s):
                if g == 0:
                    act.wait_ge(q_stored, 3 * ic + 1)
                act.activation(chunked(wide[2 * widen_half(g, s)]), q_gate[:, :, ds((ic - 1) * P + P, P)], ACT.Copy)\
                   .then_inc(gate_wide, 1)

            def widen_down(g, ic, c):
                act.activation(wide[down_slot(g, c)], at(q_down, ic), ACT.Copy).then_inc(down_wide[0], 1)

            def copy_z_opt(k, s):
                pairs = field(act, F_CUM, NADP - 1, NSLOT)
                with act.If(pairs > k):
                    copy_z(k, s)
                with act.If(pairs <= k):
                    act.wait_ge(z_done, k + 1)
                    high(z_nat[s][0:1, 0:1], pair[s][0:1, 0:1], 1.0).then_inc(z_copied_a, 1)

            def high_z_opt(k):
                pairs = field(act, F_CUM, NADP - 1, NSLOT)
                with act.If(pairs > k):
                    high_z(k)
                with act.If(pairs <= k):
                    act.wait_ge(z_transposed, k + 1)
                    high(act_t[0:1, 0, 0, WRITE_DUMMY * SEQ:WRITE_DUMMY * SEQ + 1], pair[2][0:1, 0:1], 1.0)\
                        .then_inc(z_high, 1)

            k = FIRST_OPTIONAL
            copy_z(k - 4, 1)
            high_z(k - 5)
            copy_z(k - 3, 0)
            for s in range(2):
                act.wait_ge(x1_stored[s], 16 * NT // 2)
            act.wait_ge(scales_ready, 1)
            store_q(0, (0, 1))
            high_z(k - 4)
            store_q(0, (2,))
            load_q(act, 1, wq_early, True)
            widen_gate(0, 0, 0)
            copy_z(k - 2, 1)
            high_z(k - 3)
            copy_z(k - 1, 0)
            store_q(1, (0, 1))
            high_z(k - 2)
            store_q(1, (2,))
            copy_z_opt(k, 1)
            high_z(k - 1)
            widen_gate(0, 1, 1)
            copy_z_opt(k + 1, 0)
            high_z_opt(k)
            copy_z_opt(k + 2, 1)
            high_z_opt(k + 1)
            high_z_opt(k + 2)
            for g in range(NG):
                if g > 0:
                    act.wait_ge(down_step, g * (IC - 2))
                    widen_gate(g, 0, 0)
                    act.wait_ge(down_done, TPG * g)
                    widen_gate(g, 1, 1)
                inter_part(g, 0, 0)
                with act.Fori(0, IC // 2 - 1) as i:
                    for s in range(2):
                        ic = 2 * i + 1 + s
                        if g == 0:
                            store_q(ic + 1)
                        if g > 0:
                            act.wait_ge(gu_done, g * IC + ic)
                        widen_gate(g, ic + 1, s)
                        inter_part(g, ic, 1 - s)
                if g == 0:
                    act.wait_ge(q_stored, 3 * IC)
                widen_down(g, 0, 0)
                inter_part(g, IC - 1, 1, last=True)
                widen_down(g, 2, 2)
                with act.Fori(0, (IC - 6) // 4) as i:
                    for c in (0, 2):
                        act.wait_ge(down_step, g * (IC - 2) + 4 * i + c + 1)
                        widen_down(g, 4 * i + c + 4, c)
                act.wait_ge(down_step, g * (IC - 2) + IC - 5)
                widen_down(g, IC - 2, 0)

        @block.vector
        def _(v):
            ps8 = [p[:, :].rearrange("p (k c) -> p k c", k=KC) for p in pair]

            def low(dst, src, scale, hi):
                return v.scalar_tensor_tensor(out=dst, in0=src, scalar=scale, in1=hi,
                                              op0=ALU.mult, op1=ALU.subtract)

            step = [0]

            def then(instruction):
                step[0] += 1
                instruction.then_inc(index_step, 1)
                v.wait_ge(index_step, step[0])

            def compare(dst, row, column, op, scale=None):
                if scale is None:
                    return v.tensor_scalar(dst, row, column, None, op)
                return v.tensor_scalar(dst, row, column, scale, op, ALU.mult)

            nums = iota[0:NB, :]
            v.wait_ge(consts_ready, 2)
            then(v.tensor_copy(iota[:, :], iota_i[:, :]))
            then(v.tensor_copy(ix_part, part_i[0:NB, :]))
            v.wait_ge(ids_loaded, 48)
            then(v.tensor_copy(ix_adp, ids_col_i[:, 0:1]))
            then(v.tensor_copy(ix_cnd, ids_col_i[:, 1:2]))
            then(v.tensor_copy(ix_adp_r, ids_row_i))
            then(v.scalar_tensor_tensor(out=ix_key_r, in0=ix_adp_r, scalar=float(NB), in1=nums,
                                        op0=ALU.mult, op1=ALU.add))
            then(v.scalar_tensor_tensor(out=ix_key, in0=ix_adp, scalar=float(NB), in1=ix_part,
                                        op0=ALU.mult, op1=ALU.add))
            then(v.tensor_copy(ix_adp_b, ix_adp.broadcast_to([NB, NB])))
            then(compare(ix_tmp, ix_key_r, ix_key, ALU.is_lt))
            then(v.tensor_reduce(ix_rank, ix_tmp, X, ALU.add))
            compare(ix_onehot, nums, ix_rank, ALU.is_equal).then_inc(index_sorted, 1)
            v.tensor_scalar(ix_lt, nums, ix_part, None, ALU.is_gt).then_inc(index_step, 1)
            v.tensor_scalar(ix_le, nums, ix_part, None, ALU.is_ge).then_inc(index_step, 1)
            v.tensor_scalar(ix_shift, nums, 1.0, ix_part, ALU.add, ALU.is_equal).then_inc(index_step, 1)
            step[0] += 3
            v.wait_ge(index_sum, 1)
            v.tensor_copy(ixi[:, 0:F_READ], ix_ps[0:1, 0:2 * NB]).then_inc(index_ready, 1)
            then(v.tensor_copy(ix_adps, ix_ps[0:NB, 96:97]))
            then(v.tensor_scalar(ix_adps1, ix_adps, 1.0, None, ALU.add))
            then(compare(ix_tmp, ix_ps[0:NB, 64:96], ix_adps, ALU.is_lt))
            then(v.tensor_reduce(ix_first, ix_tmp, X, ALU.add))
            then(v.tensor_tensor(ix_since, ix_part, ix_first, ALU.subtract))
            then(v.tensor_copy(odd_i, ix_since))
            then(v.tensor_scalar(odd_i, odd_i, 1, None, ALU.bitwise_and))
            then(v.tensor_copy(ix_start, odd_i))
            then(v.tensor_scalar(ix_start, ix_start, -1.0, 1.0, ALU.mult, ALU.add))
            v.tensor_scalar(ix_new, ix_since, 0.0, None, ALU.is_equal).then_inc(index_sorted, 1)
            v.wait_ge(index_sum, 2)
            then(v.tensor_copy(ix_before, ix_ps[0:NB, 97:98]))
            then(v.tensor_scalar(ix_gm, ix_ps[0:NB, 98:99], -1.0, None, ALU.add))
            then(v.tensor_tensor(ix_nxt, ix_ps[0:NB, 99:100], ix_adps1, ALU.is_equal))
            then(v.tensor_copy(ix_used, ix_ps[0:NB, 100:101]))
            then(v.tensor_scalar(ix_last, ix_used, -1.0, None, ALU.add))
            then(v.tensor_scalar(ix_v[0], ix_part, float(SEQ), float(-READ_DUMMY * SEQ), ALU.mult, ALU.add))
            then(v.tensor_scalar(ix_v[1], ix_part, float(SEQ), float(-WRITE_DUMMY * SEQ), ALU.mult, ALU.add))
            then(v.tensor_scalar(ix_v[2], ix_part, float(SEQ), float((1 - SECOND_DUMMY) * SEQ), ALU.mult, ALU.add))
            then(v.tensor_tensor(ix_v[2], ix_v[2], ix_nxt, ALU.mult))
            then(v.tensor_tensor(ix_v[3], ix_gm, ix_last, ALU.subtract))
            then(compare(ix_pair, nums[:, 0:NSLOT], ix_before, ALU.is_equal, ix_start))
            then(compare(ix_run, nums[:, 0:NADP], ix_gm, ALU.is_equal, ix_new))
            compare(ix_upto, nums[:, 0:NADP], ix_gm, ALU.is_ge, ix_start).then_inc(index_sorted, 1)
            v.wait_ge(index_sum, 3)
            for f, dummy in ((F_READ, float(READ_DUMMY * SEQ)), (F_WRITE, float(WRITE_DUMMY * SEQ)),
                             (F_SECOND, float(SECOND_DUMMY * SEQ)), (F_RANK, ix_last[0:1])):
                v.tensor_scalar(ixi[:, f:f + NSLOT], ix_ps[0:1, 128 + f:128 + f + NSLOT], dummy, None, ALU.add)\
                 .then_inc(index_ready, 1)
            v.tensor_copy(ixi[:, F_ADP:F_USED], ix_ps[0:1, 128 + F_ADP:128 + F_USED]).then_inc(index_ready, 1)
            v.tensor_copy(ixi[:, F_USED:NFIELD], ix_used[0:1]).then_inc(index_ready, 1)

            def low_w0(r):
                v.wait_ge(w_high, r + 1)
                low(w0_t[:, r, 1], ps8[W0_PAIR[r % 4]], WGT_SCALE, w0_t[:, r, 0]).then_inc(w_low, 1)

            low_w0(0)
            low_w0(1)
            v.wait_ge(ag_high, 1)
            low(ag[:, 1, :, ER:ER + GH], pair[2][:, 0:KC * GH].rearrange("p (k c) -> p k c", k=KC),
                WGT_SCALE, ag[:, 0, :, ER:ER + GH]).then_inc(ag_low, 1)
            for r in range(2, NPREP0):
                low_w0(r)
            v.wait_ge(ag_high, 3)
            low(lb[:, 1, :], lora_b_nat, WGT_SCALE, lb[:, 0, :]).then_inc(ag_low, 1)
            low(ag[:, 1, :, 0:ER], lora_a_nat.rearrange("p k e r -> p k (e r)"), WGT_SCALE,
                ag[:, 0, :, 0:ER]).then_inc(ag_low, 1)

            def low_y(t, s):
                v.wait_ge(y_high, t + 1)
                low(act_t[:, 1, :, ds(t * P, P)], ps8[s], ACT_SCALE, act_t[:, 0, :, ds(t * P, P)])\
                    .then_inc(y_low, 1)

            def low_w(r1, slot):
                v.wait_ge(w_high, NPREP0 + r1 + 1)
                low(w_split[slot][:, 1], ps8[3], WGT_SCALE, w_split[slot][:, 0]).then_inc(w_low, 1)

            def sum_gate(p, s, loads):
                v.wait_ge(gate_loaded[s], loads)
                v.tensor_reduce(stat_g[:, ds(p, 1)], stat_gate[s], X, ALU.add,
                                apply_absolute_value=True).then_inc(gate_summed, 1)

            for t in range(4):
                low_y(t, t % 2)
                if t < 2:
                    sum_gate(t, t, 16)
                if t % 2 == 1:
                    low_w(t // 2, t // 2)
            with v.Fori(1, 4) as i:
                for c in range(4):
                    low_y(4 * i + c, c % 2)
                    if c < 2:
                        sum_gate(2 * i + c, c, 16 * i + 16)
                    if c % 2 == 1:
                        low_w(2 * i + c // 2, c // 2)

            count = [0]

            def gthen(instruction):
                count[0] += 1
                instruction.then_inc(gate_step, 1)
                v.wait_ge(gate_step, count[0])

            def per_channel(a, n=NT):
                return a.unsqueeze(1).broadcast_to([P, n, a.shape[1]])

            def per_token(a, n):
                return a.unsqueeze(2).broadcast_to([P, NT, n])

            total, var, std, rstd, gap, ex, p1, p2 = [row[:, i, :] for i in range(8)]
            gt, one1, one2, gl, is_top, wgt = [gts[:, i] for i in range(6)]
            hd = hid[:, :, :]
            v.wait_ge(small_loaded, 80)
            v.wait_ge(tmp_copied, NT)
            gthen(v.tensor_tensor(hd, tmp[:, :, ER:ER + GH], per_channel(g1b[:, :]), ALU.add))
            gthen(v.tensor_reduce(total, hd, X, ALU.add))
            gthen(v.tensor_scalar(total, total, 1.0 / GH, None, ALU.mult))
            gthen(v.tensor_tensor(hd, hd, per_token(total, GH), ALU.subtract))
            gthen(v.tensor_tensor(hid2, hd, hd, ALU.mult))
            gthen(v.tensor_reduce(var, hid2, X, ALU.add))
            v.tensor_scalar(var, var, 1.0 / GH, LN_EPS, ALU.mult, ALU.add).then_inc(var_ready, 1)
            v.wait_ge(gate_std, 1)
            gthen(v.reciprocal(rstd, std))
            gthen(v.tensor_tensor(gap, rstd, rstd, ALU.mult))
            gthen(v.tensor_tensor(gap, gap, var, ALU.mult))
            gthen(v.tensor_scalar(gap, gap, -0.5, 1.5, ALU.mult, ALU.add))
            gthen(v.tensor_tensor(rstd, rstd, gap, ALU.mult))
            gthen(v.tensor_tensor(hd, hd, per_token(rstd, GH), ALU.mult))
            gthen(v.tensor_tensor(hd, hd, per_channel(lng[:, :]), ALU.mult))
            gthen(v.tensor_tensor(hd, hd, per_channel(lnb[:, :]), ALU.add))
            gthen(v.tensor_scalar(hd, hd, 0.0, None, ALU.max))
            g2 = g2w[:, :].rearrange("p (e h) -> p e h", e=E)
            hf = NT // 2
            for s in range(2):
                v.wait_ge(w_stored[s], 16 * KC // 2)
            for half in range(2):
                for tt in range(hf):
                    v.tensor_tensor(gate_prod[:, tt], hid[:, half * hf + tt, :].unsqueeze(1).broadcast_to([P, E, GH]),
                                    g2, ALU.mult).then_inc(gate_half, 1)
                v.wait_ge(gate_half, hf * (half + 1))
                gthen(v.tensor_reduce(gt[:, half * hf:(half + 1) * hf, :], gate_prod, X, ALU.add))
            gthen(v.tensor_tensor(gt, gt, per_channel(g2b[:, :]), ALU.add))

            def choose(top, one):
                gthen(v.tensor_reduce(top, gt, X, ALU.max))
                gthen(v.tensor_tensor(is_top, gt, per_token(top, E), ALU.is_equal))
                gthen(v.scalar_tensor_tensor(out=gl, in0=is_top, scalar=-float(E), in1=per_channel(iota[:, 0:E]),
                                             op0=ALU.mult, op1=ALU.add))
                gthen(v.tensor_reduce(total, gl, X, ALU.min))
                gthen(v.tensor_tensor(one, gl, per_token(total, E), ALU.is_equal))

            choose(p1, one1)
            gthen(v.scalar_tensor_tensor(out=gt, in0=one1, scalar=-3.0e38, in1=gt, op0=ALU.mult, op1=ALU.add))
            choose(p2, one2)
            v.tensor_tensor(gap, p2, p1, ALU.subtract).then_inc(gap_ready, 1)
            gthen(v.tensor_reduce(cnt[:, 0, :], one1.rearrange("p t e -> p e t"), X, ALU.add))
            v.tensor_reduce(cnt[:, 1, :], one2.rearrange("p t e -> p e t"), X, ALU.add).then_inc(count_ready, 1)
            v.wait_ge(gate_exp, 1)
            gthen(v.tensor_scalar(p1, ex, 1.0, None, ALU.add))
            gthen(v.reciprocal(p1, p1))
            gthen(v.tensor_tensor(p2, ex, p1, ALU.mult))
            v.wait_ge(counted, 1)
            gthen(v.tensor_scalar(okay[:, :, :], pair[3][:, 0:2 * E].rearrange("p (a b) -> p a b", a=2),
                                  float(CAPACITY), None, ALU.is_le))
            gthen(v.tensor_tensor(one1, one1, per_channel(okay[:, 0, :]), ALU.mult))
            gthen(v.tensor_tensor(one2, one2, per_channel(okay[:, 1, :]), ALU.mult))
            gthen(v.tensor_tensor(one1, one1, per_token(p1, E), ALU.mult))
            gthen(v.tensor_tensor(one2, one2, per_token(p2, E), ALU.mult))
            gthen(v.tensor_tensor(wgt, one1, one2, ALU.add))
            for e in range(E):
                ins = v.tensor_tensor(tmpw[:, :, e, :], tmp[:, :, e * R:(e + 1) * R],
                                      wgt[:, :, e].unsqueeze(2).broadcast_to([P, NT, R]), ALU.mult)
            ins.then_inc(tmpw_ready, 1)
            for i in range(2):
                v.wait_ge(tmpw_high, i + 1)
                low(tmpw_t[:, 1, i * D:(i + 1) * D], pair[2 + i][:, :], 1.0, tmpw_t[:, 0, i * D:(i + 1) * D])\
                    .then_inc(tmpw_low, 1)

            def residual(t, s):
                v.wait_ge(main_done, t + 1)
                v.wait_ge(x_loaded[s], 32 * (t // 2 + 1) if isinstance(t, int) else 16 * t + 32 - 16 * s)
                wait_if(v, x1_stored[s], 8 * (t - s))
                v.scalar_tensor_tensor(out=x1_nat[s], in0=pair[s][:, :], scalar=1.0 / PROD, in1=x_nat[s],
                                       op0=ALU.mult, op1=ALU.add).then_inc(acc_released, 1)

            def low_x1(t):
                v.wait_ge(x1_high, t + 1)
                low(act_t[:, 1, :, ds(t * P, P)], ps8[2], ACT_SCALE, act_t[:, 0, :, ds(t * P, P)])\
                    .then_inc(x1_low, 1)

            residual(0, 0)
            residual(1, 1)
            low_x1(0)
            def layer0(i, pieces):
                for s in range(2):
                    t = 2 * i + s
                    low_x1(t - 1)
                    used = field(v, F_USED, 0, NADP)
                    with v.If(used > i):
                        for q in range(4):
                            low_w(4 * t + q, q)
                    if pieces:
                        sum_gate(t, s, 16 * i + 16)
                    residual(t, s)

            with v.Fori(1, NT // 4) as i:
                layer0(i, False)
            with v.Fori(NT // 4, NT // 2) as i:
                layer0(i, True)
            low_x1(NT - 1)
            v.wait_ge(gate_summed, NPIECE_G)
            v.tensor_reduce(ssum[:, 0:1], stat_g[:, :], X, ALU.add).then_inc(stat_summed, 1)

            def copy_z(k, s):
                v.wait_ge(z_done, k + 1)
                v.tensor_scalar(z_nat[s][:, H:D], pair[s][:, H:D], 1.0 / PROD, None, ALU.mult).then_inc(z_copied_v, 1)

            def low_z(k):
                d0 = field(v, F_WRITE, k, WRITE_DUMMY * SEQ)
                d1 = field(v, F_SECOND, k, SECOND_DUMMY * SEQ)
                v.wait_ge(z_high, k + 1)
                low(act_t[:, 1, :, ds(d0, SEQ)], ps8[2][:, :, 0:SEQ], ACT_SCALE, act_t[:, 0, :, ds(d0, SEQ)])
                low(act_t[:, 1, :, ds(d1, SEQ)], ps8[2][:, :, SEQ:P], ACT_SCALE, act_t[:, 0, :, ds(d1, SEQ)])\
                    .then_inc(z_low, 1)

            def sum_piece(p, s, loads, last=False):
                n = PIECE if not last else INNER * D // P - (NPIECE - 1) * PIECE
                v.wait_ge(stat_loaded[s], loads)
                v.tensor_reduce(stat[:, :, ds(p, 1)].rearrange("p a b -> p (a b)"), stat_in[s][:, :, 0:n], X, ALU.add,
                                apply_absolute_value=True).then_inc(stat_done, 1)

            def layer1(i, last=False):
                copy_z(2 * i + 1, 1)
                low_z(2 * i)
                sum_piece(2 * i, 0, 32 * i + 32)
                copy_z(2 * i + 2, 0)
                low_z(2 * i + 1)
                sum_piece(2 * i + 1, 1, 32 * i + 32, last)

            copy_z(0, 0)
            with v.Fori(0, NPIECE // 2 - 1) as i:
                layer1(i)
            layer1(NPIECE // 2 - 1, last=True)
            v.wait_ge(stat_done, NPIECE)
            v.tensor_reduce(ssum[:, 1:3], stat[:, :, :], X, ALU.add).then_inc(stat_summed, 1)

            def copy_z_opt(k, s):
                pairs = field(v, F_CUM, NADP - 1, NSLOT)
                with v.If(pairs > k):
                    copy_z(k, s)
                with v.If(pairs <= k):
                    v.wait_ge(z_done, k + 1)
                    v.tensor_copy(z_nat[s][0:1, H:H + 1], pair[s][0:1, H:H + 1]).then_inc(z_copied_v, 1)

            def low_z_opt(k):
                pairs = field(v, F_CUM, NADP - 1, NSLOT)
                with v.If(pairs > k):
                    low_z(k)
                with v.If(pairs <= k):
                    v.wait_ge(z_high, k + 1)
                    v.tensor_copy(act_t[0:1, 1, 0, WRITE_DUMMY * SEQ:WRITE_DUMMY * SEQ + 1], pair[2][0:1, 0:1])\
                     .then_inc(z_low, 1)

            def ternary(ic, n_load, last=False):
                place = wq_early if isinstance(ic, int) and ic < 2 else wq_nat
                for kind in range(3):
                    if not isinstance(ic, int) or ic > 0:
                        v.wait_ge(q_transposed, 3 * ic - 2 + kind)
                    if last and kind > 0:
                        rest = place[1][LAST:P, :] if kind == 1 else chunked(place[2])[:, :, LAST:P]
                        v.memset(rest, 0.0).then_inc(zeroed, 1)
                        v.wait_ge(zeroed, kind)
                    v.wait_ge(wq_loaded[kind], 16 * (n_load + 1 if last and kind == 0 else n_load))
                    if not isinstance(ic, int) or 3 * ic + kind > 0:
                        v.wait_ge(q_ready, 3 * ic + kind)
                    c = 3 if last and kind == 0 else kind
                    v.tensor_scalar(le_mask, place[kind], thr[:, c:c + 1], None, ALU.is_le).then_inc(mask_ready, 1)
                    v.wait_ge(mask_ready, 3 * ic + kind + 1)
                    v.scalar_tensor_tensor(out=q16[kind], in0=place[kind], scalar=nthr[:, c:c + 1], in1=le_mask,
                                           op0=ALU.is_ge, op1=ALU.subtract).then_inc(q_ready, 1)

            def product(n, s, last=False):
                v.wait_ge(gate_scaled, n + 1)
                if last:
                    v.tensor_tensor(gate_s[s][0:LAST], pair[0][LAST:2 * LAST, s * H:(s + 1) * H],
                                    gate_s[s][LAST:2 * LAST], ALU.mult).then_inc(prod_done, 1)
                else:
                    v.tensor_tensor(gate_s[s], pair[1][:, s * H:(s + 1) * H], gate_s[s], ALU.mult)\
                     .then_inc(prod_done, 1)

            def result(g, tt):
                v.wait_ge(down_done, TPG * g + tt + 1)
                v.wait_ge(res_loaded[tt], 16 * g + 16)
                v.scalar_tensor_tensor(out=res[tt], in0=pair[tt][:, :], scalar=out_c[:, 0:1], in1=res[tt],
                                       op0=ALU.mult, op1=ALU.add).then_inc(res_done, 1)

            def widen_down(g, ic, c):
                v.tensor_copy(wide[down_slot(g, c)], at(q_down, ic)).then_inc(down_wide[1], 1)

            def finish(g):
                v.wait_ge(gu_done, g * IC + IC - 1)
                widen_down(g, 1, 1)
                product(g * IC + IC - 1, 1, last=True)
                widen_down(g, 3, 3)
                with v.Fori(0, (IC - 6) // 4) as i:
                    for c in (1, 3):
                        v.wait_ge(down_step, g * (IC - 2) + 4 * i + c + 1)
                        widen_down(g, 4 * i + c + 4, c)
                v.wait_ge(down_step, g * (IC - 2) + IC - 4)
                widen_down(g, IC - 1, 1)
                for tt in range(TPG):
                    result(g, tt)

            k = FIRST_OPTIONAL
            copy_z(k - 4, 1)
            low_z(k - 5)
            v.wait_ge(mean_done, 1)
            v.tensor_scalar(mean[:, 0:3], pair[3][:, 0:3], 1.0 / (INNER * D), None, ALU.mult).then_inc(stat_step, 1)
            v.wait_ge(stat_step, 1)
            v.tensor_scalar(thr[:, 0:3], mean[:, 0:3], Q_EPS, 0.5, ALU.add, ALU.mult).then_inc(stat_step, 1)
            v.tensor_scalar(out_c[:, :], mean[:, 2:3], 1.0 / INTER_SCALE, None, ALU.mult).then_inc(stat_step, 1)
            v.scalar_tensor_tensor(out=inter_c[:, :], in0=mean[:, 0:1], scalar=INTER_SCALE / ACT_SCALE ** 2,
                                   in1=mean[:, 1:2], op0=ALU.mult, op1=ALU.mult).then_inc(stat_step, 1)
            v.wait_ge(stat_step, 4)
            v.tensor_copy(thr[0:LAST, 3:4], thr[0:LAST, 0:1]).then_inc(stat_step, 1)
            v.tensor_copy(thr[LAST:P, 3:4], thr[LAST:P, 1:2]).then_inc(stat_step, 1)
            v.wait_ge(stat_step, 6)
            v.tensor_scalar(nthr[:, :], thr[:, :], -1.0, None, ALU.mult).then_inc(scales_ready, 1)
            v.wait_ge(scales_ready, 1)
            ternary(0, 1)
            copy_z(k - 3, 0)
            low_z(k - 4)
            copy_z(k - 2, 1)
            low_z(k - 3)
            ternary(1, 2)
            copy_z(k - 1, 0)
            low_z(k - 2)
            copy_z_opt(k, 1)
            low_z(k - 1)
            copy_z_opt(k + 1, 0)
            low_z_opt(k)
            copy_z_opt(k + 2, 1)
            low_z_opt(k + 1)
            low_z_opt(k + 2)
            with v.Fori(0, IC // 2 - 2) as i:
                for s in range(2):
                    ternary(2 * i + s + 2, 2 * i + s + 3)
                    product(2 * i + s, s)
            ternary(IC - 2, IC - 1)
            product(IC - 4, 0)
            ternary(IC - 1, IC, last=True)
            product(IC - 3, 1)
            product(IC - 2, 0)
            v.wait_ge(q_stored, 3 * IC)
            finish(0)
            for g in range(1, NG):
                with v.Fori(0, IC // 2 - 1) as i:
                    for s in range(2):
                        product(g * IC + 2 * i + s, s)
                product(g * IC + IC - 2, 0)
                finish(g)


_INS = ['x', 'itok_B_3_7', 'itok_B_0_15', 'L0_cond_weights', 'L0_ffn_weight', 'L0_ffn_lora_A', 'L0_ffn_lora_B',
        'L0_ffn_gw1', 'L0_ffn_gb1', 'L0_ffn_ln_gamma', 'L0_ffn_ln_beta', 'L0_ffn_gw2', 'L0_ffn_gb2',
        'L1_cond_weight', 'L1_ffn_w_gate', 'L1_ffn_w_up', 'L1_ffn_w_down']


def kernel(**inputs):
    import numpy as _np
    import concourse.bacc as _bacc
    from concourse import mybir as _mybir
    from concourse.bass_utils import run_bass_kernel_spmd as _run

    nc = _bacc.Bacc("TRN2", target_bir_lowering=False, num_devices=1, dynamic_dma_scratch_size=1024)
    arrays, args = {}, []
    for name in _INS:
        a = _np.ascontiguousarray(inputs[name])
        arrays[f"in_{name}"] = a
        args.append(nc.dram_tensor(f"in_{name}", a.shape, _mybir.dt.from_np(a.dtype), kind="ExternalInput").ap())
    args.append(nc.dram_tensor("out", (NB, SEQ, D), F32, kind="ExternalOutput").ap())
    build_program(nc, *args)
    r = _run(nc, [arrays], core_ids=[0])
    return r.results[0]["out"]
```
